# Optimizing a Trainium2 kernel written in Bass

```python
import numpy as np
import jax
import jax.numpy as jnp

def _softmax(x, axis=-1):
    return jax.nn.softmax(x, axis=axis)

def _gelu(x):
    return jax.nn.gelu(x, approximate=True)

def _silu(x):
    return jax.nn.silu(x)

def _sigmoid(x):
    return jax.nn.sigmoid(x)

def _layernorm(x, axis=-1, eps=1e-05):
    m = jnp.mean(x, axis=axis, keepdims=True)
    v = jnp.var(x, axis=axis, keepdims=True)
    return (x - m) / jnp.sqrt(v + eps)

def _scatter_add(tgt, idx, src, axis=0):
    return tgt.at[idx].add(src)

def _segment_sum(src, seg, n):
    return jax.ops.segment_sum(src, seg, n)
kernel_name = 'mk_early_fusion_d4_tok_img1024_r4_73052e'

def setup_inputs(seed: int=0):
    np.random.seed(seed)
    _w = jnp.asarray

    def _rec_inputs():
        import jax
        import jax.numpy as jnp
        _rk = jax.random.key(seed)
        x = -0.00016672 + 0.999947 * jax.random.normal(jax.random.fold_in(_rk, 1), (32, 3, 96, 96), jnp.float32)
        txt = 0.00213415 + 1.41303 * jax.random.normal(jax.random.fold_in(_rk, 2), (32, 77, 256), jnp.float32)
        return (x, txt)
    x, txt = _rec_inputs()

    def _L0_tok_setup():
        import jax, jax.numpy as jnp
        import numpy as np
        EMBED_DIM = 256
        IMAGE_SIZE = 96
        CHANNELS = 3
        PATCH = 16
        NUM_PATCHES = (IMAGE_SIZE // PATCH) ** 2
        PATCH_DIM = PATCH * PATCH * CHANNELS

        def _patchify(x, patch):
            B, C, H, W = x.shape
            hp, wp = (H // patch, W // patch)
            x = x.reshape(B, C, hp, patch, wp, patch)
            x = x.transpose(0, 2, 4, 1, 3, 5)
            return x.reshape(B, hp * wp, C * patch * patch)
        key = jax.random.key(seed)
        k_x, k_w, k_b, k_cls, k_pos = jax.random.split(key, 5)
        x = jax.random.normal(k_x, (64, CHANNELS, IMAGE_SIZE, IMAGE_SIZE), dtype=jnp.float32)
        W = jax.random.normal(k_w, (EMBED_DIM, PATCH_DIM), dtype=jnp.float32) / np.sqrt(PATCH_DIM)
        b = jax.random.normal(k_b, (EMBED_DIM,), dtype=jnp.float32) * 0.01
        cls_token = jax.random.normal(k_cls, (1, 1, EMBED_DIM), dtype=jnp.float32)
        pos_embedding = jax.random.normal(k_pos, (1, 1 + NUM_PATCHES, EMBED_DIM), dtype=jnp.float32)
        return {'x': x, 'W': W, 'b': b, 'cls_token': cls_token, 'pos_embedding': pos_embedding}
    _L0_tok_all = _L0_tok_setup()
    _L0_tok_in = {k: v for k, v in _L0_tok_all.items() if k in ('W', 'b', 'cls_token', 'pos_embedding')}
    del _L0_tok_all

    def _L0_attn_setup():
        import math
        import jax, jax.numpy as jnp
        import numpy as np
        DIM, HEADS, RFF = (256, 16, 128)
        DK = DIM // HEADS

        def _phi_rff(t, Wr, br):
            proj = jnp.einsum('bnhd,hdr->bnhr', t, Wr) + br
            return jnp.concatenate([jnp.cos(proj), jnp.sin(proj)], axis=-1) / math.sqrt(RFF)
        key = jax.random.key(seed)
        ks = jax.random.split(key, 8)
        B, N = (2, 2048)
        x = jax.random.normal(ks[0], (B, N, DIM), dtype=jnp.float32)
        Wq = jax.random.normal(ks[1], (DIM, DIM), dtype=jnp.float32) / math.sqrt(DIM)
        Wk = jax.random.normal(ks[2], (DIM, DIM), dtype=jnp.float32) / math.sqrt(DIM)
        Wv = jax.random.normal(ks[3], (DIM, DIM), dtype=jnp.float32) / math.sqrt(DIM)
        Wp = jax.random.normal(ks[4], (DIM, DIM), dtype=jnp.float32) / math.sqrt(DIM)
        bp = jnp.zeros((DIM,), dtype=jnp.float32)
        Wr = jax.random.normal(ks[5], (HEADS, DK, RFF), dtype=jnp.float32) / math.sqrt(DK)
        br = 2.0 * math.pi * jax.random.uniform(ks[6], (HEADS, RFF), dtype=jnp.float32)
        return {'x': x, 'Wq': Wq, 'Wk': Wk, 'Wv': Wv, 'Wp': Wp, 'bp': bp, 'Wr': Wr, 'br': br}
    _L0_attn_all = _L0_attn_setup()
    _L0_attn_in = {k: v for k, v in _L0_attn_all.items() if k in ('Wq', 'Wk', 'Wv', 'Wp', 'bp', 'Wr', 'br')}
    del _L0_attn_all

    def _L0_ffn_setup():
        import jax, jax.numpy as jnp
        import numpy as np
        D_MODEL = 256
        D_FF = 1024
        NUM_EXPERTS = 8
        key = jax.random.key(seed)
        ks = jax.random.split(key, 8)
        scale_in = 1.0 / np.sqrt(D_MODEL)
        scale_ff = 1.0 / np.sqrt(D_FF)
        x = jax.random.normal(ks[0], (4, 512, D_MODEL), dtype=jnp.float32)
        gate_w = jax.random.uniform(ks[1], (NUM_EXPERTS, D_MODEL), jnp.float32, -scale_in, scale_in)
        gate_b = jax.random.uniform(ks[2], (NUM_EXPERTS,), jnp.float32, -scale_in, scale_in)
        expert_bias = jnp.zeros((NUM_EXPERTS,), dtype=jnp.float32)
        w1 = jax.random.uniform(ks[3], (NUM_EXPERTS, D_MODEL, D_FF), jnp.float32, -scale_in, scale_in)
        b1 = jax.random.uniform(ks[4], (NUM_EXPERTS, D_FF), jnp.float32, -scale_in, scale_in)
        w2 = jax.random.uniform(ks[5], (NUM_EXPERTS, D_FF, D_MODEL), jnp.float32, -scale_ff, scale_ff)
        b2 = jax.random.uniform(ks[6], (NUM_EXPERTS, D_MODEL), jnp.float32, -scale_ff, scale_ff)
        return {'x': x, 'gate_w': gate_w, 'gate_b': gate_b, 'expert_bias': expert_bias, 'w1': w1, 'b1': b1, 'w2': w2, 'b2': b2}
    _L0_ffn_all = _L0_ffn_setup()
    _L0_ffn_in = {k: v for k, v in _L0_ffn_all.items() if k in ('gate_w', 'gate_b', 'expert_bias', 'w1', 'b1', 'w2', 'b2')}
    del _L0_ffn_all

    def _L1_attn_setup():
        import jax, jax.numpy as jnp
        import numpy as np
        HIDDEN = 256
        HEADS = 16
        HEAD = HIDDEN // HEADS

        def _ternary_weight(key, shape):
            g = jax.random.normal(key, shape, dtype=jnp.float32)
            return jnp.where(jnp.abs(g) < 0.6, 0.0, jnp.sign(g)).astype(jnp.float32)

        def _tlin(x, w, s, b):
            return jnp.einsum('bsh,oh->bso', x, w) * s + b
        key = jax.random.key(seed)
        ks = jax.random.split(key, 10)
        x = jax.random.normal(ks[0], (2, 512, HIDDEN), dtype=jnp.float32)
        d = {'x': x}
        names = ['q', 'k', 'v', 'o']
        for i, n in enumerate(names):
            d[f'w_{n}'] = _ternary_weight(ks[1 + i], (HIDDEN, HIDDEN))
            d[f's_{n}'] = jnp.float32(0.02)
            d[f'b_{n}'] = jax.random.normal(ks[5 + i], (HIDDEN,), dtype=jnp.float32) * 0.02
        return d
    _L1_attn_all = _L1_attn_setup()
    _L1_attn_in = {k: v for k, v in _L1_attn_all.items() if k in ('w_q', 's_q', 'b_q', 'w_k', 's_k', 'b_k', 'w_v', 's_v', 'b_v', 'w_o', 's_o', 'b_o')}
    del _L1_attn_all

    def _L1_ffn_setup():
        import jax, jax.numpy as jnp
        import numpy as np
        N_HEADS = 16
        N_KV_HEADS = 4
        N_EMBD = 256
        HEAD_DIM = N_EMBD // N_HEADS
        N_EXPERTS = 8
        TOP_K = 2
        EPS = 1e-06

        def _rmsnorm(x, w):
            xf = x.astype(jnp.float32)
            n = xf * jax.lax.rsqrt(jnp.mean(xf * xf, axis=-1, keepdims=True) + EPS)
            return n.astype(x.dtype) * w

        def _gqa(x, wq, wk, wv, wo):
            B, S, C = x.shape
            n_rep = N_HEADS // N_KV_HEADS
            q = (x @ wq.T).reshape(B, S, N_HEADS, HEAD_DIM)
            k = (x @ wk.T).reshape(B, S, N_KV_HEADS, HEAD_DIM)
            v = (x @ wv.T).reshape(B, S, N_KV_HEADS, HEAD_DIM)
            k = jnp.repeat(k, n_rep, axis=2)
            v = jnp.repeat(v, n_rep, axis=2)
            scale = 1.0 / np.sqrt(HEAD_DIM).astype(np.float32)
            attn = jnp.einsum('bqhd,bkhd->bhqk', q, k) * scale
            causal = jnp.tril(jnp.ones((S, S), dtype=bool))
            attn = jnp.where(causal, attn, jnp.float32(-jnp.inf))
            attn = jax.nn.softmax(attn, axis=-1)
            out = jnp.einsum('bhqk,bkhd->bqhd', attn, v).reshape(B, S, C)
            return out @ wo.T

        def _moe(x, gate_w, expert_w):
            B, S, C = x.shape
            t = x.reshape(B * S, C)
            logits = t @ gate_w.T
            w, sel = jax.lax.top_k(logits, TOP_K)
            w = jax.nn.softmax(w.astype(jnp.float32), axis=1).astype(t.dtype)
            comb = jnp.sum(w[..., None] * jax.nn.one_hot(sel, N_EXPERTS, dtype=t.dtype), axis=1)
            out = jnp.zeros_like(t)
            for e in range(N_EXPERTS):
                out = out + comb[:, e, None] * (t @ expert_w[e].T)
            return out.reshape(B, S, C)
        key = jax.random.key(seed)
        ks = jax.random.split(key, 10)
        B, S, C = (4, 512, N_EMBD)
        s = 0.02
        return {'x': jax.random.normal(ks[0], (B, S, C), dtype=jnp.float32), 'attn_norm_w': jnp.ones((C,), dtype=jnp.float32), 'ffn_norm_w': jnp.ones((C,), dtype=jnp.float32), 'wq': jax.random.normal(ks[1], (C, C), dtype=jnp.float32) * s, 'wk': jax.random.normal(ks[2], (N_KV_HEADS * HEAD_DIM, C), dtype=jnp.float32) * s, 'wv': jax.random.normal(ks[3], (N_KV_HEADS * HEAD_DIM, C), dtype=jnp.float32) * s, 'wo': jax.random.normal(ks[4], (C, C), dtype=jnp.float32) * s, 'gate_w': jax.random.normal(ks[5], (N_EXPERTS, C), dtype=jnp.float32) * s, 'expert_w': jax.random.normal(ks[6], (N_EXPERTS, C, C), dtype=jnp.float32) * s}
    _L1_ffn_all = _L1_ffn_setup()
    _L1_ffn_in = {k: v for k, v in _L1_ffn_all.items() if k in ('attn_norm_w', 'ffn_norm_w', 'wq', 'wk', 'wv', 'wo', 'gate_w', 'expert_w')}
    del _L1_ffn_all

    def _L2_attn_setup():
        import jax, jax.numpy as jnp
        import numpy as np
        from jax import lax
        B, L, D, H = (4, 512, 256, 16)
        DK = D // H
        DV = D // H
        SCALE = DK ** (-0.5)

        def _gla_forward(hidden_states, Wq, Wf, Wi, Wo):
            b, l, d = hidden_states.shape
            q_logits = hidden_states @ Wq
            f_logits = hidden_states @ Wf
            v = hidden_states @ Wi
            q = jax.nn.softmax(q_logits, axis=-1)
            k = 1.0 - jax.nn.softmax(f_logits, axis=-1)
            g = jax.nn.log_softmax(f_logits, axis=-1)

            def split_heads(x, hd):
                return x.reshape(b, l, H, hd).transpose(1, 0, 2, 3)
            q_t = split_heads(q, DK)
            k_t = split_heads(k, DK)
            g_t = split_heads(g, DK)
            v_t = split_heads(v, DV)

            def step(S, inp):
                qt, kt, vt, gt = inp
                S = S * jnp.exp(gt)[..., None] + kt[..., None] * vt[..., None, :]
                ot = jnp.einsum('bhk,bhkv->bhv', qt * SCALE, S)
                return (S, ot)
            S0 = jnp.zeros((b, H, DK, DV), hidden_states.dtype)
            _, o = lax.scan(step, S0, (q_t, k_t, v_t, g_t))
            o = o.transpose(1, 0, 2, 3).reshape(b, l, d)
            return o @ Wo
        key = jax.random.key(seed)
        ks = jax.random.split(key, 5)
        std = 0.02
        return {'hidden_states': jax.random.normal(ks[0], (B, L, D), jnp.float32), 'Wq': jax.random.normal(ks[1], (D, D), jnp.float32) * std, 'Wf': jax.random.normal(ks[2], (D, D), jnp.float32) * std, 'Wi': jax.random.normal(ks[3], (D, D), jnp.float32) * std, 'Wo': jax.random.normal(ks[4], (D, D), jnp.float32) * std}
    _L2_attn_all = _L2_attn_setup()
    _L2_attn_in = {k: v for k, v in _L2_attn_all.items() if k in ('Wq', 'Wf', 'Wi', 'Wo')}
    del _L2_attn_all

    def _L2_ffn_setup():
        import jax, jax.numpy as jnp
        import numpy as np
        HIDDEN = 256
        INNER = 1024

        def _weight_quant(w):
            scale = 1.0 / jnp.clip(jnp.mean(jnp.abs(w)), 1e-05)
            wq = jnp.clip(jnp.round(w * scale), -1.0, 1.0) / scale
            return w + jax.lax.stop_gradient(wq - w)

        def _act_quant(x):
            scale = 127.0 / jnp.clip(jnp.max(jnp.abs(x), axis=-1, keepdims=True), 1e-05)
            xq = jnp.clip(jnp.round(x * scale), -128.0, 127.0) / scale
            return x + jax.lax.stop_gradient(xq - x)

        def _bitlinear(x, w):
            return jnp.einsum('bsi,oi->bso', _act_quant(x), _weight_quant(w))
        key = jax.random.key(seed)
        k0, k1, k2, k3 = jax.random.split(key, 4)
        x = jax.random.normal(k0, (4, 512, HIDDEN), dtype=jnp.float32)
        w_gate = jax.random.normal(k1, (INNER, HIDDEN), dtype=jnp.float32) / np.sqrt(HIDDEN)
        w_up = jax.random.normal(k2, (INNER, HIDDEN), dtype=jnp.float32) / np.sqrt(HIDDEN)
        w_down = jax.random.normal(k3, (HIDDEN, INNER), dtype=jnp.float32) / np.sqrt(INNER)
        return {'x': x, 'w_gate': w_gate, 'w_up': w_up, 'w_down': w_down}
    _L2_ffn_all = _L2_ffn_setup()
    _L2_ffn_in = {k: v for k, v in _L2_ffn_all.items() if k in ('w_gate', 'w_up', 'w_down')}
    del _L2_ffn_all

    def _L3_attn_setup():
        import jax, jax.numpy as jnp
        import numpy as np
        import math
        EMBED_DIM = 256
        NUM_HEADS = 16
        DEPTH = 12
        HEAD_DIM = EMBED_DIM // NUM_HEADS // 2
        LAMBDA_INIT = 0.8 - 0.6 * math.exp(-0.3 * DEPTH)
        EPS = 1e-05
        key = jax.random.key(seed)
        ks = jax.random.split(key, 11)
        E = EMBED_DIM
        x = jax.random.normal(ks[0], (2, 512, E), dtype=jnp.float32)
        s = 1.0 / math.sqrt(E)
        Wq = jax.random.normal(ks[1], (E, E), dtype=jnp.float32) * s
        Wk = jax.random.normal(ks[2], (E, E), dtype=jnp.float32) * s
        Wv = jax.random.normal(ks[3], (E, E), dtype=jnp.float32) * s
        Wo = jax.random.normal(ks[4], (E, E), dtype=jnp.float32) * s
        lambda_q1 = jax.random.normal(ks[5], (HEAD_DIM,), dtype=jnp.float32) * 0.1
        lambda_k1 = jax.random.normal(ks[6], (HEAD_DIM,), dtype=jnp.float32) * 0.1
        lambda_q2 = jax.random.normal(ks[7], (HEAD_DIM,), dtype=jnp.float32) * 0.1
        lambda_k2 = jax.random.normal(ks[8], (HEAD_DIM,), dtype=jnp.float32) * 0.1
        subln_w = jnp.ones((2 * HEAD_DIM,), dtype=jnp.float32)
        return {'x': x, 'Wq': Wq, 'Wk': Wk, 'Wv': Wv, 'Wo': Wo, 'lambda_q1': lambda_q1, 'lambda_k1': lambda_k1, 'lambda_q2': lambda_q2, 'lambda_k2': lambda_k2, 'subln_w': subln_w}
    _L3_attn_all = _L3_attn_setup()
    _L3_attn_in = {k: v for k, v in _L3_attn_all.items() if k in ('Wq', 'Wk', 'Wv', 'Wo', 'lambda_q1', 'lambda_k1', 'lambda_q2', 'lambda_k2', 'subln_w')}
    del _L3_attn_all

    def _L3_ffn_setup():
        import math
        import jax, jax.numpy as jnp
        import numpy as np
        D_MODEL = 256
        NUM_EXPERTS = 8
        D_FF_EXPERT = max(64, int(D_MODEL * 4 * 0.25))
        THRESHOLD = 0.9
        CAP_FACTOR = 1.0
        INIT_STD = 0.02

        def _xmoe_route(probs):
            N, E = probs.shape
            order = jnp.argsort(-probs, axis=-1)
            p_sorted = jnp.take_along_axis(probs, order, axis=-1)
            csum = jnp.cumsum(p_sorted, axis=-1)
            reached = (csum >= THRESHOLD).at[:, -1].set(True)
            k_idx = jnp.argmax(reached, axis=-1)
            select_prefix = jnp.arange(E)[None, :] <= k_idx[:, None]
            rows = jnp.arange(N)[:, None]
            assign_mask = jnp.zeros((N, E), dtype=bool).at[rows, order].set(select_prefix)
            rank = jnp.arange(1, E + 1, dtype=probs.dtype)[None, :]
            R_sorted = jnp.where(select_prefix, p_sorted - rank, jnp.full_like(p_sorted, -1000000000.0))
            R = jnp.zeros((N, E), dtype=probs.dtype).at[rows, order].set(R_sorted)
            capacity = int(math.ceil(N / E) * CAP_FACTOR)
            C = min(capacity, N)
            tok_order = jnp.argsort(-R, axis=0)
            topC = tok_order[:C, :]
            keep = jnp.zeros((N, E), dtype=bool).at[topC, jnp.arange(E)[None, :]].set(True)
            final_mask = assign_mask & keep
            return jnp.where(final_mask, probs, jnp.zeros_like(probs))
        key = jax.random.key(seed)
        k_x, k_g, k_w1, k_w2 = jax.random.split(key, 4)
        B, T = (4, 512)
        x = jax.random.normal(k_x, (B, T, D_MODEL), dtype=jnp.float32)
        bound = 1.0 / math.sqrt(D_MODEL)
        gate_w = jax.random.uniform(k_g, (NUM_EXPERTS, D_MODEL), minval=-bound, maxval=bound, dtype=jnp.float32)
        w1 = INIT_STD * jax.random.normal(k_w1, (NUM_EXPERTS, D_FF_EXPERT, D_MODEL), dtype=jnp.float32)
        w2 = INIT_STD * jax.random.normal(k_w2, (NUM_EXPERTS, D_MODEL, D_FF_EXPERT), dtype=jnp.float32)
        return {'x': x, 'gate_w': gate_w, 'w1': w1, 'w2': w2}
    _L3_ffn_all = _L3_ffn_setup()
    _L3_ffn_in = {k: v for k, v in _L3_ffn_all.items() if k in ('gate_w', 'w1', 'w2')}
    del _L3_ffn_all
    return {'x': x, 'txt': txt, 'L0_tok_W': _L0_tok_in['W'], 'L0_tok_b': _L0_tok_in['b'], 'L0_tok_cls_token': _L0_tok_in['cls_token'], 'L0_tok_pos_embedding': _L0_tok_in['pos_embedding'], 'L0_attn_Wq': _L0_attn_in['Wq'], 'L0_attn_Wk': _L0_attn_in['Wk'], 'L0_attn_Wv': _L0_attn_in['Wv'], 'L0_attn_Wp': _L0_attn_in['Wp'], 'L0_attn_bp': _L0_attn_in['bp'], 'L0_attn_Wr': _L0_attn_in['Wr'], 'L0_attn_br': _L0_attn_in['br'], 'L0_ffn_gate_w': _L0_ffn_in['gate_w'], 'L0_ffn_gate_b': _L0_ffn_in['gate_b'], 'L0_ffn_expert_bias': _L0_ffn_in['expert_bias'], 'L0_ffn_w1': _L0_ffn_in['w1'], 'L0_ffn_b1': _L0_ffn_in['b1'], 'L0_ffn_w2': _L0_ffn_in['w2'], 'L0_ffn_b2': _L0_ffn_in['b2'], 'L1_attn_w_q': _L1_attn_in['w_q'], 'L1_attn_s_q': _L1_attn_in['s_q'], 'L1_attn_b_q': _L1_attn_in['b_q'], 'L1_attn_w_k': _L1_attn_in['w_k'], 'L1_attn_s_k': _L1_attn_in['s_k'], 'L1_attn_b_k': _L1_attn_in['b_k'], 'L1_attn_w_v': _L1_attn_in['w_v'], 'L1_attn_s_v': _L1_attn_in['s_v'], 'L1_attn_b_v': _L1_attn_in['b_v'], 'L1_attn_w_o': _L1_attn_in['w_o'], 'L1_attn_s_o': _L1_attn_in['s_o'], 'L1_attn_b_o': _L1_attn_in['b_o'], 'L1_ffn_attn_norm_w': _L1_ffn_in['attn_norm_w'], 'L1_ffn_ffn_norm_w': _L1_ffn_in['ffn_norm_w'], 'L1_ffn_wq': _L1_ffn_in['wq'], 'L1_ffn_wk': _L1_ffn_in['wk'], 'L1_ffn_wv': _L1_ffn_in['wv'], 'L1_ffn_wo': _L1_ffn_in['wo'], 'L1_ffn_gate_w': _L1_ffn_in['gate_w'], 'L1_ffn_expert_w': _L1_ffn_in['expert_w'], 'L2_attn_Wq': _L2_attn_in['Wq'], 'L2_attn_Wf': _L2_attn_in['Wf'], 'L2_attn_Wi': _L2_attn_in['Wi'], 'L2_attn_Wo': _L2_attn_in['Wo'], 'L2_ffn_w_gate': _L2_ffn_in['w_gate'], 'L2_ffn_w_up': _L2_ffn_in['w_up'], 'L2_ffn_w_down': _L2_ffn_in['w_down'], 'L3_attn_Wq': _L3_attn_in['Wq'], 'L3_attn_Wk': _L3_attn_in['Wk'], 'L3_attn_Wv': _L3_attn_in['Wv'], 'L3_attn_Wo': _L3_attn_in['Wo'], 'L3_attn_lambda_q1': _L3_attn_in['lambda_q1'], 'L3_attn_lambda_k1': _L3_attn_in['lambda_k1'], 'L3_attn_lambda_q2': _L3_attn_in['lambda_q2'], 'L3_attn_lambda_k2': _L3_attn_in['lambda_k2'], 'L3_attn_subln_w': _L3_attn_in['subln_w'], 'L3_ffn_gate_w': _L3_ffn_in['gate_w'], 'L3_ffn_w1': _L3_ffn_in['w1'], 'L3_ffn_w2': _L3_ffn_in['w2']}

def reference(x, txt, L0_tok_W, L0_tok_b, L0_tok_cls_token, L0_tok_pos_embedding, L0_attn_Wq, L0_attn_Wk, L0_attn_Wv, L0_attn_Wp, L0_attn_bp, L0_attn_Wr, L0_attn_br, L0_ffn_gate_w, L0_ffn_gate_b, L0_ffn_expert_bias, L0_ffn_w1, L0_ffn_b1, L0_ffn_w2, L0_ffn_b2, L1_attn_w_q, L1_attn_s_q, L1_attn_b_q, L1_attn_w_k, L1_attn_s_k, L1_attn_b_k, L1_attn_w_v, L1_attn_s_v, L1_attn_b_v, L1_attn_w_o, L1_attn_s_o, L1_attn_b_o, L1_ffn_attn_norm_w, L1_ffn_ffn_norm_w, L1_ffn_wq, L1_ffn_wk, L1_ffn_wv, L1_ffn_wo, L1_ffn_gate_w, L1_ffn_expert_w, L2_attn_Wq, L2_attn_Wf, L2_attn_Wi, L2_attn_Wo, L2_ffn_w_gate, L2_ffn_w_up, L2_ffn_w_down, L3_attn_Wq, L3_attn_Wk, L3_attn_Wv, L3_attn_Wo, L3_attn_lambda_q1, L3_attn_lambda_k1, L3_attn_lambda_q2, L3_attn_lambda_k2, L3_attn_subln_w, L3_ffn_gate_w, L3_ffn_w1, L3_ffn_w2):
    import jax
    import jax.numpy as jnp

    def _L0_tok_ref(x, W, b, cls_token, pos_embedding):
        import jax, jax.numpy as jnp
        import numpy as np
        EMBED_DIM = 256
        IMAGE_SIZE = 96
        CHANNELS = 3
        PATCH = 16
        NUM_PATCHES = (IMAGE_SIZE // PATCH) ** 2
        PATCH_DIM = PATCH * PATCH * CHANNELS

        def _patchify(x, patch):
            B, C, H, W = x.shape
            hp, wp = (H // patch, W // patch)
            x = x.reshape(B, C, hp, patch, wp, patch)
            x = x.transpose(0, 2, 4, 1, 3, 5)
            return x.reshape(B, hp * wp, C * patch * patch)
        B = x.shape[0]
        patches = _patchify(x, PATCH)
        tokens = jnp.einsum('bnd,ed->bne', patches, W) + b
        cls = jnp.broadcast_to(cls_token, (B, 1, EMBED_DIM))
        out = jnp.concatenate([cls, tokens], axis=1)
        return out + pos_embedding

    def _L0_attn_ref(x, Wq, Wk, Wv, Wp, bp, Wr, br):
        import math
        import jax, jax.numpy as jnp
        import numpy as np
        DIM, HEADS, RFF = (256, 16, 128)
        DK = DIM // HEADS

        def _phi_rff(t, Wr, br):
            proj = jnp.einsum('bnhd,hdr->bnhr', t, Wr) + br
            return jnp.concatenate([jnp.cos(proj), jnp.sin(proj)], axis=-1) / math.sqrt(RFF)
        B, N, D = x.shape
        H, dk = (HEADS, DK)
        q = (x @ Wq.T).reshape(B, N, H, dk)
        k = (x @ Wk.T).reshape(B, N, H, dk)
        v = (x @ Wv.T).reshape(B, N, H, dk)
        qf = _phi_rff(q, Wr, br)
        kf = _phi_rff(k, Wr, br)
        Kv = jnp.einsum('bnhf,bnhd->bhfd', kf, v)
        z = 1.0 / (jnp.einsum('bnhf,bhf->bnh', qf, kf.sum(axis=1)) + 1e-06)
        out = jnp.einsum('bnhf,bhfd->bnhd', qf, Kv) * z[..., None]
        out = out.reshape(B, N, D)
        return out @ Wp.T + bp

    def _L0_ffn_ref(x, gate_w, gate_b, expert_bias, w1, b1, w2, b2):
        import jax, jax.numpy as jnp
        import numpy as np
        D_MODEL = 256
        D_FF = 1024
        NUM_EXPERTS = 8
        gate_logits = jnp.einsum('bsd,ed->bse', x, gate_w) + gate_b + expert_bias
        top_idx = jnp.argmax(gate_logits, axis=-1)
        out = jnp.zeros_like(x)
        for e in range(NUM_EXPERTS):
            mask = (top_idx == e)[..., None].astype(x.dtype)
            h = jax.nn.relu(jnp.einsum('bsd,df->bsf', x, w1[e]) + b1[e])
            y = jnp.einsum('bsf,fd->bsd', h, w2[e]) + b2[e]
            out = out + mask * y
        return out

    def _L1_attn_ref(x, w_q, s_q, b_q, w_k, s_k, b_k, w_v, s_v, b_v, w_o, s_o, b_o):
        import jax, jax.numpy as jnp
        import numpy as np
        HIDDEN = 256
        HEADS = 16
        HEAD = HIDDEN // HEADS

        def _ternary_weight(key, shape):
            g = jax.random.normal(key, shape, dtype=jnp.float32)
            return jnp.where(jnp.abs(g) < 0.6, 0.0, jnp.sign(g)).astype(jnp.float32)

        def _tlin(x, w, s, b):
            return jnp.einsum('bsh,oh->bso', x, w) * s + b
        B, S, H = x.shape

        def split_heads(t):
            return t.reshape(B, S, HEADS, HEAD).transpose(0, 2, 1, 3)
        q = split_heads(_tlin(x, w_q, s_q, b_q))
        k = split_heads(_tlin(x, w_k, s_k, b_k))
        v = split_heads(_tlin(x, w_v, s_v, b_v))
        scores = jnp.einsum('bhqd,bhkd->bhqk', q, k) / jnp.sqrt(jnp.float32(HEAD))
        attn = jax.nn.softmax(scores, axis=-1)
        ctx = jnp.einsum('bhqk,bhkd->bhqd', attn, v)
        ctx = ctx.transpose(0, 2, 1, 3).reshape(B, S, H)
        return _tlin(ctx, w_o, s_o, b_o)

    def _L1_ffn_ref(x, attn_norm_w, ffn_norm_w, wq, wk, wv, wo, gate_w, expert_w):
        import jax, jax.numpy as jnp
        import numpy as np
        N_HEADS = 16
        N_KV_HEADS = 4
        N_EMBD = 256
        HEAD_DIM = N_EMBD // N_HEADS
        N_EXPERTS = 8
        TOP_K = 2
        EPS = 1e-06

        def _rmsnorm(x, w):
            xf = x.astype(jnp.float32)
            n = xf * jax.lax.rsqrt(jnp.mean(xf * xf, axis=-1, keepdims=True) + EPS)
            return n.astype(x.dtype) * w

        def _gqa(x, wq, wk, wv, wo):
            B, S, C = x.shape
            n_rep = N_HEADS // N_KV_HEADS
            q = (x @ wq.T).reshape(B, S, N_HEADS, HEAD_DIM)
            k = (x @ wk.T).reshape(B, S, N_KV_HEADS, HEAD_DIM)
            v = (x @ wv.T).reshape(B, S, N_KV_HEADS, HEAD_DIM)
            k = jnp.repeat(k, n_rep, axis=2)
            v = jnp.repeat(v, n_rep, axis=2)
            scale = 1.0 / np.sqrt(HEAD_DIM).astype(np.float32)
            attn = jnp.einsum('bqhd,bkhd->bhqk', q, k) * scale
            causal = jnp.tril(jnp.ones((S, S), dtype=bool))
            attn = jnp.where(causal, attn, jnp.float32(-jnp.inf))
            attn = jax.nn.softmax(attn, axis=-1)
            out = jnp.einsum('bhqk,bkhd->bqhd', attn, v).reshape(B, S, C)
            return out @ wo.T

        def _moe(x, gate_w, expert_w):
            B, S, C = x.shape
            t = x.reshape(B * S, C)
            logits = t @ gate_w.T
            w, sel = jax.lax.top_k(logits, TOP_K)
            w = jax.nn.softmax(w.astype(jnp.float32), axis=1).astype(t.dtype)
            comb = jnp.sum(w[..., None] * jax.nn.one_hot(sel, N_EXPERTS, dtype=t.dtype), axis=1)
            out = jnp.zeros_like(t)
            for e in range(N_EXPERTS):
                out = out + comb[:, e, None] * (t @ expert_w[e].T)
            return out.reshape(B, S, C)
        h = x + _gqa(_rmsnorm(x, attn_norm_w), wq, wk, wv, wo)
        out = h + _moe(_rmsnorm(h, ffn_norm_w), gate_w, expert_w)
        return out

    def _L2_attn_ref(hidden_states, Wq, Wf, Wi, Wo):
        import jax, jax.numpy as jnp
        import numpy as np
        from jax import lax
        B, L, D, H = (4, 512, 256, 16)
        DK = D // H
        DV = D // H
        SCALE = DK ** (-0.5)

        def _gla_forward(hidden_states, Wq, Wf, Wi, Wo):
            b, l, d = hidden_states.shape
            q_logits = hidden_states @ Wq
            f_logits = hidden_states @ Wf
            v = hidden_states @ Wi
            q = jax.nn.softmax(q_logits, axis=-1)
            k = 1.0 - jax.nn.softmax(f_logits, axis=-1)
            g = jax.nn.log_softmax(f_logits, axis=-1)

            def split_heads(x, hd):
                return x.reshape(b, l, H, hd).transpose(1, 0, 2, 3)
            q_t = split_heads(q, DK)
            k_t = split_heads(k, DK)
            g_t = split_heads(g, DK)
            v_t = split_heads(v, DV)

            def step(S, inp):
                qt, kt, vt, gt = inp
                S = S * jnp.exp(gt)[..., None] + kt[..., None] * vt[..., None, :]
                ot = jnp.einsum('bhk,bhkv->bhv', qt * SCALE, S)
                return (S, ot)
            S0 = jnp.zeros((b, H, DK, DV), hidden_states.dtype)
            _, o = lax.scan(step, S0, (q_t, k_t, v_t, g_t))
            o = o.transpose(1, 0, 2, 3).reshape(b, l, d)
            return o @ Wo
        return _gla_forward(hidden_states, Wq, Wf, Wi, Wo)

    def _L2_ffn_ref(x, w_gate, w_up, w_down):
        import jax, jax.numpy as jnp
        import numpy as np
        HIDDEN = 256
        INNER = 1024

        def _weight_quant(w):
            scale = 1.0 / jnp.clip(jnp.mean(jnp.abs(w)), 1e-05)
            wq = jnp.clip(jnp.round(w * scale), -1.0, 1.0) / scale
            return w + jax.lax.stop_gradient(wq - w)

        def _act_quant(x):
            scale = 127.0 / jnp.clip(jnp.max(jnp.abs(x), axis=-1, keepdims=True), 1e-05)
            xq = jnp.clip(jnp.round(x * scale), -128.0, 127.0) / scale
            return x + jax.lax.stop_gradient(xq - x)

        def _bitlinear(x, w):
            return jnp.einsum('bsi,oi->bso', _act_quant(x), _weight_quant(w))
        gate = jax.nn.silu(_bitlinear(x, w_gate))
        up = _bitlinear(x, w_up)
        return _bitlinear(gate * up, w_down)

    def _L3_attn_ref(x, Wq, Wk, Wv, Wo, lambda_q1, lambda_k1, lambda_q2, lambda_k2, subln_w):
        import jax, jax.numpy as jnp
        import numpy as np
        import math
        EMBED_DIM = 256
        NUM_HEADS = 16
        DEPTH = 12
        HEAD_DIM = EMBED_DIM // NUM_HEADS // 2
        LAMBDA_INIT = 0.8 - 0.6 * math.exp(-0.3 * DEPTH)
        EPS = 1e-05
        bsz, tgt_len, E = x.shape
        H, D = (NUM_HEADS, HEAD_DIM)
        scaling = D ** (-0.5)
        q = jnp.einsum('bse,oe->bso', x, Wq)
        k = jnp.einsum('bse,oe->bso', x, Wk)
        v = jnp.einsum('bse,oe->bso', x, Wv)
        q = q.reshape(bsz, tgt_len, 2 * H, D).transpose(0, 2, 1, 3) * scaling
        k = k.reshape(bsz, tgt_len, 2 * H, D).transpose(0, 2, 1, 3)
        v = v.reshape(bsz, tgt_len, H, 2 * D).transpose(0, 2, 1, 3)
        attn_weights = jnp.einsum('bhqd,bhkd->bhqk', q, k)
        attn_weights = jnp.nan_to_num(attn_weights)
        attn_weights = jax.nn.softmax(attn_weights.astype(jnp.float32), axis=-1).astype(q.dtype)
        lambda_1 = jnp.exp(jnp.sum(lambda_q1 * lambda_k1).astype(jnp.float32)).astype(q.dtype)
        lambda_2 = jnp.exp(jnp.sum(lambda_q2 * lambda_k2).astype(jnp.float32)).astype(q.dtype)
        lambda_full = lambda_1 - lambda_2 + LAMBDA_INIT
        aw = attn_weights.reshape(bsz, H, 2, tgt_len, tgt_len)
        aw = aw[:, :, 0] - lambda_full * aw[:, :, 1]
        attn = jnp.einsum('bhqk,bhkd->bhqd', aw, v)
        var = jnp.mean(jnp.square(attn), axis=-1, keepdims=True)
        attn = attn * jax.lax.rsqrt(var + EPS) * subln_w
        attn = attn * (1.0 - LAMBDA_INIT)
        attn = attn.transpose(0, 2, 1, 3).reshape(bsz, tgt_len, H * 2 * D)
        return jnp.einsum('bse,oe->bso', attn, Wo)

    def _L3_ffn_ref(x, gate_w, w1, w2):
        import math
        import jax, jax.numpy as jnp
        import numpy as np
        D_MODEL = 256
        NUM_EXPERTS = 8
        D_FF_EXPERT = max(64, int(D_MODEL * 4 * 0.25))
        THRESHOLD = 0.9
        CAP_FACTOR = 1.0
        INIT_STD = 0.02

        def _xmoe_route(probs):
            N, E = probs.shape
            order = jnp.argsort(-probs, axis=-1)
            p_sorted = jnp.take_along_axis(probs, order, axis=-1)
            csum = jnp.cumsum(p_sorted, axis=-1)
            reached = (csum >= THRESHOLD).at[:, -1].set(True)
            k_idx = jnp.argmax(reached, axis=-1)
            select_prefix = jnp.arange(E)[None, :] <= k_idx[:, None]
            rows = jnp.arange(N)[:, None]
            assign_mask = jnp.zeros((N, E), dtype=bool).at[rows, order].set(select_prefix)
            rank = jnp.arange(1, E + 1, dtype=probs.dtype)[None, :]
            R_sorted = jnp.where(select_prefix, p_sorted - rank, jnp.full_like(p_sorted, -1000000000.0))
            R = jnp.zeros((N, E), dtype=probs.dtype).at[rows, order].set(R_sorted)
            capacity = int(math.ceil(N / E) * CAP_FACTOR)
            C = min(capacity, N)
            tok_order = jnp.argsort(-R, axis=0)
            topC = tok_order[:C, :]
            keep = jnp.zeros((N, E), dtype=bool).at[topC, jnp.arange(E)[None, :]].set(True)
            final_mask = assign_mask & keep
            return jnp.where(final_mask, probs, jnp.zeros_like(probs))
        B, T, D = x.shape
        N = B * T
        xf = x.reshape(N, D)
        probs = jax.nn.softmax(xf @ gate_w.T, axis=-1)
        scores_sel = _xmoe_route(probs)
        h = jax.nn.gelu(jnp.einsum('nd,efd->enf', xf, w1), approximate=False)
        y_e = jnp.einsum('enf,edf->end', h, w2)
        y = jnp.einsum('ne,end->nd', scores_sel, y_e)
        return y.reshape(B, T, D)
    h = _L0_tok_ref(x, L0_tok_W, L0_tok_b, L0_tok_cls_token, L0_tok_pos_embedding)
    h = jnp.concatenate([h, txt], axis=1)
    h = h + _L0_attn_ref(_layernorm(h, axis=-1), L0_attn_Wq, L0_attn_Wk, L0_attn_Wv, L0_attn_Wp, L0_attn_bp, L0_attn_Wr, L0_attn_br)
    h = h + _L0_ffn_ref(_layernorm(h, axis=-1), L0_ffn_gate_w, L0_ffn_gate_b, L0_ffn_expert_bias, L0_ffn_w1, L0_ffn_b1, L0_ffn_w2, L0_ffn_b2)
    h = h + _L1_attn_ref(_layernorm(h, axis=-1), L1_attn_w_q, L1_attn_s_q, L1_attn_b_q, L1_attn_w_k, L1_attn_s_k, L1_attn_b_k, L1_attn_w_v, L1_attn_s_v, L1_attn_b_v, L1_attn_w_o, L1_attn_s_o, L1_attn_b_o)
    h = h + _L1_ffn_ref(_layernorm(h, axis=-1), L1_ffn_attn_norm_w, L1_ffn_ffn_norm_w, L1_ffn_wq, L1_ffn_wk, L1_ffn_wv, L1_ffn_wo, L1_ffn_gate_w, L1_ffn_expert_w)
    h = h + _L2_attn_ref(_layernorm(h, axis=-1), L2_attn_Wq, L2_attn_Wf, L2_attn_Wi, L2_attn_Wo)
    h = h + _L2_ffn_ref(_layernorm(h, axis=-1), L2_ffn_w_gate, L2_ffn_w_up, L2_ffn_w_down)
    h = h + _L3_attn_ref(_layernorm(h, axis=-1), L3_attn_Wq, L3_attn_Wk, L3_attn_Wv, L3_attn_Wo, L3_attn_lambda_q1, L3_attn_lambda_k1, L3_attn_lambda_q2, L3_attn_lambda_k2, L3_attn_subln_w)
    h = h + _L3_ffn_ref(_layernorm(h, axis=-1), L3_ffn_gate_w, L3_ffn_w1, L3_ffn_w2)
    return h

_drawn_inputs = setup_inputs


def setup_inputs(seed=0):
    import zlib

    import numpy as np

    out = dict(_drawn_inputs(seed))
    spreads = {'L0_attn_bp': (0.0, 0.1),
     'L0_ffn_expert_bias': (0.0, 0.1),
     'L1_ffn_attn_norm_w': (1.0, 0.6),
     'L1_ffn_ffn_norm_w': (1.0, 0.2),
     'L3_attn_subln_w': (1.0, 0.6)}
    factors = {'L0_tok_b': 4.279,
     'L0_attn_br': 64.0,
     'L0_ffn_b1': 4.237,
     'L0_ffn_b2': 3.621,
     'L1_attn_w_q': 8.0,
     'L1_attn_b_q': 8.0,
     'L1_attn_w_k': 8.0,
     'L1_attn_b_k': 64.0,
     'L1_attn_w_v': 6.428,
     'L1_attn_b_v': 8.0,
     'L1_attn_w_o': 5.882,
     'L1_attn_b_o': 3.521,
     'L1_ffn_wq': 8.0,
     'L1_ffn_wk': 8.0,
     'L1_ffn_wv': 3.188,
     'L1_ffn_wo': 3.165,
     'L2_attn_Wq': 8.0,
     'L2_attn_Wf': 24.72,
     'L2_attn_Wi': 8.0,
     'L2_attn_Wo': 8.0,
     'L3_attn_lambda_q1': 8.0,
     'L3_attn_lambda_k1': 8.0,
     'L3_attn_lambda_q2': 8.0,
     'L3_attn_lambda_k2': 8.0,
     'L3_ffn_gate_w': 8.0,
     'L3_ffn_w1': 8.0,
     'L3_ffn_w2': 8.0}
    for name, (base, spread) in spreads.items():
        noise = np.random.default_rng([zlib.crc32(name.encode()), seed]).standard_normal(out[name].shape)
        drawn = base * np.exp(spread * noise) if base else spread * noise
        out[name] = jnp.asarray(drawn.astype(out[name].dtype))
    for name, factor in factors.items():
        out[name] = (out[name] * factor).astype(out[name].dtype)
    return out
```

```python
import math
from contextlib import ExitStack

import numpy as np

import concourse.bass as bass
from concourse import mybir

F32 = mybir.dt.float32
BF16 = mybir.dt.bfloat16
ALU = mybir.AluOpType
ACT = mybir.ActivationFunctionType
AX = mybir.AxisListType

P = 128
NI = 96
PATCH = 16
NPATCH = (NI // PATCH) ** 2
CLS = 1 + NPATCH
NTXT = 77
T = CLS + NTXT
B = 32
D = 256
KD = D // P
G = 4
NG = B // G
N = G * T
H = 16
DH = D // H
E = 8
FF = 1024
KT = 3 * PATCH * PATCH // P
BANK = 512
ROUND = 1.5 * 2.0 ** 23


def flat(ap):
    return ap.rearrange("p a b -> p (a b)")


class Link:

    def __init__(self, eng, sem, i=0, per=0):
        self.eng, self.sem, self.base, self.per, self.n = eng, sem, i * per, per, 0

    def after(self, ins):
        ins.then_inc(self.sem, 1)
        self.n += 1
        self.eng.wait_ge(self.sem, self.base + self.n)

    def end(self):
        assert self.per in (0, self.n), (self.per, self.n)


class Core:

    def __init__(self, nc, stack):
        self.nc, self.in_use = nc, []
        self.resid = self.sb(stack, "resid", [P, B, D])
        self.moments = self.sb(stack, "moments", [P, B, 2])
        self.rstd = self.sb(stack, "rstd", [P, B])
        self.ident = self.sb(stack, "ident", [P, P])
        self.ones = self.sb(stack, "ones", [P, P])

    def sb(self, stack, name, shape, dt=F32):
        return stack.enter_context(self.nc.sbuf_tensor(name, shape, dt))

    def banks(self, stack, name, n, dt=F32):
        return stack.enter_context(self.nc.psum_tensor(name, [P, n, BANK], dt))

    def sems(self, names, phase):
        made = [self.nc.alloc_semaphore(f"{phase}_{n}") for n in names.split()]
        self.in_use += made
        return made

    def end_of_phase(self):
        self.nc.clear_and_free_semaphores(self.in_use)
        self.in_use = []
        self.nc.all_engine_barrier()

    def tile(self, b):
        return flat(self.resid[:T, bass.ds(b, 1), :])

    def mean(self, b):
        return flat(self.moments[:T, bass.ds(b, 1), 0:1])

    def scale(self, b):
        return self.rstd[:T, bass.ds(b, 1)]


def row(ap, parts):
    return bass.AP(ap.tensor, ap.offset, [[0, parts]] + [list(x) for x in ap.ap])


def stats(eng, link, six, tiles):
    eng.memset(six[0:1, 0, 8:9], 0.0)
    for n, (src, _) in enumerate(tiles):
        last = eng.bn_stats(six[:T, n, 0:6], src)
    link.after(last)
    eng.memset(six[0:1, 0, 8:9], 0.0)
    for n in range(len(tiles)):
        last = eng.bn_aggr(six[:T, n, 6:8], six[:T, n, 0:6])
    link.after(last)
    eng.memset(six[0:1, 0, 8:9], 0.0)
    for n, (_, dst) in enumerate(tiles):
        last = eng.tensor_copy(dst, six[:T, n, 6:8])
    return last


def constants(c):
    (zero, made) = c.sems("zero made", "const")
    with c.nc.Block() as block:
        @block.vector
        def _(dve):
            dve.memset(c.ones[:], 1.0)

        @block.gpsimd
        def _(pool):
            pool.memset(c.ident[:], 0.0).then_inc(zero, 1)
            pool.wait_ge(zero, 1)
            pool.affine_select(out=c.ident[:], in_=c.ident[:], compare_op=ALU.not_equal, fill=1.0,
                               base=0, pattern=[[-1, P]], channel_multiplier=1).then_inc(made, 1)
            pool.wait_ge(made, 1)


def inverse_deviation(c, eps, ph):
    added, rooted, inverted = c.sems("added rooted inverted", ph + "_rstd")
    with c.nc.Block() as block:
        @block.vector
        def _(dve):
            dve.tensor_scalar(c.rstd[:T, :], c.moments[:T, :, 1], eps, None, ALU.add).then_inc(added, 1)
            dve.wait_ge(rooted, 1)
            dve.reciprocal(c.rstd[:T, :], c.rstd[:T, :]).then_inc(inverted, 1)
            dve.wait_ge(inverted, 1)

        @block.scalar
        def _(act):
            act.wait_ge(added, 1)
            act.activation(c.rstd[:T, :], c.rstd[:T, :], ACT.Sqrt).then_inc(rooted, 1)


def tokens(c, a):
    nc = c.nc
    with ExitStack() as st:
        patches = c.sb(st, "patches", [P, 2, KT, G, CLS])
        weight = c.sb(st, "tok_w", [P, KT, D])
        base = c.sb(st, "tok_base", [P, D])
        first = c.sb(st, "tok_first", [P, D])
        six = c.sb(st, "tok_six", [P, G, 9])
        acc = c.banks(st, "tok_acc", 4)
        (text_in, fixed_in, cls_in, patch_in0, patch_in1, summed, based, acc_free, link_s) = c.sems(
            "text_in fixed_in cls_in patch_in0 patch_in1 summed based acc_free link", "tok")
        patch_in = (patch_in0, patch_in1)
        with nc.Block() as block:
            @block.sync
            def _(sp):
                sp.dma_start(weight[:], a["tok_w"]).then_inc(fixed_in, 16)
                sp.dma_start(base[:CLS, :], a["tok_pos"]).then_inc(fixed_in, 16)
                sp.dma_start(first[:CLS, :], row(a["tok_b"], CLS)).then_inc(fixed_in, 16)
                sp.wait_ge(fixed_in, 48)
                sp.dma_start(first[0:1, :], a["tok_cls"]).then_inc(cls_in, 16)
                with sp.Fori(0, NG // 2) as i:
                    for u in range(2):
                        sp.wait_ge(summed, 2 * i + u + 1)
                        sp.dma_start(patches[:, u], a["patches"][bass.ds(2 * i + u, 1)].rearrange(
                            "a p k g c -> p (a k) g c")).then_inc(patch_in[u], 16)

            @block.scalar
            def _(act):
                act.dma_start(c.resid[CLS:T, :, :], a["txt"]).then_inc(text_in, 16)

            @block.tensor
            def _(pe):
                pe.sem_inc(summed, 2)
                pe.wait_ge(cls_in, 16)
                with pe.Fori(0, NG // 2) as i:
                    for u in range(2):
                        pe.wait_ge(patch_in[u], 16 * (i + 1))
                        pe.wait_ge(acc_free, 2 * i + u + 1)
                        for j in range(G):
                            for k in range(KT):
                                last = pe.matmul(acc[:CLS, 2 * u + j // 2, j % 2 * D:(j % 2 + 1) * D],
                                                 patches[:, u, k, j, :], weight[:, k, :],
                                                 start=k == 0, stop=k == KT - 1)
                        last.then_inc(summed, 1)

            @block.vector
            def _(dve):
                dve.sem_inc(acc_free, 2)
                dve.wait_ge(cls_in, 16)
                dve.tensor_tensor(base[:CLS, :], base[:CLS, :], first[:CLS, :], ALU.add).then_inc(based, 1)
                dve.wait_ge(based, 1)
                dve.wait_ge(text_in, 16)
                with dve.Fori(0, NG // 2) as i:
                    link = Link(dve, link_s, i, 6)
                    for u in range(2):
                        dve.wait_ge(summed, 2 * i + u + 3)
                        for j in range(G):
                            last = dve.tensor_tensor(
                                flat(c.resid[:CLS, bass.ds(8 * i + 4 * u + j, 1), :]),
                                acc[:CLS, 2 * u + j // 2, j % 2 * D:(j % 2 + 1) * D], base[:CLS, :], ALU.add)
                        link.after(last)
                        last = stats(dve, link, six, [
                            (c.tile(8 * i + 4 * u + j), flat(c.moments[:T, bass.ds(8 * i + 4 * u + j, 1), :]))
                            for j in range(G)])
                        last.then_inc(acc_free, 1)
                        dve.wait_ge(acc_free, 2 * i + u + 3)
                    link.end()


def store(c, out):
    (stored,) = c.sems("stored", "out")
    with c.nc.Block() as block:
        @block.sync
        def _(sp):
            sp.dma_start(out.rearrange("b t d -> t b d"), c.resid[:T, :, :]).then_inc(stored, 16)
            sp.wait_ge(stored, 16)



def normalize(dve, c, z, g, scale=None):
    for j in range(G):
        b = G * g + j
        last = dve.tensor_scalar(z[:T, j, :], c.tile(b), c.mean(b),
                                 c.scale(b) if scale is None else scale[:T, bass.ds(b, 1)],
                                 ALU.subtract, ALU.mult)
    return last


def to_features(pe, c, out, x):
    for k in range(KD):
        for j in range(G):
            last = pe.transpose(out[:, k, j * T:(j + 1) * T], x[:T, j, k * P:(k + 1) * P], c.ident[:T, :T])
    return last


def feature_product(pe, out, weight, xt):
    for m in range(KD):
        for k in range(KD):
            last = pe.matmul(out[:, m, :N], weight[:, k, m * P:(m + 1) * P], xt[:, k, :],
                             start=k == 0, stop=k == KD - 1)
    return last


def token_product(pe, out, xt, weight, bias=None, ones=None):
    for j in range(G):
        dst = out[:T, j // 2, j % 2 * D:(j % 2 + 1) * D]
        for k in range(KD):
            last = pe.matmul(dst, xt[:, k, j * T:(j + 1) * T], weight[:, k, :],
                             start=k == 0, stop=k == KD - 1 and bias is None)
        if bias is not None:
            last = pe.matmul(dst, ones[0:1, :T], bias[0:1, :], start=False, stop=True)
    return last


def add_to_residual(dve, c, y, g):
    for j in range(G):
        b = G * g + j
        last = dve.tensor_tensor(c.tile(b), y[:T, j // 2, j % 2 * D:(j % 2 + 1) * D], c.tile(b), ALU.add)
    return last


def tile_stats(dve, c, link, six, g):
    return stats(dve, link, six, [(c.tile(G * g + j), flat(c.moments[:T, bass.ds(G * g + j, 1), :]))
                                  for j in range(G)])


RFF = 128
TAU_1 = 6.28125
TAU_2 = float(np.float32(round((2 * math.pi - TAU_1) * 2.0 ** 22) / 2.0 ** 22))
TAU_3 = 2 * math.pi - TAU_1 - TAU_2
TAU_IN = 2 * math.pi * (1 - 2.0 ** -22)


def random_feature_attention(c, a):
    nc = c.nc
    inverse_deviation(c, 1e-5, "rff")
    with ExitStack() as st:
        wq, wk, wv, wp = (c.sb(st, f"rff_w{n}", [P, KD, D]) for n in "qkvp")
        wr = c.sb(st, "rff_wr", [P, H, RFF])
        br = c.sb(st, "rff_br", [P, H])
        brs = c.sb(st, "rff_brs", [P, H])
        turns = c.sb(st, "rff_turns", [P, H])
        bp = c.sb(st, "rff_bp", [1, D])
        quarter = c.sb(st, "rff_quarter", [P, 1])
        z = c.sb(st, "rff_z", [P, G, D])
        zt = c.sb(st, "rff_zt", [P, KD, N])
        qt = c.sb(st, "rff_qt", [P, KD, N])
        kt = c.sb(st, "rff_kt", [P, KD, N])
        v1 = c.sb(st, "rff_v1", [P, G, H, DH + 1])
        rounded = c.sb(st, "rff_rounded", [P, 2, 2, N])
        less = c.sb(st, "rff_less", [P, 2, 2, N])
        size = c.sb(st, "rff_size", [P, 2, 2, N])
        sines = c.sb(st, "rff_sines", [P, 2, 2, N])
        cosines = c.sb(st, "rff_cosines", [P, 2, 2, N])
        pair = c.sb(st, "rff_pair", [P, 2, N])
        mixed = c.sb(st, "rff_mixed", [P, H, G, DH + 1])
        inverse = c.sb(st, "rff_inverse", [P, H, G])
        o = c.sb(st, "rff_o", [P, G, D])
        ot = c.sb(st, "rff_ot", [P, KD, N])
        six = c.sb(st, "rff_six", [P, G, 9])
        pg = c.banks(st, "rff_pg", 2)
        pp = c.banks(st, "rff_pp", 4)
        pa = c.banks(st, "rff_pa", 2)
        (w_in, wr_in, cleared, fixed, prep_s, z_ready, zt_sum, zt_ready, qk_sum, qk_ready, v_sum, v_ready,
         angle_sum, less_ready, size_ready, waves_ready, pair_sum, pair_ready, mix_sum, mix_ready,
         o_ready, ot_sum, ot_ready, y_sum, done, link_s) = c.sems(
            "w_in wr_in cleared fixed prep z_ready zt_sum zt_ready qk_sum qk_ready v_sum v_ready "
            "angle_sum less_ready size_ready waves_ready pair_sum pair_ready mix_sum mix_ready "
            "o_ready ot_sum ot_ready y_sum done link", "rff")

        with nc.Block() as block:
            @block.sync
            def _(sp):
                for w, name in ((wq, "rff_wq"), (wk, "rff_wk"), (wv, "rff_wv"), (wp, "rff_wp"),
                                (br, "rff_br"), (bp, "rff_bp")):
                    sp.dma_start(w[:], a[name]).then_inc(w_in, 16)
                sp.wait_ge(cleared, 1)
                for s in range(P // DH):
                    sp.dma_start(wr[DH * s:DH * (s + 1), s:H:P // DH, :], a["rff_wr"][:, s:H:P // DH, :])\
                      .then_inc(wr_in, 16)

            @block.tensor
            def _(pe):
                pe.sem_inc(pair_sum, 2)
                pe.sem_inc(mix_sum, 2)
                pe.wait_ge(w_in, 96)
                pe.wait_ge(fixed, 1)
                with pe.Fori(0, NG) as g:
                    pe.wait_ge(z_ready, g + 1)
                    to_features(pe, c, pg, z).then_inc(zt_sum, 1)
                    pe.wait_ge(zt_ready, g + 1)
                    pe.wait_ge(done, g + 1)
                    feature_product(pe, pp[:, 0:2], wq, zt)
                    feature_product(pe, pp[:, 2:4], wk, zt).then_inc(qk_sum, 1)
                    token_product(pe, pg, zt, wv).then_inc(v_sum, 1)
                    pe.wait_ge(qk_ready, g + 1)

                    def angles(h):
                        if h < 2:
                            pe.wait_ge(qk_ready, g + 1)
                        else:
                            pe.wait_ge(less_ready, H * g + h - 2 + 1)
                        for s, src in enumerate((qt, kt)):
                            last = pe.matmul(pp[:, 2 * (h % 2) + s, :N], wr[:, h, :], src[:, h // 8, :],
                                             start=True, stop=True)
                        last.then_inc(angle_sum, 1)

                    def pairs(h):
                        pe.wait_ge(waves_ready, H * g + h + 3)
                        pe.wait_ge(pair_ready, H * g + h + 1)
                        for j in range(G):
                            t = slice(j * T, (j + 1) * T)
                            for n, waves in enumerate((cosines, sines)):
                                last = pe.matmul(pa[:T, h % 2, t], waves[:, h % 2, 1, t], waves[:, h % 2, 0, t],
                                                 start=n == 0, stop=n == 1)
                        last.then_inc(pair_sum, 1)

                    def mix(h):
                        pe.wait_ge(pair_ready, H * g + h + 3)
                        if h == 0:
                            pe.wait_ge(v_ready, g + 1)
                        if h % 4 == 0 and h >= 8:
                            pe.wait_ge(mix_ready, 4 * g + h // 4 - 1)
                        for j in range(G):
                            at = (DH + 1) * (G * (h % 4) + j)
                            last = pe.matmul(pg[:T, h // 4 % 2, at:at + DH + 1], pair[:T, h % 2, j * T:(j + 1) * T],
                                             v1[:T, j, h, :], start=True, stop=True)
                        last.then_inc(mix_sum, 1)

                    angles(0)
                    angles(1)
                    for h in range(H):
                        pairs(h)
                        if h + 2 < H:
                            angles(h + 2)
                        if h >= 1:
                            mix(h - 1)
                    mix(H - 1)
                    pe.wait_ge(o_ready, g + 1)
                    to_features(pe, c, pg, o).then_inc(ot_sum, 1)
                    pe.wait_ge(ot_ready, g + 1)
                    token_product(pe, pp[:, 0:2], ot, wp, bp, c.ones).then_inc(y_sum, 1)

            @block.scalar
            def _(act):
                act.sem_inc(waves_ready, 2)
                act.wait_ge(fixed, 1)
                with act.Fori(0, NG) as g:
                    act.wait_ge(zt_sum, g + 1)
                    act.activation(zt[:], pg[:, :, :N], ACT.Copy).then_inc(zt_ready, 1)
                    act.wait_ge(qk_sum, g + 1)
                    act.activation(qt[:], pp[:, 0:2, :N], ACT.Copy)
                    act.activation(kt[:], pp[:, 2:4, :N], ACT.Copy).then_inc(qk_ready, 1)

                    for h in range(H):
                        act.wait_ge(less_ready, H * g + h + 1)
                        act.activation(size[:, h % 2], less[:, h % 2], ACT.Abs, bias=br[:, h:h + 1],
                                       scale=-1.0).then_inc(size_ready, 1)
                        act.wait_ge(pair_sum, H * g + h + 1)
                        act.activation(sines[:, h % 2], less[:, h % 2], ACT.Sin, bias=brs[:, h:h + 1],
                                       scale=-TAU_IN)
                        act.wait_ge(size_ready, H * g + h + 1)
                        act.activation(cosines[:, h % 2], size[:, h % 2], ACT.Sin, bias=quarter[:, 0:1],
                                       scale=-TAU_IN).then_inc(waves_ready, 1)
                    act.wait_ge(ot_sum, g + 1)
                    act.activation(ot[:], pg[:, :, :N], ACT.Copy).then_inc(ot_ready, 1)

            @block.vector
            def _(dve):
                dve.memset(wr[:], 0.0).then_inc(cleared, 1)
                dve.memset(v1[:, :, :, DH:DH + 1], 1.0)
                dve.memset(quarter[:], math.pi / 2)
                prep = Link(dve, prep_s)
                dve.wait_ge(w_in, 96)
                prep.after(dve.tensor_scalar(turns[:], br[:], 1 / (2 * math.pi), ROUND, ALU.mult, ALU.add))
                prep.after(dve.tensor_scalar(turns[:], turns[:], ROUND, None, ALU.subtract))
                for part in (TAU_1, TAU_2, TAU_3):
                    prep.after(dve.scalar_tensor_tensor(br[:], turns[:], -part, br[:], ALU.mult, ALU.add))
                prep.after(dve.tensor_scalar(br[:], br[:], 1 / (2 * math.pi), None, ALU.mult))
                dve.tensor_scalar(brs[:], br[:], TAU_IN, None, ALU.mult)
                dve.wait_ge(wr_in, 16 * (P // DH))
                dve.tensor_scalar(wr[:], wr[:], 1 / (2 * math.pi), None, ALU.mult).then_inc(fixed, 1)
                dve.sem_inc(done, 1)
                dve.sem_inc(pair_ready, 2)
                with dve.Fori(0, NG) as g:
                    link = Link(dve, link_s, g, H + 5)
                    normalize(dve, c, z, g).then_inc(z_ready, 1)
                    dve.wait_ge(v_sum, g + 1)
                    for n in range(2):
                        last = dve.tensor_copy(v1[:T, 2 * n:2 * n + 2, :, 0:DH],
                                               pg[:T, n, :].rearrange("p (j h d) -> p j h d", j=2, h=H))
                    last.then_inc(v_ready, 1)

                    def keep_pair(h):
                        dve.wait_ge(pair_sum, H * g + h + 3)
                        dve.wait_ge(mix_sum, H * g + h + 1)
                        dve.tensor_copy(pair[:T, h % 2, :], pa[:T, h % 2, :N]).then_inc(pair_ready, 1)

                    def keep_mix(q):
                        dve.wait_ge(mix_sum, H * g + 4 * q + 3 + 3)
                        dve.tensor_copy(mixed[:T, 4 * q:4 * q + 4].rearrange("p h j d -> p (h j d)"),
                                        pg[:T, q % 2, :4 * G * (DH + 1)]).then_inc(mix_ready, 1)

                    for h in range(H):
                        angle = pp[:, 2 * (h % 2):2 * (h % 2) + 2, :N]
                        dve.wait_ge(angle_sum, H * g + h + 1)
                        dve.wait_ge(waves_ready, H * g + h + 1)
                        link.after(dve.tensor_scalar(rounded[:, h % 2], angle, br[:, h:h + 1], ROUND,
                                                     ALU.add, ALU.add))
                        last = dve.scalar_tensor_tensor(less[:, h % 2], rounded[:, h % 2], ROUND, angle,
                                                        ALU.subtract, ALU.subtract)
                        last.then_inc(less_ready, 1)
                        if h % 4 == 2 and h >= 6:
                            keep_mix(h // 4 - 1)
                        if h >= 1:
                            keep_pair(h - 1)
                    keep_pair(H - 1)
                    keep_mix(H // 4 - 1)
                    dve.wait_ge(mix_ready, 4 * g + 4)
                    link.after(dve.tensor_scalar(inverse[:T], mixed[:T, :, :, DH], 1e-6 * RFF, None, ALU.add))
                    link.after(dve.reciprocal(inverse[:T], inverse[:T]))
                    dve.tensor_tensor(o[:T].rearrange("p j (h d) -> p h j d", h=H), mixed[:T, :, :, 0:DH],
                                      inverse[:T].unsqueeze(3).to_broadcast([T, H, G, DH]), ALU.mult)\
                       .then_inc(o_ready, 1)
                    dve.wait_ge(y_sum, g + 1)
                    link.after(add_to_residual(dve, c, pp[:, 0:2], g))
                    tile_stats(dve, c, link, six, g).then_inc(done, 1)
                    link.end()


class Routing:

    def __init__(self, c, st, ph):
        self.ph = ph
        self.zt = c.sb(st, ph + "_zta", [P, KD, B * T])
        self.share = c.sb(st, ph + "_share", [P, B, E])


def gather_tokens(c, r, z_of, w_gate, gate_biases, w_norm, a):
    nc = c.nc
    with ExitStack() as st:
        wg = c.sb(st, r.ph + "_wg", [P, KD, E])
        extra = c.sb(st, r.ph + "_extra", [P, 2, E])
        norm = c.sb(st, r.ph + "_norm", [P, KD])
        z = c.sb(st, r.ph + "_z", [P, 2, G, D])
        zt = c.sb(st, r.ph + "_zt", [P, 2, KD, N])
        pt = c.banks(st, r.ph + "_pt", 4)
        pl = c.banks(st, r.ph + "_pl", 2)
        (w_in, z_ready, zt_sum, zt_ready, copied, logits_sum, logits_ready, link_s) = c.sems(
            "w_in z_ready zt_sum zt_ready copied logits_sum logits_ready link", r.ph + "_gather")
        names = [w_gate] + list(gate_biases) + ([w_norm] if w_norm else [])

        with nc.Block() as block:
            @block.sync
            def _(sp):
                sp.dma_start(wg[:], a[w_gate]).then_inc(w_in, 16)
                for n, name in enumerate(gate_biases):
                    sp.dma_start(extra[:T, n, :], row(a[name], T)).then_inc(w_in, 16)
                if w_norm:
                    sp.dma_start(norm[:], a[w_norm]).then_inc(w_in, 16)

            @block.tensor
            def _(pe):
                pe.sem_inc(zt_sum, 2)
                pe.sem_inc(logits_sum, 2)
                pe.wait_ge(w_in, 16 * len(names))
                with pe.Fori(0, NG // 2) as i:
                    for u in range(2):
                        n = 2 * i + u
                        pe.wait_ge(z_ready, n + 1)
                        pe.wait_ge(zt_ready, n + 1)
                        to_features(pe, c, pt[:, 2 * u:2 * u + 2], z[:, u]).then_inc(zt_sum, 1)
                        pe.wait_ge(zt_ready, n + 3)
                        pe.wait_ge(logits_ready, n + 1)
                        for j in range(G):
                            for k in range(KD):
                                last = pe.matmul(pl[:T, u, j * E:(j + 1) * E], zt[:, u, k, j * T:(j + 1) * T],
                                                 wg[:, k, :], start=k == 0, stop=k == KD - 1)
                        last.then_inc(logits_sum, 1)

            @block.scalar
            def _(act):
                act.sem_inc(zt_ready, 2)
                act.wait_ge(w_in, 16 * len(names))
                with act.Fori(0, NG // 2) as i:
                    for u in range(2):
                        n = 2 * i + u
                        act.wait_ge(zt_sum, n + 3)
                        act.wait_ge(logits_sum, n + 1)
                        act.wait_ge(copied, n + 1)
                        for k in range(KD):
                            last = act.activation(zt[:, u, k, :], pt[:, 2 * u + k, :N], ACT.Copy,
                                                  scale=norm[:, k:k + 1] if w_norm else 1.0)
                        last.then_inc(zt_ready, 1)

            @block.gpsimd
            def _(pool):
                pool.sem_inc(copied, 2)
                with pool.Fori(0, NG // 2) as i:
                    for u in range(2):
                        n = 2 * i + u
                        pool.wait_ge(zt_ready, n + 3)
                        pool.tensor_copy(r.zt[:, :, bass.ds(N * n, N)], zt[:, u]).then_inc(copied, 1)

            @block.vector
            def _(dve):
                dve.sem_inc(logits_ready, 2)
                dve.wait_ge(w_in, 16 * len(names))
                link = Link(dve, link_s)

                def logits(n, u):
                    dve.wait_ge(logits_sum, n + 3)
                    dst = r.share[:T, bass.ds(G * n, G), :]
                    src = pl[:T, u, :G * E].rearrange("p (j e) -> p j e", j=G)
                    bias = [extra[:T, m:m + 1, :].to_broadcast([T, G, E]) for m in range(len(gate_biases))]
                    if bias:
                        dve.tensor_tensor(dst, src, bias[0], ALU.add).then_inc(logits_ready, 1)
                        dve.wait_ge(logits_ready, n + 3)
                        for m in bias[1:]:
                            dve.tensor_tensor(dst, dst, m, ALU.add)
                    else:
                        dve.tensor_scalar(dst, src, 0.0, None, ALU.add).then_inc(logits_ready, 1)

                with dve.Fori(0, NG // 2) as i:
                    for u in range(2):
                        dve.wait_ge(zt_sum, 2 * i + u + 1)
                        z_of(dve, z[:, u], 2 * i + u).then_inc(z_ready, 1)
                    for u in range(2):
                        logits(2 * i + u, u)


def ranks(dve, link, r, above, tie, before, rank):
    mine = r.share[:T].unsqueeze(3).to_broadcast([T, B, E, E])
    other = r.share[:T].unsqueeze(2).to_broadcast([T, B, E, E])
    dve.tensor_tensor(above[:T], other, mine, ALU.is_gt)
    link.after(dve.tensor_tensor(tie[:T], other, mine, ALU.is_equal))
    link.after(dve.tensor_tensor(tie[:T], tie[:T],
                                 before[:T].unsqueeze(1).to_broadcast([T, B, E, E]), ALU.mult))
    link.after(dve.tensor_tensor(above[:T], above[:T], tie[:T], ALU.add))
    link.after(dve.tensor_reduce(rank[:T], above[:T], AX.X, ALU.add))


def lower_index(pool, made, before):
    pool.memset(before[:], 1.0).then_inc(made, 1)
    pool.wait_ge(made, 1)
    pool.affine_select(out=before[:], in_=before[:], compare_op=ALU.is_gt, fill=0.0, base=0,
                       pattern=[[1, E], [-1, E]], channel_multiplier=0).then_inc(made, 1)


def route_first(c, r, a):
    nc = c.nc
    with ExitStack() as st:
        above, tie = (c.sb(st, f"first_{n}", [P, B, E, E]) for n in ("above", "tie"))
        rank = c.sb(st, "first_rank", [P, B, E])
        before = c.sb(st, "first_before", [P, E, E])
        b2 = c.sb(st, "first_b2", [G * E, G, D])
        chosen = c.sb(st, "first_chosen", [G * E, 2, T])
        pc = c.banks(st, "first_pc", 2)
        py = c.banks(st, "first_py", 4)
        (b2_in, cleared, made, link_s, shared, turned, kept, y_sum, added) = c.sems(
            "b2_in cleared made link shared turned kept y_sum added", "first")
        with nc.Block() as block:
            @block.sync
            def _(sp):
                sp.wait_ge(cleared, 1)
                for j in range(G):
                    sp.dma_start(b2[j * E:(j + 1) * E, j, :], a["top1_b2"]).then_inc(b2_in, 16)

            @block.gpsimd
            def _(pool):
                pool.memset(b2[:], 0.0).then_inc(cleared, 1)
                lower_index(pool, made, before)

            @block.vector
            def _(dve):
                link = Link(dve, link_s)
                dve.wait_ge(made, 2)
                ranks(dve, link, r, above, tie, before, rank)
                dve.tensor_scalar(r.share[:T], rank[:T], 0.0, None, ALU.is_equal).then_inc(shared, 1)
                for g in range(NG):
                    dve.wait_ge(turned, g + 1)
                    if g >= 2:
                        dve.wait_ge(y_sum, g - 1)
                    dve.tensor_copy(chosen[:, g % 2, :], pc[:G * E, g % 2, :T]).then_inc(kept, 1)
                    dve.wait_ge(y_sum, g + 1)
                    add_to_residual(dve, c, py[:, 2 * (g % 2):2 * (g % 2) + 2], g).then_inc(added, 1)

            @block.tensor
            def _(pe):
                pe.wait_ge(shared, 1)
                pe.wait_ge(b2_in, 16 * G)
                for g in range(NG):
                    if g >= 2:
                        pe.wait_ge(kept, g - 1)
                    pe.transpose(pc[:G * E, g % 2, :T],
                                 r.share[:T, G * g:G * (g + 1), :].rearrange("p j e -> p (j e)"),
                                 c.ident[:T, :T]).then_inc(turned, 1)
                    pe.wait_ge(kept, g + 1)
                    if g >= 2:
                        pe.wait_ge(added, g - 1)
                    for m in range(2):
                        last = pe.matmul(py[:T, 2 * (g % 2) + m, :], chosen[:, g % 2, :],
                                         b2[:, 2 * m:2 * m + 2, :].rearrange("p j d -> p (j d)"),
                                         start=True, stop=True)
                    last.then_inc(y_sum, 1)


def experts(c, r, a, names, nf, func, bias):
    nc = c.nc
    w1n, w2n = names
    flat_share = r.share[:T].rearrange("p b e -> p (b e)")
    with ExitStack() as st:
        w1 = c.sb(st, r.ph + "_w1", [P, 2, KD, nf * P])
        w2 = c.sb(st, r.ph + "_w2", [P, 2, nf, D])
        b1 = c.sb(st, r.ph + "_b1", [P, 2, nf])
        loads = 3 if bias else 2
        inner = c.sb(st, r.ph + "_inner", [P, 2, nf, N])
        ph = c.banks(st, r.ph + "_ph", 4)
        py = c.banks(st, r.ph + "_py", 4)
        (w_in0, w_in1, inner_sum, inner_ready, y_sum, added) = c.sems(
            "w_in0 w_in1 inner_sum inner_ready y_sum added", r.ph + "_experts")
        w_in = (w_in0, w_in1)

        with nc.Block() as block:
            @block.sync
            def _(sp):
                with sp.Fori(0, E // 2) as i:
                    for v in range(2):
                        sp.wait_ge(y_sum, NG * (2 * i + v + 1))
                        sp.dma_start(w1[:, v], a[w1n][bass.ds(2 * i + v, 1)].rearrange(
                            "a p k f -> p (a k) f")).then_inc(w_in[v], 16)
                        if bias:
                            sp.dma_start(b1[:, v], a[bias][bass.ds(2 * i + v, 1)].rearrange(
                                "a p f -> p (a f)")).then_inc(w_in[v], 16)
                        sp.dma_start(w2[:, v], a[w2n][bass.ds(2 * i + v, 1)].rearrange(
                            "a p k f -> p (a k) f")).then_inc(w_in[v], 16)

            @block.tensor
            def _(pe):
                pe.sem_inc(y_sum, 2 * NG)
                with pe.Fori(0, E // 2) as i:
                    for v in range(2):
                        with pe.Fori(0, NG // 2) as q:
                            for u in range(2):
                                n = NG * (2 * i + v) + 2 * q + u
                                if u == 0:
                                    pe.wait_ge(w_in[v], 16 * loads * (i + 1))
                                for f in range(nf):
                                    bank = (nf * u + f) % 4
                                    pe.wait_ge(inner_ready, nf * n + f + 1)
                                    for k in range(KD):
                                        last = pe.matmul(ph[:, bank, :N], w1[:, v, k, f * P:(f + 1) * P],
                                                         r.zt[:, k, bass.ds(N * (2 * q + u), N)],
                                                         start=k == 0, stop=k == KD - 1)
                                    last.then_inc(inner_sum, 1)
                                pe.wait_ge(added, n + 1)
                                for j in range(G):
                                    for f in range(nf):
                                        if j == 0:
                                            pe.wait_ge(inner_ready, nf * n + f + 5)
                                        last = pe.matmul(py[:T, 2 * u + j // 2, j % 2 * D:(j % 2 + 1) * D],
                                                         inner[:, u, f, j * T:(j + 1) * T], w2[:, v, f, :],
                                                         start=f == 0, stop=f == nf - 1)
                                last.then_inc(y_sum, 1)

            @block.scalar
            def _(act):
                act.sem_inc(inner_ready, 4)
                with act.Fori(0, E // 2) as i:
                    for v in range(2):
                        with act.Fori(0, NG // 2) as q:
                            for u in range(2):
                                n = NG * (2 * i + v) + 2 * q + u
                                if bias and u == 0:
                                    act.wait_ge(w_in[v], 16 * loads * (i + 1))
                                act.wait_ge(y_sum, 2 * NG + n - 1)
                                for f in range(nf):
                                    act.wait_ge(inner_sum, nf * n + f + 1)
                                    act.activation(inner[:, u, f, :], ph[:, (nf * u + f) % 4, :N], func,
                                                   bias=b1[:, v, f:f + 1] if bias else 0.0).then_inc(inner_ready, 1)

            @block.vector
            def _(dve):
                dve.sem_inc(added, 2)
                with dve.Fori(0, E // 2) as i:
                    for v in range(2):
                        with dve.Fori(0, NG // 2) as q:
                            for u in range(2):
                                n = NG * (2 * i + v) + 2 * q + u
                                dve.wait_ge(y_sum, 2 * NG + n + 1)
                                dve.wait_ge(added, n + 2)
                                for j in range(G):
                                    b = G * (2 * q + u) + j
                                    last = dve.scalar_tensor_tensor(
                                        c.tile(b), py[:T, 2 * u + j // 2, j % 2 * D:(j % 2 + 1) * D],
                                        flat_share[:, bass.ds(E * b + 2 * i + v, 1)], c.tile(b),
                                        ALU.mult, ALU.add)
                                last.then_inc(added, 1)


def all_stats(c, ph):
    with ExitStack() as st:
        six = c.sb(st, ph + "_six", [P, G, 9])
        link_s, done = c.sems("link done", ph + "_stats")
        with c.nc.Block() as block:
            @block.vector
            def _(dve):
                dve.sem_inc(done, 1)
                with dve.Fori(0, NG) as g:
                    link = Link(dve, link_s, g, 2)
                    dve.wait_ge(done, g + 1)
                    tile_stats(dve, c, link, six, g).then_inc(done, 1)
                    link.end()


def top1_experts(c, a):
    inverse_deviation(c, 1e-5, "top1")
    with ExitStack() as st:
        r = Routing(c, st, "top1")
        gather_tokens(c, r, lambda dve, z, g: normalize(dve, c, z, g), "top1_wg",
                      ("top1_gate_b", "top1_expert_bias"), None, a)
        route_first(c, r, a)
        experts(c, r, a, ("top1_w1", "top1_w2"), FF // P, ACT.Relu, "top1_b1")
    all_stats(c, "top1")


class Attention:

    def __init__(self, ph, dm=DH, kv=H, scale=DH ** -0.5, causal=False, affine=False, norm=None,
                 differential=False, keep=None):
        self.ph, self.dm, self.kv, self.scale, self.causal = ph, dm, kv, scale, causal
        self.affine, self.norm, self.differential, self.keep = affine, norm, differential, keep


NX = 16
LAMBDA_INIT = 0.8 - 0.6 * math.exp(-0.3 * 12)
LARGEST = float(np.finfo(np.float32).max)


def softmax_attention(c, a, s):
    nc = c.nc
    ph, dm = s.ph, s.dm
    maps = D // dm
    nr = G * maps // NX
    nh = P // dm
    share = maps // H
    with ExitStack() as st:
        wq, wk, wo = (c.sb(st, f"{ph}_w{n}", [P, KD, D]) for n in "qko")
        wv = c.sb(st, ph + "_wv", [P, KD, s.kv * DH])
        fore = c.sb(st, ph + "_fore", [P, 2, KD])
        factors = c.sb(st, ph + "_factors", [P, 4])
        vbias = c.sb(st, ph + "_vbias", [P, D])
        obias = c.sb(st, ph + "_obias", [P, D])
        norm = c.sb(st, ph + "_norm", [P, KD])
        lam = c.sb(st, ph + "_lam", [P, 4, 8])
        lams = c.sb(st, ph + "_lams", [P, 2])
        neglam = c.sb(st, ph + "_neglam", [P, 1])
        subln = c.sb(st, ph + "_subln", [P, DH])
        own = c.sb(st, ph + "_own", [P, nh])
        future = c.sb(st, ph + "_future", [P, 4, T], BF16)
        identh = c.sb(st, ph + "_identh", [P, P], BF16)
        scale2 = c.sb(st, ph + "_scale2", [P, B])
        z = c.sb(st, ph + "_z", [P, G, D])
        zt = c.sb(st, ph + "_zt", [P, KD, N])
        qt = c.sb(st, ph + "_qt", [P, KD, N])
        kt = c.sb(st, ph + "_kt", [P, KD, N])
        km = c.sb(st, ph + "_km", [P, 2, NX, T])
        v1 = c.sb(st, ph + "_v1", [P, G, s.kv, DH + 1])
        most = c.sb(st, ph + "_most", [P, 2, NX])
        p = c.sb(st, ph + "_p", [P, 2, NX, T])
        pt = c.sb(st, ph + "_pt", [P, 2, NX, T])
        inverse = c.sb(st, ph + "_inverse", [P, NX])
        two = c.sb(st, ph + "_two", [P, NX, DH])
        o = c.sb(st, ph + "_o", [P, G, D])
        squares = c.sb(st, ph + "_squares", [P, G, D])
        roots = c.sb(st, ph + "_roots", [P, G * H])
        ot = c.sb(st, ph + "_ot", [P, KD, N])
        six = c.sb(st, ph + "_six", [P, G, 9])
        ps = c.banks(st, ph + "_ps", 4)
        pp = c.banks(st, ph + "_pp", 2)
        po = c.banks(st, ph + "_po", 1)
        (w_in, own_made, fixed, prep_s, lam_sum, lam_exp, z_ready, zt_sum, zt_ready, qk_sum, qk_ready, v_sum,
         v_ready, masked, score_sum, less_ready, exp_ready, turned, kept, mix_sum, mix_ready, square_ready,
         root_ready, o_ready, ot_sum, ot_ready, y_sum, done, link_s) = c.sems(
            "w_in own_made fixed prep lam_sum lam_exp z_ready zt_sum zt_ready qk_sum qk_ready v_sum "
            "v_ready masked score_sum less_ready exp_ready turned kept mix_sum mix_ready square_ready "
            "root_ready o_ready ot_sum ot_ready y_sum done link", ph)
        loads = [(wq[:], a[ph + "_wq"]), (wk[:], a[ph + "_wk"]), (wv[:], a[ph + "_wv"]), (wo[:], a[ph + "_wo"])]
        if s.affine:
            loads += [(fore[:, 0, :], a[ph + "_bq"]), (fore[:, 1, :], a[ph + "_bk"]),
                      (vbias[:T, :], row(a[ph + "_bv"], T)), (obias[:T, :], row(a[ph + "_bo"], T))]
            loads += [(factors[:, n:n + 1], row(a[f"{ph}_s{x}"], P)) for n, x in enumerate("qkvo")]
        if s.norm:
            loads += [(norm[:], a[s.norm])]
        if s.differential:
            loads += [(lam[:T, n, :], row(a[f"{ph}_lambda_{x}"], T)) for n, x in enumerate(("q1", "k1", "q2", "k2"))]
            loads += [(subln[:T, :], row(a[ph + "_subln"], T))]

        links = nr * (4 if s.differential else 2) + (3 if not (s.affine or s.keep is not None) else 4) + 5 * s.differential

        def half(x):
            return x // nh

        def at(n):
            return n * NX // maps, n % (maps // NX)

        with nc.Block() as block:
            @block.sync
            def _(sp):
                for dst, src in loads:
                    sp.dma_start(dst, src).then_inc(w_in, 16)

            @block.gpsimd
            def _(pool):
                pool.memset(own[:], 1.0).then_inc(own_made, 1)
                pool.memset(future[:], 0.0).then_inc(own_made, 1)
                pool.tensor_copy(identh[:], c.ident[:]).then_inc(own_made, 1)
                pool.wait_ge(own_made, 3)
                pool.affine_select(out=own[:], in_=own[:], compare_op=ALU.is_ge, fill=0.0, base=0,
                                   pattern=[[-dm, nh]], channel_multiplier=1).then_inc(own_made, 1)
                pool.affine_select(out=future[:], in_=future[:], compare_op=ALU.is_ge, fill=-1e30, base=0,
                                   pattern=[[0, 4], [-1, T]], channel_multiplier=1).then_inc(own_made, 1)
                pool.wait_ge(own_made, 5)
                pool.affine_select(out=own[:], in_=own[:], compare_op=ALU.is_ge, fill=0.0, base=dm - 1,
                                   pattern=[[dm, nh]], channel_multiplier=-1).then_inc(own_made, 1)
                pool.wait_ge(own_made, 6)
                with pool.Fori(0, NG) as g:
                    pool.wait_ge(qk_ready, g + 1)
                    for n in range(nr):
                        j, m0 = at(n)
                        pool.wait_ge(score_sum, nr * g + n + 1)
                        for x in range(0, NX, nh):
                            src = kt[:, m0 + x // nh, j * T:(j + 1) * T]
                            last = pool.tensor_tensor(
                                km[:, n % 2, x:x + nh, :], src.unsqueeze(1).to_broadcast([P, nh, T]),
                                own[:].unsqueeze(2).to_broadcast([P, nh, T]), ALU.mult)
                        last.then_inc(masked, 1)

            @block.tensor
            def _(pe):
                pe.sem_inc(score_sum, 2)
                pe.sem_inc(mix_sum, 2)
                pe.wait_ge(w_in, 16 * len(loads))
                pe.wait_ge(own_made, 6)
                with pe.Fori(0, NG) as g:
                    pe.wait_ge(z_ready, g + 1)
                    to_features(pe, c, pp, z).then_inc(zt_sum, 1)
                    pe.wait_ge(zt_ready, g + 1)
                    pe.wait_ge(done, g + 1)
                    feature_product(pe, ps[:, 0:2], wq, zt)
                    feature_product(pe, ps[:, 2:4], wk, zt).then_inc(qk_sum, 1)
                    for j in range(G):
                        for k in range(KD):
                            last = pe.matmul(pp[:T, j // 2, j % 2 * D:j % 2 * D + s.kv * DH],
                                             zt[:, k, j * T:(j + 1) * T], wv[:, k, :],
                                             start=k == 0, stop=k == KD - 1)
                    last.then_inc(v_sum, 1)
                    pe.wait_ge(qk_ready, g + 1)

                    def scores(n):
                        j, m0 = at(n)
                        pe.wait_ge(masked, nr * g + n + 1)
                        if n:
                            pe.wait_ge(less_ready, nr * g + n)
                        for x in range(0, NX, 4):
                            if s.causal:
                                pe.matmul(ps[:T, x // 4, :N], identh[:T, :T],
                                          future[:T].rearrange("p x t -> p (x t)"), start=True, stop=False)
                            last = pe.matmul(ps[:T, x // 4, :N], qt[:, m0 + half(x), j * T:(j + 1) * T],
                                             km[:, n % 2, x:x + 4, :].rearrange("p x t -> p (x t)"),
                                             start=not s.causal, stop=True)
                        last.then_inc(score_sum, 1)

                    def turn(n, q):
                        if q == 0:
                            pe.wait_ge(exp_ready, nr * g + n + 1)
                        if n == 0 and q == 0:
                            pe.wait_ge(v_ready, g + 1)
                        if 4 * n + q >= 2:
                            pe.wait_ge(kept, 4 * (nr * g + n) + q - 1)
                        for x in range(4):
                            last = pe.transpose(pp[:T, q % 2, x * T:(x + 1) * T], p[:T, n % 2, 4 * q + x, :],
                                                c.ident[:T, :T])
                        last.then_inc(turned, 1)

                    def mix(n, q):
                        j, m0 = at(n)
                        pe.wait_ge(kept, 4 * (nr * g + n) + q + 1)
                        if q == 0:
                            pe.wait_ge(mix_ready, nr * g + n + 1)
                        for x in range(4 * q, 4 * q + 4):
                            head = (m0 * NX + x) // share // (H // s.kv)
                            last = pe.matmul(po[:T, 0, x * (DH + 1):(x + 1) * (DH + 1)], pt[:T, n % 2, x, :],
                                             v1[:T, j, head, :], start=True, stop=True)
                        if q == 3:
                            last.then_inc(mix_sum, 1)

                    scores(0)
                    for n in range(nr):
                        if n + 1 < nr:
                            scores(n + 1)
                        for q in range(4):
                            turn(n, q)
                            if q:
                                mix(n, q - 1)
                        mix(n, 3)
                    if s.differential:
                        pe.wait_ge(o_ready, g + 1)
                    else:
                        pe.wait_ge(mix_ready, nr * (g + 1) + 1)
                    to_features(pe, c, pp, o).then_inc(ot_sum, 1)
                    pe.wait_ge(ot_ready, g + 1)
                    token_product(pe, ps[:, 0:2], ot, wo).then_inc(y_sum, 1)

            @block.scalar
            def _(act):
                act.wait_ge(w_in, 16 * len(loads))
                if s.differential:
                    act.wait_ge(lam_sum, 1)
                    act.activation(lams[:T, :], lams[:T, :], ACT.Exp).then_inc(lam_exp, 1)
                if s.keep is not None:
                    act.wait_ge(lam_sum, 1)
                    act.activation(scale2[:T, :], scale2[:T, :], ACT.Sqrt).then_inc(lam_exp, 1)
                with act.Fori(0, NG) as g:
                    act.wait_ge(zt_sum, g + 1)
                    for k in range(KD):
                        last = act.activation(zt[:, k, :], pp[:, k, :N], ACT.Copy,
                                              scale=norm[:, k:k + 1] if s.norm else 1.0)
                    last.then_inc(zt_ready, 1)
                    act.wait_ge(qk_sum, g + 1)
                    for n, dst in enumerate((qt, kt)):
                        for m in range(KD):
                            if s.affine:
                                last = act.activation(dst[:, m, :], ps[:, 2 * n + m, :N], ACT.Identity,
                                                      bias=fore[:, n, m:m + 1], scale=factors[:, n:n + 1])
                            else:
                                last = act.activation(dst[:, m, :], ps[:, 2 * n + m, :N], ACT.Copy)
                    last.then_inc(qk_ready, 1)
                    for n in range(nr):
                        r = nr * g + n
                        act.wait_ge(less_ready, r + 1)
                        act.activation(p[:T, n % 2], p[:T, n % 2], ACT.Exp, scale=s.scale).then_inc(exp_ready, 1)
                        act.wait_ge(mix_sum, r + 1)
                        for q in range(4):
                            act.wait_ge(turned, 4 * r + q + 1)
                            act.activation(pt[:T, n % 2, 4 * q:4 * q + 4, :].rearrange("p x t -> p (x t)"),
                                           pp[:T, q % 2, :N], ACT.Copy).then_inc(kept, 1)
                    if s.differential:
                        act.wait_ge(square_ready, g + 1)
                        act.activation(roots[:T, :], roots[:T, :], ACT.Sqrt).then_inc(root_ready, 1)
                    act.wait_ge(ot_sum, g + 1)
                    act.activation(ot[:], pp[:, :, :N], ACT.Copy).then_inc(ot_ready, 1)

            @block.vector
            def _(dve):
                dve.memset(v1[:], 1.0)
                prep = Link(dve, prep_s)
                dve.wait_ge(w_in, 16 * len(loads))
                if s.differential:
                    for n in range(2):
                        last = dve.tensor_tensor(lam[:T, 2 * n, :], lam[:T, 2 * n, :], lam[:T, 2 * n + 1, :], ALU.mult)
                    prep.after(last)
                    dve.tensor_reduce(lams[:T, :], lam[:T, 0:4:2, :], AX.X, ALU.add).then_inc(lam_sum, 1)
                    dve.wait_ge(lam_exp, 1)
                    prep.after(dve.tensor_tensor(neglam[:T, :], lams[:T, 1:2], lams[:T, 0:1], ALU.subtract))
                    dve.tensor_scalar(neglam[:T, :], neglam[:T, :], -LAMBDA_INIT, None, ALU.add)
                    dve.tensor_scalar(subln[:T, :], subln[:T, :], 1.0 - LAMBDA_INIT, None, ALU.mult)
                if s.keep is not None:
                    prep.after(dve.tensor_tensor(scale2[:T, :], c.rstd[:T, :], c.rstd[:T, :], ALU.mult))
                    prep.after(dve.tensor_tensor(scale2[:T, :], scale2[:T, :], c.moments[:T, :, 1], ALU.mult))
                    dve.tensor_scalar(scale2[:T, :], scale2[:T, :], 1e-6, None, ALU.add).then_inc(lam_sum, 1)
                    dve.wait_ge(lam_exp, 1)
                    prep.after(dve.reciprocal(scale2[:T, :], scale2[:T, :]))
                    prep.after(dve.tensor_tensor(scale2[:T, :], scale2[:T, :], c.rstd[:T, :], ALU.mult))
                prep.after(dve.memset(six[:], 0.0))
                dve.sem_inc(done, 1)
                dve.sem_inc(mix_ready, 1)
                with dve.Fori(0, NG) as g:
                    link = Link(dve, link_s, g, links)
                    normalize(dve, c, z, g, scale2 if s.keep is not None else None).then_inc(z_ready, 1)
                    dve.wait_ge(v_sum, g + 1)
                    for j in range(G):
                        src = pp[:T, j // 2, j % 2 * D:j % 2 * D + s.kv * DH]
                        dst = v1[:T, j, :, 0:DH]
                        if s.affine:
                            last = dve.scalar_tensor_tensor(
                                dst, src.rearrange("p (h d) -> p h d", d=DH), factors[:T, 2:3],
                                vbias[:T, :].rearrange("p (h d) -> p h d", d=DH), ALU.mult, ALU.add)
                        else:
                            last = dve.tensor_copy(dst, src.rearrange("p (h d) -> p h d", d=DH))
                    last.then_inc(v_ready, 1)

                    def subtract_most(n):
                        score = ps[:T, :, :N].rearrange("p c (x t) -> p c x t", x=4)
                        high = most[:T, n % 2, :]
                        dve.wait_ge(score_sum, nr * g + n + 3)
                        link.after(dve.tensor_reduce(high.rearrange("p (c x) -> p c x", c=4), score, AX.X, ALU.max))
                        if s.differential:
                            link.after(dve.tensor_scalar(high, high, LARGEST, -LARGEST, ALU.min, ALU.max))
                            for q in range(4):
                                last = dve.scalar_tensor_tensor(
                                    p[:T, n % 2, 4 * q:4 * q + 4, :], score[:, q], LARGEST,
                                    high[:, 4 * q:4 * q + 4].unsqueeze(2).to_broadcast([T, 4, T]),
                                    ALU.min, ALU.subtract)
                            last.then_inc(less_ready, 1)
                            return
                        dve.tensor_tensor(p[:T, n % 2].rearrange("p (c x) t -> p c x t", c=4), score,
                                          high.rearrange("p (c x) -> p c x", c=4).unsqueeze(3)
                                          .to_broadcast([T, 4, 4, T]), ALU.subtract).then_inc(less_ready, 1)

                    def divide(n):
                        j, m0 = at(n)
                        sums = po[:T, 0, :NX * (DH + 1)].rearrange("p (x d) -> p x d", x=NX)
                        dve.wait_ge(mix_sum, nr * g + n + 3)
                        link.after(dve.reciprocal(inverse[:T, :], sums[:, :, DH]))
                        if s.differential:
                            link.after(dve.tensor_scalar(inverse[:T, 1:NX:2], inverse[:T, 1:NX:2],
                                                         neglam[:T, 0:1], None, ALU.mult))
                        out = o[:T, j, :].rearrange("p (h d) -> p h d", d=DH) if not s.differential else two[:T]
                        last = dve.tensor_tensor(out, sums[:, :, 0:DH],
                                                 inverse[:T, :].unsqueeze(2).to_broadcast([T, NX, DH]), ALU.mult)
                        last.then_inc(mix_ready, 1)
                        if s.differential:
                            dve.wait_ge(mix_ready, nr * g + n + 2)
                            last = dve.tensor_tensor(
                                o[:T, j, m0 * P:(m0 + 1) * P].rearrange("p (h d) -> p h d", d=DH),
                                two[:T, 0:NX:2, :], two[:T, 1:NX:2, :], ALU.add)
                        return last

                    for n in range(nr):
                        subtract_most(n)
                        if n:
                            divide(n - 1)
                    last = divide(nr - 1)
                    if s.differential:
                        link.after(last)
                        heads = o[:T].rearrange("p j (h d) -> p (j h) d", d=DH)
                        flat_o = o[:T].rearrange("p j d -> p (j d)")
                        flat_s = squares[:T].rearrange("p j d -> p (j d)")
                        link.after(dve.tensor_tensor(flat_s, flat_o, flat_o, ALU.mult))
                        link.after(dve.tensor_reduce(roots[:T, :], flat_s.rearrange("p (x d) -> p x d", d=DH),
                                                     AX.X, ALU.add))
                        dve.tensor_scalar(roots[:T, :], roots[:T, :], 1 / DH, 1e-5, ALU.mult,
                                          ALU.add).then_inc(square_ready, 1)
                        dve.wait_ge(root_ready, g + 1)
                        link.after(dve.reciprocal(roots[:T, :], roots[:T, :]))
                        link.after(dve.tensor_tensor(heads, heads, roots[:T, :].unsqueeze(2)
                                                     .to_broadcast([T, G * H, DH]), ALU.mult))
                        last = dve.tensor_tensor(heads, heads, subln[:T, :].unsqueeze(1)
                                                 .to_broadcast([T, G * H, DH]), ALU.mult)
                        last.then_inc(o_ready, 1)
                    if s.keep is not None:
                        dve.wait_ge(zt_sum, g + 1)
                        link.after(normalize(dve, c, z, g))
                    dve.wait_ge(y_sum, g + 1)
                    if s.affine:
                        for j in range(G):
                            last = dve.scalar_tensor_tensor(z[:T, j, :], ps[:T, j // 2, j % 2 * D:(j % 2 + 1) * D],
                                                            factors[:T, 3:4], obias[:T, :], ALU.mult, ALU.add)
                        link.after(last)
                        for j in range(G):
                            last = dve.tensor_tensor(c.tile(G * g + j), z[:T, j, :], c.tile(G * g + j), ALU.add)
                        link.after(last)
                        last = tile_stats(dve, c, link, six, g)
                    elif s.keep is not None:
                        for j in range(G):
                            last = dve.tensor_tensor(flat(s.keep[:T, bass.ds(G * g + j, 1), :]),
                                                     ps[:T, j // 2, j % 2 * D:(j % 2 + 1) * D], z[:T, j, :], ALU.add)
                        link.after(last)
                        for j in range(G):
                            b = G * g + j
                            last = dve.tensor_tensor(c.tile(b), flat(s.keep[:T, bass.ds(b, 1), :]), c.tile(b), ALU.add)
                        last = stats(dve, link, six, [(flat(s.keep[:T, bass.ds(G * g + j, 1), :]),
                                                       flat(c.moments[:T, bass.ds(G * g + j, 1), :]))
                                                      for j in range(G)])
                    else:
                        link.after(add_to_residual(dve, c, ps[:, 0:2], g))
                        last = tile_stats(dve, c, link, six, g)
                    last.then_inc(done, 1)
                    dve.wait_ge(done, g + 2)
                    link.end()


def scaled_attention(c, a):
    inverse_deviation(c, 1e-5, "tern")
    softmax_attention(c, a, Attention("tern", affine=True))


def weigh_two(c, r):
    with ExitStack() as st:
        above, tie = (c.sb(st, f"two_{n}", [P, B, E, E]) for n in ("above", "tie"))
        rank, taken = (c.sb(st, f"two_{n}", [P, B, E]) for n in ("rank", "taken"))
        before = c.sb(st, "two_before", [P, E, E])
        most, total = (c.sb(st, f"two_{n}", [P, B]) for n in ("most", "total"))
        made, link_s, less_ready, exp_ready = c.sems("made link less_ready exp_ready", "two")
        with c.nc.Block() as block:
            @block.gpsimd
            def _(pool):
                lower_index(pool, made, before)

            @block.scalar
            def _(act):
                act.wait_ge(less_ready, 1)
                act.activation(r.share[:T], r.share[:T], ACT.Exp).then_inc(exp_ready, 1)

            @block.vector
            def _(dve):
                link = Link(dve, link_s)
                dve.wait_ge(made, 2)
                ranks(dve, link, r, above, tie, before, rank)
                dve.tensor_scalar(taken[:T], rank[:T], 2.0, None, ALU.is_lt)
                link.after(dve.tensor_reduce(most[:T, :], r.share[:T], AX.X, ALU.max))
                dve.tensor_tensor(r.share[:T], r.share[:T], most[:T, :].unsqueeze(2).to_broadcast([T, B, E]),
                                  ALU.subtract).then_inc(less_ready, 1)
                dve.wait_ge(exp_ready, 1)
                link.after(dve.tensor_tensor(r.share[:T], r.share[:T], taken[:T], ALU.mult))
                link.after(dve.tensor_reduce(total[:T, :], r.share[:T], AX.X, ALU.add))
                link.after(dve.reciprocal(total[:T, :], total[:T, :]))
                link.after(dve.tensor_tensor(r.share[:T], r.share[:T],
                                             total[:T, :].unsqueeze(2).to_broadcast([T, B, E]), ALU.mult))


def linear_experts(c, r, a, name):
    nc = c.nc
    flat_share = r.share[:T].rearrange("p b e -> p (b e)")
    pairs = B // 2
    with ExitStack() as st:
        w = c.sb(st, r.ph + "_w", [P, KD, E * D])
        py = c.banks(st, r.ph + "_py", 8)
        w_in, y_sum, added = c.sems("w_in y_sum added", r.ph + "_experts")
        with nc.Block() as block:
            @block.sync
            def _(sp):
                sp.dma_start(w[:], a[name]).then_inc(w_in, 16)

            @block.tensor
            def _(pe):
                pe.wait_ge(w_in, 16)
                with pe.Fori(0, E) as e:
                    for n in range(pairs):
                        pe.wait_ge(added, pairs * e + n + 1)
                        for j in range(2):
                            b = 2 * n + j
                            for k in range(KD):
                                last = pe.matmul(py[:T, n % 8, j * D:(j + 1) * D], r.zt[:, k, b * T:(b + 1) * T],
                                                 w[:, k, bass.ds(D * e, D)], start=k == 0, stop=k == KD - 1)
                        last.then_inc(y_sum, 1)

            @block.vector
            def _(dve):
                dve.sem_inc(added, 8)
                with dve.Fori(0, E) as e:
                    for n in range(pairs):
                        dve.wait_ge(y_sum, pairs * e + n + 1)
                        dve.wait_ge(added, pairs * e + n + 1)
                        for j in range(2):
                            b = 2 * n + j
                            last = dve.scalar_tensor_tensor(
                                c.resid[:T, b, :], py[:T, n % 8, j * D:(j + 1) * D],
                                flat_share[:, bass.ds(E * b + e, 1)], c.resid[:T, b, :], ALU.mult, ALU.add)
                        last.then_inc(added, 1)


def grouped_block(c, a):
    inverse_deviation(c, 1e-5, "gqa")
    with ExitStack() as st:
        inner = c.sb(st, "gqa_inner", [P, B, D])
        softmax_attention(c, a, Attention("gqa", kv=4, causal=True, norm="gqa_norm", keep=inner))
        (squared,) = c.sems("squared", "gqa_square")
        with c.nc.Block() as block:
            @block.vector
            def _(dve):
                dve.tensor_tensor(c.rstd[:T, :], c.moments[:T, :, 0], c.moments[:T, :, 0], ALU.mult).then_inc(squared, 1)
                dve.wait_ge(squared, 1)
                dve.tensor_tensor(c.moments[:T, :, 1], c.moments[:T, :, 1], c.rstd[:T, :], ALU.add)\
                   .then_inc(squared, 1)
                dve.wait_ge(squared, 2)
        inverse_deviation(c, 1e-6, "gqa_rms")
        r = Routing(c, st, "top2")

        def rms(dve, z, g):
            for j in range(G):
                b = G * g + j
                last = dve.tensor_scalar(z[:T, j, :], flat(inner[:T, bass.ds(b, 1), :]), c.scale(b), None, ALU.mult)
            return last

        gather_tokens(c, r, rms, "top2_wg", (), "top2_norm", a)
        weigh_two(c, r)
        linear_experts(c, r, a, "top2_w")
    all_stats(c, "top2")


def differential_attention(c, a):
    inverse_deviation(c, 1e-5, "diff")
    softmax_attention(c, a, Attention("diff", dm=DH // 2, scale=(DH // 2) ** -0.5, differential=True))


CAPACITY = math.ceil(B * T / E)
ENOUGH = 0.9


def route_by_threshold(c, r):
    nc = c.nc
    with ExitStack() as st:
        above, tie = (c.sb(st, f"cap_{n}", [P, B, E, E]) for n in ("above", "tie"))
        rank, value, at_least, equal = (c.sb(st, f"cap_{n}", [P, B, E]) for n in ("rank", "value", "at_least", "equal"))
        places, runs, totals = (c.sb(st, f"cap_{n}", [P, E, B]) for n in ("places", "runs", "totals"))
        before = c.sb(st, "cap_before", [P, E, E])
        earlier = c.sb(st, "cap_earlier", [P, P])
        most = c.sb(st, "cap_most", [P, B])
        count, level, step, trial, room = (c.sb(st, f"cap_{n}", [P, E]) for n in ("count", "level", "step", "trial", "room"))
        pc = c.banks(st, "cap_pc", 3)
        made, link_s, less_ready, exp_ready, counted, summed, counted2, summed2, marked, prefixed, scan_s = c.sems(
            "made link less_ready exp_ready counted summed counted2 summed2 marked prefixed scan", "cap")
        steps = 27

        def per_expert(x):
            return x[:T].unsqueeze(1).to_broadcast([T, B, E])

        with nc.Block() as block:
            @block.gpsimd
            def _(pool):
                lower_index(pool, made, before)
                pool.memset(earlier[:], 1.0).then_inc(made, 1)
                pool.wait_ge(made, 3)
                pool.affine_select(out=earlier[:], in_=earlier[:], compare_op=ALU.is_gt, fill=0.0, base=0,
                                   pattern=[[1, P]], channel_multiplier=-1).then_inc(made, 1)

            @block.scalar
            def _(act):
                act.wait_ge(less_ready, 1)
                act.activation(r.share[:T], r.share[:T], ACT.Exp).then_inc(exp_ready, 1)

            @block.tensor
            def _(pe):
                with pe.Fori(0, steps) as i:
                    pe.wait_ge(counted, i + 1)
                    pe.matmul(pc[:, 0, :E], c.ones[:T, :], count[:T, :], start=True, stop=True).then_inc(summed, 1)
                pe.wait_ge(counted2, 1)
                pe.matmul(pc[:, 0, :E], c.ones[:T, :], count[:T, :], start=True, stop=True).then_inc(summed2, 1)
                pe.wait_ge(made, 4)
                pe.wait_ge(marked, 1)
                marks = equal[:T].rearrange("p b e -> p (b e)")
                pe.matmul(pc[:T, 1, :B * E], earlier[:T, :T], marks, start=True, stop=True)
                pe.matmul(pc[:T, 2, :B * E], c.ones[:T, :T], marks, start=True, stop=True).then_inc(prefixed, 1)

            @block.vector
            def _(dve):
                link = Link(dve, link_s)
                link.after(dve.tensor_reduce(most[:T, :], r.share[:T], AX.X, ALU.max))
                dve.tensor_tensor(r.share[:T], r.share[:T], most[:T, :].unsqueeze(2).to_broadcast([T, B, E]),
                                  ALU.subtract).then_inc(less_ready, 1)
                dve.wait_ge(exp_ready, 1)
                link.after(dve.tensor_reduce(most[:T, :], r.share[:T], AX.X, ALU.add))
                link.after(dve.reciprocal(most[:T, :], most[:T, :]))
                link.after(dve.tensor_tensor(r.share[:T], r.share[:T],
                                             most[:T, :].unsqueeze(2).to_broadcast([T, B, E]), ALU.mult))
                dve.wait_ge(made, 2)
                ranks(dve, link, r, above, tie, before, rank)
                link.after(dve.tensor_tensor(above[:T], above[:T],
                                             r.share[:T].unsqueeze(2).to_broadcast([T, B, E, E]), ALU.mult))
                link.after(dve.tensor_reduce(equal[:T], above[:T], AX.X, ALU.add))
                dve.tensor_scalar(at_least[:T], equal[:T], ENOUGH, None, ALU.is_lt)
                link.after(dve.tensor_scalar(rank[:T], rank[:T], 1.0, None, ALU.add))
                link.after(dve.tensor_tensor(value[:T], r.share[:T], rank[:T], ALU.subtract))
                dve.tensor_tensor(value[:T], value[:T], at_least[:T], ALU.mult)
                link.after(dve.tensor_scalar(equal[:T], at_least[:T], 1.0, 1e9, ALU.subtract, ALU.mult))
                dve.memset(level[:], -8.0)
                dve.memset(step[:], 4.0)
                link.after(dve.tensor_tensor(value[:T], value[:T], equal[:T], ALU.add))

                with dve.Fori(0, steps) as i:
                    loop = Link(dve, scan_s, i, 5)
                    loop.after(dve.tensor_tensor(trial[:T, :], level[:T, :], step[:T, :], ALU.add))
                    loop.after(dve.tensor_tensor(at_least[:T], value[:T], per_expert(trial), ALU.is_ge))
                    dve.tensor_reduce(count[:T, :], at_least[:T].rearrange("p b e -> p e b"), AX.X,
                                      ALU.add).then_inc(counted, 1)
                    dve.wait_ge(summed, i + 1)
                    loop.after(dve.scalar_tensor_tensor(trial[:T, :], pc[:T, 0, :E], float(CAPACITY), step[:T, :],
                                                        ALU.is_ge, ALU.mult))
                    dve.tensor_scalar(step[:T, :], step[:T, :], 0.5, None, ALU.mult)
                    loop.after(dve.tensor_tensor(level[:T, :], level[:T, :], trial[:T, :], ALU.add))
                    loop.after(dve.memset(room[:], 0.0))
                    loop.end()
                link.after(dve.tensor_tensor(at_least[:T], value[:T], per_expert(level), ALU.is_gt))
                dve.tensor_tensor(equal[:T], value[:T], per_expert(level), ALU.is_equal).then_inc(marked, 1)
                dve.tensor_reduce(count[:T, :], at_least[:T].rearrange("p b e -> p e b"), AX.X,
                                  ALU.add).then_inc(counted2, 1)
                dve.wait_ge(summed2, 1)
                dve.tensor_scalar(room[:T, :], pc[:T, 0, :E], -1.0, float(CAPACITY), ALU.mult, ALU.add)
                dve.memset(runs[:], 1.0)
                dve.wait_ge(prefixed, 1)
                link.after(dve.tensor_copy(totals[:T], pc[:T, 2, :B * E].rearrange("p (b e) -> p e b", e=E)))
                link.after(dve.memset(runs[:, :, 0:1], 0.0))
                link.after(dve.tensor_tensor_scan(places[:T].rearrange("p e b -> p (e b)"),
                                                  runs[:T].rearrange("p e b -> p (e b)"),
                                                  totals[:T].rearrange("p e b -> p (e b)"), 0.0, ALU.mult, ALU.add))
                link.after(dve.tensor_tensor(places[:T], places[:T], totals[:T], ALU.subtract))
                link.after(dve.tensor_tensor(rank[:T], places[:T].rearrange("p e b -> p b e"),
                                             pc[:T, 1, :B * E].rearrange("p (b e) -> p b e", e=E), ALU.add))
                link.after(dve.tensor_tensor(rank[:T], rank[:T], per_expert(room), ALU.is_lt))
                link.after(dve.tensor_tensor(rank[:T], rank[:T], equal[:T], ALU.mult))
                link.after(dve.tensor_tensor(rank[:T], rank[:T], at_least[:T], ALU.add))
                link.after(dve.tensor_tensor(r.share[:T], r.share[:T], rank[:T], ALU.mult))


def capacity_experts(c, a):
    inverse_deviation(c, 1e-5, "xmoe")
    with ExitStack() as st:
        r = Routing(c, st, "xmoe")
        gather_tokens(c, r, lambda dve, z, g: normalize(dve, c, z, g), "xmoe_wg", (), None, a)
        route_by_threshold(c, r)
        experts(c, r, a, ("xmoe_w1", "xmoe_w2"), D // P, ACT.Gelu, None)


def gated_linear_attention(c, a):
    nc = c.nc
    inverse_deviation(c, 1e-5, "gla")
    L = T + 1
    NH2 = P // DH
    with ExitStack() as st:
        wqf = c.sb(st, "gla_wqf", [P, KD, 2 * D])
        wv, wo = (c.sb(st, f"gla_w{n}", [P, KD, D]) for n in "vo")
        own = c.sb(st, "gla_own", [P, NH2])
        falls = c.sb(st, "gla_falls", [P, L])
        nexts = c.sb(st, "gla_nexts", [P, T])
        z = c.sb(st, "gla_z", [P, G, D])
        zt = c.sb(st, "gla_zt", [P, KD, N])
        rows = c.sb(st, "gla_rows", [P, G, 2, D])
        high, total = (c.sb(st, f"gla_{n}", [P, G * 2]) for n in ("high", "total"))
        v = c.sb(st, "gla_v", [P, G, D])
        fall = c.sb(st, "gla_fall", [P, G, D])
        after = c.sb(st, "gla_after", [P, G, D])
        wide = c.sb(st, "gla_wide", [P, 4, G, P])
        weight = c.sb(st, "gla_weight", [P, G, H])
        qt = c.sb(st, "gla_qt", [P, KD, G, T])
        at = c.sb(st, "gla_at", [P, KD, G, L])
        state = c.sb(st, "gla_state", [P, 2, G, L])
        read = c.sb(st, "gla_read", [P, 2, G, T])
        o = c.sb(st, "gla_o", [P, G, D])
        ot = c.sb(st, "gla_ot", [P, KD, N])
        six = c.sb(st, "gla_six", [P, G, 9])
        ps = c.banks(st, "gla_ps", 4)
        pp = c.banks(st, "gla_pp", 2)
        po = c.banks(st, "gla_po", 2)
        (w_in, made, z_ready, zt_sum, zt_ready, rows_sum, less_ready, exp_ready, rows_ready, v_sum, v_ready,
         fall_sum, fall_ready, after_sum, after_ready, turned, turned_ready, spread, state_ready, read_ready, repeated,
         o_sum, o_ready, ot_sum, ot_ready, y_sum, done, link_s) = c.sems(
            "w_in made z_ready zt_sum zt_ready rows_sum less_ready exp_ready rows_ready v_sum v_ready "
            "fall_sum fall_ready after_sum after_ready turned turned_ready spread state_ready read_ready repeated "
            "o_sum o_ready ot_sum ot_ready y_sum done link", "gla")
        nu = KD * DH

        with nc.Block() as block:
            @block.sync
            def _(sp):
                for dst, name in ((wqf[:, :, :D], "gla_wq"), (wqf[:, :, D:], "gla_wf"), (wv[:], "gla_wv"),
                                  (wo[:], "gla_wo")):
                    sp.dma_start(dst, a[name]).then_inc(w_in, 16)

            @block.gpsimd
            def _(pool):
                def band(x, base, value, width, ready):
                    pool.affine_select(out=x, in_=x, compare_op=ALU.not_equal, fill=value, base=-base,
                                       pattern=[[-1, width]], channel_multiplier=1).then_inc(made, 1)
                    pool.wait_ge(made, ready)

                pool.memset(own[:], 1.0).then_inc(made, 1)
                pool.memset(falls[:], 0.0).then_inc(made, 1)
                pool.memset(nexts[:], 0.0).then_inc(made, 1)
                pool.wait_ge(made, 3)
                pool.affine_select(out=own[:], in_=own[:], compare_op=ALU.is_ge, fill=0.0, base=0,
                                   pattern=[[-DH, NH2]], channel_multiplier=1).then_inc(made, 1)
                pool.wait_ge(made, 4)
                pool.affine_select(out=own[:], in_=own[:], compare_op=ALU.is_ge, fill=0.0, base=DH - 1,
                                   pattern=[[DH, NH2]], channel_multiplier=-1).then_inc(made, 1)
                band(falls[:], -1, 1.0, L, 6)
                band(falls[:], 0, -1.0, L, 7)
                band(nexts[:], 1, 1.0, T, 8)
                pool.sem_inc(read_ready, 2)
                with pool.Fori(0, NG) as g:
                    for w in range(nu):
                        pool.wait_ge(state_ready, nu * g + w + 1)
                        pool.wait_ge(o_sum, nu * g + w + 1)
                        pool.tensor_tensor(read[:, w % 2], state[:, w % 2, :, 1:], qt[:, w // DH],
                                           ALU.mult).then_inc(read_ready, 1)

            @block.tensor
            def _(pe):
                pe.sem_inc(o_sum, 2)
                pe.sem_inc(spread, 4)
                pe.wait_ge(w_in, 64)
                pe.wait_ge(made, 8)
                with pe.Fori(0, NG) as g:
                    pe.wait_ge(z_ready, g + 1)
                    to_features(pe, c, pp, z).then_inc(zt_sum, 1)
                    pe.wait_ge(zt_ready, g + 1)
                    pe.wait_ge(done, g + 1)
                    for j in range(G):
                        for k in range(KD):
                            last = pe.matmul(ps[:T, j, :], zt[:, k, j * T:(j + 1) * T], wqf[:, k, :],
                                             start=k == 0, stop=k == KD - 1)
                    last.then_inc(rows_sum, 1)
                    token_product(pe, pp, zt, wv).then_inc(v_sum, 1)
                    pe.wait_ge(v_ready, g + 1)
                    for n in range(2):
                        last = pe.matmul(pp[:L, n, :], falls[:T, :], v[:T, 2 * n:2 * n + 2, :].rearrange(
                            "p j d -> p (j d)"), start=True, stop=True)
                    last.then_inc(fall_sum, 1)
                    pe.wait_ge(fall_ready, g + 1)
                    for n in range(2):
                        last = pe.matmul(pp[:T, n, :], nexts[:T, :], v[:T, 2 * n:2 * n + 2, :].rearrange(
                            "p j d -> p (j d)"), start=True, stop=True)
                    last.then_inc(after_sum, 1)
                    pe.wait_ge(rows_ready, g + 1)
                    for n in range(2):
                        for k in range(KD):
                            for j in range(G):
                                last = pe.transpose(ps[:, 2 * n + k, j * T:(j + 1) * T],
                                                    rows[:T, j, n, k * P:(k + 1) * P], c.ident[:T, :T])
                    last.then_inc(turned, 1)
                    pe.wait_ge(turned_ready, g + 1)
                    pe.wait_ge(after_ready, g + 1)

                    def increments(w):
                        if w >= 4:
                            pe.wait_ge(state_ready, nu * g + w - 3)
                        pe.wait_ge(repeated, nu * g + w + 1)
                        for j in range(G):
                            last = pe.transpose(ps[:, w % 4, j * L:(j + 1) * L], wide[:L, w % 4, j, :],
                                                c.ident[:L, :L])
                        last.then_inc(spread, 1)

                    def contract(w):
                        m, e = w // DH, w % DH
                        pe.wait_ge(read_ready, nu * g + w + 3)
                        for j in range(G):
                            out = po[:T, j // 2, j % 2 * D + m * P:j % 2 * D + (m + 1) * P]
                            last = pe.matmul(out.rearrange("p (h d) -> p h d", d=DH)[:, :, e],
                                             read[:, w % 2, j, :], own[:], start=True, stop=True)
                        last.then_inc(o_sum, 1)

                    for w in range(4):
                        increments(w)
                    for w in range(nu):
                        contract(w)
                        if w + 4 < nu:
                            increments(w + 4)
                    pe.wait_ge(o_ready, g + 1)
                    to_features(pe, c, pp, o).then_inc(ot_sum, 1)
                    pe.wait_ge(ot_ready, g + 1)
                    token_product(pe, ps[:, 0:2], ot, wo).then_inc(y_sum, 1)

            @block.scalar
            def _(act):
                with act.Fori(0, NG) as g:
                    act.wait_ge(zt_sum, g + 1)
                    act.activation(zt[:], pp[:, :, :N], ACT.Copy).then_inc(zt_ready, 1)
                    act.wait_ge(v_sum, g + 1)
                    act.activation(v[:T].rearrange("p j d -> p (j d)"),
                                   pp[:T, :, :].rearrange("p n d -> p (n d)"), ACT.Copy).then_inc(v_ready, 1)
                    act.wait_ge(less_ready, g + 1)
                    act.activation(rows[:T].rearrange("p j n d -> p (j n d)"),
                                   rows[:T].rearrange("p j n d -> p (j n d)"), ACT.Exp).then_inc(exp_ready, 1)
                    act.wait_ge(fall_sum, g + 1)
                    act.activation(fall[:L].rearrange("p j d -> p (j d)"),
                                   pp[:L, :, :].rearrange("p n d -> p (n d)"), ACT.Copy).then_inc(fall_ready, 1)
                    act.wait_ge(after_sum, g + 1)
                    act.activation(after[:T].rearrange("p j d -> p (j d)"),
                                   pp[:T, :, :].rearrange("p n d -> p (n d)"), ACT.Copy).then_inc(after_ready, 1)
                    act.wait_ge(turned, g + 1)
                    for k in range(KD):
                        act.activation(qt[:, k], ps[:, k, :N].rearrange("p (j t) -> p j t", j=G), ACT.Copy)
                        last = act.activation(at[:, k, :, 1:], ps[:, 2 + k, :N].rearrange("p (j t) -> p j t", j=G),
                                              ACT.Copy)
                    last.then_inc(turned_ready, 1)
                    for w in range(nu):
                        m, e = w // DH, w % DH
                        act.wait_ge(spread, nu * g + w + 1)
                        column = fall[:L, :, m * P:(m + 1) * P].rearrange("p j (h d) -> p j h d", d=DH)[:, :, :, e:e + 1]
                        act.activation(wide[:L, w % 4].rearrange("p j (h k) -> p j h k", k=DH),
                                       column.to_broadcast([L, G, NH2, DH]), ACT.Copy).then_inc(repeated, 1)
                    act.wait_ge(ot_sum, g + 1)
                    act.activation(ot[:], pp[:, :, :N], ACT.Copy).then_inc(ot_ready, 1)

            @block.vector
            def _(dve):
                dve.memset(at[:, :, :, 0:1], 0.0)
                dve.sem_inc(done, 1)
                with dve.Fori(0, NG) as g:
                    link = Link(dve, link_s, g, 9)
                    normalize(dve, c, z, g).then_inc(z_ready, 1)
                    dve.wait_ge(rows_sum, g + 1)
                    both = ps[:T].rearrange("p j (n d) -> p (j n) d", n=2)
                    rows8 = rows[:T].rearrange("p j n d -> p (j n) d")
                    link.after(dve.tensor_reduce(high[:T, :], both, AX.X, ALU.max))
                    dve.tensor_tensor(rows8, both, high[:T, :].unsqueeze(2).to_broadcast([T, 2 * G, D]),
                                      ALU.subtract).then_inc(less_ready, 1)
                    dve.wait_ge(exp_ready, g + 1)
                    link.after(dve.tensor_reduce(total[:T, :], rows8, AX.X, ALU.add))
                    link.after(dve.reciprocal(total[:T, :], total[:T, :]))
                    for j in range(G):
                        dve.tensor_scalar(rows[:T, j, 0, :], rows[:T, j, 0, :], total[:T, 2 * j:2 * j + 1],
                                          DH ** -0.5, ALU.mult, ALU.mult)
                        last = dve.tensor_scalar(rows[:T, j, 1, :], rows[:T, j, 1, :], total[:T, 2 * j + 1:2 * j + 2],
                                                 None, ALU.mult)
                    last.then_inc(rows_ready, 1)
                    dve.wait_ge(rows_ready, g + 1)
                    link.after(dve.tensor_reduce(weight[:T], rows[:T, :, 0, :].rearrange("p j (h d) -> p j h d", d=DH),
                                                 AX.X, ALU.add))
                    dve.wait_ge(after_ready, g + 1)
                    dve.tensor_tensor(after[:T].rearrange("p j (h d) -> p (j h) d", d=DH),
                                      after[:T].rearrange("p j (h d) -> p (j h) d", d=DH),
                                      weight[:T].rearrange("p j h -> p (j h)").unsqueeze(2)
                                      .to_broadcast([T, G * H, DH]), ALU.mult)
                    dve.wait_ge(turned_ready, g + 1)
                    for w in range(nu):
                        dve.wait_ge(spread, nu * g + w + 5)
                        dve.wait_ge(read_ready, nu * g + w + 1)
                        dve.tensor_tensor_scan(state[:, w % 2].rearrange("p j t -> p (j t)"),
                                               at[:, w // DH].rearrange("p j t -> p (j t)"),
                                               ps[:, w % 4, :G * L], 0.0, ALU.mult, ALU.add).then_inc(state_ready, 1)
                    dve.wait_ge(o_sum, nu * (g + 1) + 2)
                    dve.tensor_tensor(o[:T].rearrange("p j d -> p (j d)"), po[:T].rearrange("p n d -> p (n d)"),
                                      after[:T].rearrange("p j d -> p (j d)"), ALU.add).then_inc(o_ready, 1)
                    dve.wait_ge(y_sum, g + 1)
                    link.after(add_to_residual(dve, c, ps[:, 0:2], g))
                    link.after(tile_stats(dve, c, link, six, g))
                    link.after(dve.memset(six[:, 0, 8:9], 0.0))
                    dve.tensor_copy(six[:, 1, 8:9], six[:, 0, 8:9]).then_inc(done, 1)
                    link.end()


LEVELS = 127.0
TINY = 1e-5


def ternary_network(c, a):
    nc = c.nc
    inverse_deviation(c, 1e-5, "bit")
    NF = FF // P
    with ExitStack() as st:
        w = c.sb(st, "bit_w", [P, 3, KD * FF])
        wt = c.sb(st, "bit_wt", [P, 3, KD * FF], BF16)
        gate, up = (wt[:, n, :].rearrange("p (k f) -> p k f", k=KD) for n in range(2))
        down = wt[:, 2, :].rearrange("p (f d) -> p f d", f=NF)
        mean = c.sb(st, "bit_mean", [P, 3])
        factor = c.sb(st, "bit_factor", [P, 3])
        identh = c.sb(st, "bit_identh", [P, P], BF16)
        z = c.sb(st, "bit_z", [P, G, D])
        xh = c.sb(st, "bit_xh", [P, G, D], BF16)
        xt = c.sb(st, "bit_xt", [P, KD, N], BF16)
        size, grid, back, back2 = (c.sb(st, f"bit_{n}", [P, G]) for n in ("size", "grid", "back", "back2"))
        swish = c.sb(st, "bit_swish", [P, 2, FF])
        inner = c.sb(st, "bit_inner", [P, 2, FF])
        ih = c.sb(st, "bit_ih", [P, 2, FF], BF16)
        it = c.sb(st, "bit_it", [P, 2, NF, T], BF16)
        isize, igrid, iback = (c.sb(st, f"bit_{n}", [P, 2]) for n in ("isize", "igrid", "iback"))
        six = c.sb(st, "bit_six", [P, G, 9])
        pg = c.banks(st, "bit_pg", 4)
        px = st.enter_context(nc.psum_tensor("bit_px", [P, 1, 2 * BANK], BF16))
        pi = st.enter_context(nc.psum_tensor("bit_pi", [P, 1, 2 * BANK], BF16))
        py = c.banks(st, "bit_py", 2)
        (w_in, means, mean_sum, prep_s, ready, x_ready, xt_sum, xt_ready, gate_sum, swish_ready, inner_used,
         i_ready, it_sum, it_ready, y_sum, done, link_s) = c.sems(
            "w_in means mean_sum prep ready x_ready xt_sum xt_ready gate_sum swish_ready inner_used "
            "i_ready it_sum it_ready y_sum done link", "bit")

        with nc.Block() as block:
            @block.sync
            def _(sp):
                for n, name in enumerate(("bit_gate", "bit_up", "bit_down")):
                    sp.dma_start(w[:, n, :], a[name].rearrange("p k f -> p (k f)")).then_inc(w_in, 16)

            @block.tensor
            def _(pe):
                pe.sem_inc(y_sum, 2)
                pe.wait_ge(means, 1)
                pe.matmul(pg[:, 0, :3], c.ones[:], mean[:], start=True, stop=True).then_inc(mean_sum, 1)
                pe.wait_ge(ready, 1)
                with pe.Fori(0, NG) as g:
                    pe.wait_ge(x_ready, g + 1)
                    for k in range(KD):
                        for j in range(G):
                            last = pe.transpose(px[:, 0, k * BANK + j * T:k * BANK + (j + 1) * T],
                                                xh[:T, j, k * P:(k + 1) * P], identh[:T, :T])
                    last.then_inc(xt_sum, 1)
                    pe.wait_ge(xt_ready, g + 1)

                    def open_up(j):
                        if j:
                            pe.wait_ge(inner_used, G * g + j + 1)
                        for n, weight in enumerate((gate, up)):
                            for f in range(2):
                                for k in range(KD):
                                    last = pe.matmul(pg[:T, 2 * n + f, :], xt[:, k, j * T:(j + 1) * T],
                                                     weight[:, k, f * BANK:(f + 1) * BANK],
                                                     start=k == 0, stop=k == KD - 1)
                        last.then_inc(gate_sum, 1)

                    def turn(j):
                        pe.wait_ge(i_ready, G * g + j + 1)
                        pe.wait_ge(it_ready, G * g + j + 1)
                        for f in range(NF):
                            last = pe.transpose(pi[:, 0, f * P:f * P + T], ih[:T, j % 2, f * P:(f + 1) * P],
                                                identh[:T, :T])
                        last.then_inc(it_sum, 1)

                    def close(j):
                        pe.wait_ge(it_ready, G * g + j + 2)
                        pe.wait_ge(done, G * g + j + 1)
                        for f in range(NF):
                            last = pe.matmul(py[:T, j % 2, :D], it[:, j % 2, f, :], down[:, f, :],
                                             start=f == 0, stop=f == NF - 1)
                        last.then_inc(y_sum, 1)

                    open_up(0)
                    for j in range(G):
                        if j + 1 < G:
                            open_up(j + 1)
                        turn(j)
                        close(j)

            @block.scalar
            def _(act):
                act.sem_inc(it_ready, 1)
                act.activation(identh[:], c.ident[:], ACT.Copy).then_inc(ready, 1)
                with act.Fori(0, NG) as g:
                    act.wait_ge(xt_sum, g + 1)
                    act.activation(xt[:], px[:, 0, :].rearrange("p (k n) -> p k n", k=KD)[:, :, :N],
                                   ACT.Copy).then_inc(xt_ready, 1)

                    def swishes(j):
                        act.wait_ge(gate_sum, G * g + j + 1)
                        act.wait_ge(inner_used, G * g + j + 1)
                        act.activation(swish[:T, j % 2, :], pg[:T, 0:2, :].rearrange("p n d -> p (n d)"), ACT.Silu,
                                       scale=back[:T, j:j + 1]).then_inc(swish_ready, 1)

                    for j in range(G):
                        swishes(j)
                        if j:
                            act.wait_ge(it_sum, G * g + j)
                            act.wait_ge(y_sum, G * g + j)
                            act.activation(it[:, (j - 1) % 2], pi[:, 0, :].rearrange("p (f n) -> p f n", n=P)[:, :, :T],
                                           ACT.Copy).then_inc(it_ready, 1)
                    act.wait_ge(it_sum, G * g + G)
                    act.wait_ge(y_sum, G * g + G)
                    act.activation(it[:, (G - 1) % 2], pi[:, 0, :].rearrange("p (f n) -> p f n", n=P)[:, :, :T],
                                   ACT.Copy).then_inc(it_ready, 1)

            @block.vector
            def _(dve):
                prep = Link(dve, prep_s)
                for n in range(3):
                    dve.wait_ge(w_in, 48)
                    last = dve.tensor_reduce(mean[:, n:n + 1], w[:, n, :], AX.X, ALU.add, apply_absolute_value=True)
                last.then_inc(means, 1)
                dve.wait_ge(mean_sum, 1)
                prep.after(dve.tensor_scalar(mean[:], pg[:, 0, :3], 1.0 / (D * FF), TINY, ALU.mult, ALU.max))
                prep.after(dve.reciprocal(factor[:], mean[:]))
                for n in range(3):
                    last = dve.tensor_scalar(w[:, n, :], w[:, n, :], factor[:, n:n + 1], ROUND, ALU.mult, ALU.add)
                prep.after(last)
                flat_w = w[:].rearrange("p n f -> p (n f)")
                prep.after(dve.tensor_scalar(flat_w, flat_w, ROUND, -1.0, ALU.subtract, ALU.max))
                prep.after(dve.tensor_scalar(wt[:].rearrange("p n f -> p (n f)"), flat_w, 1.0, None, ALU.min))
                dve.tensor_scalar(factor[:], mean[:], 1.0 / LEVELS, None, ALU.mult)
                dve.memset(size[:], 0.0)
                dve.wait_ge(ready, 1)
                dve.memset(grid[:], 0.0).then_inc(ready, 1)
                dve.wait_ge(ready, 2)
                dve.sem_inc(done, 2)
                dve.sem_inc(inner_used, 1)
                with dve.Fori(0, NG) as g:
                    link = Link(dve, link_s, g, 6 + G * 9)
                    link.after(normalize(dve, c, z, g))
                    link.after(dve.tensor_reduce(size[:T, :], z[:T], AX.X, ALU.max, apply_absolute_value=True))
                    link.after(dve.tensor_scalar(size[:T, :], size[:T, :], TINY, None, ALU.max))
                    dve.tensor_scalar(back[:T, :], size[:T, :], factor[:T, 0:1], None, ALU.mult)
                    dve.tensor_scalar(back2[:T, :], size[:T, :], factor[:T, 1:2], None, ALU.mult)
                    link.after(dve.reciprocal(grid[:T, :], size[:T, :]))
                    link.after(dve.tensor_scalar(grid[:T, :], grid[:T, :], LEVELS, None, ALU.mult))
                    for j in range(G):
                        last = dve.tensor_scalar(z[:T, j, :], z[:T, j, :], grid[:T, j:j + 1], ROUND, ALU.mult, ALU.add)
                    link.after(last)
                    dve.tensor_scalar(xh[:T].rearrange("p j d -> p (j d)"), z[:T].rearrange("p j d -> p (j d)"),
                                      ROUND, None, ALU.subtract).then_inc(x_ready, 1)
                    for j in range(G):
                        x = inner[:T, j % 2, :]
                        n = j % 2
                        dve.wait_ge(swish_ready, G * g + j + 1)
                        dve.scalar_tensor_tensor(x, pg[:T, 2:4, :].rearrange("p n d -> p (n d)"),
                                                 back2[:T, j:j + 1], swish[:T, j % 2, :], ALU.mult,
                                                 ALU.mult).then_inc(inner_used, 1)
                        dve.wait_ge(inner_used, G * g + j + 2)
                        link.after(dve.tensor_reduce(isize[:T, n:n + 1], x, AX.X, ALU.max, apply_absolute_value=True))
                        link.after(dve.tensor_scalar(isize[:T, n:n + 1], isize[:T, n:n + 1], TINY, None, ALU.max))
                        dve.tensor_scalar(iback[:T, n:n + 1], isize[:T, n:n + 1], factor[:T, 2:3], None, ALU.mult)
                        link.after(dve.reciprocal(igrid[:T, n:n + 1], isize[:T, n:n + 1]))
                        link.after(dve.tensor_scalar(igrid[:T, n:n + 1], igrid[:T, n:n + 1], LEVELS, None, ALU.mult))
                        link.after(dve.tensor_scalar(x, x, igrid[:T, n:n + 1], ROUND, ALU.mult, ALU.add))
                        dve.tensor_scalar(ih[:T, j % 2, :], x, ROUND, None, ALU.subtract).then_inc(i_ready, 1)
                        dve.wait_ge(y_sum, G * g + j + 3)
                        b = G * g + j
                        link.after(dve.scalar_tensor_tensor(c.tile(b), py[:T, j % 2, :D], iback[:T, n:n + 1],
                                                            c.tile(b), ALU.mult, ALU.add))
                        link.after(stats(dve, link, six, [(c.tile(b), flat(c.moments[:T, bass.ds(b, 1), :]))]))
                        dve.memset(six[:, 0, 8:9], 0.0).then_inc(done, 1)
                    link.end()


def matrix(w):
    return w.reshape(-1, P, w.shape[1]).transpose(1, 0, 2)


def matrices(w):
    return w.reshape(w.shape[0], -1, P, w.shape[2]).transpose(0, 2, 1, 3)


def layouts(x):
    image = x["x"].reshape(NG, G, 3, NI // PATCH, PATCH, NI // PATCH, PATCH)
    image = image.transpose(0, 2, 4, 6, 1, 3, 5).reshape(NG, KT, P, G, NPATCH).transpose(0, 2, 1, 3, 4)
    patches = np.zeros((NG, P, KT, G, CLS), image.dtype)
    patches[..., 1:] = image
    t = {"patches": patches, "txt": x["txt"].transpose(1, 0, 2),
         "tok_w": matrix(x["L0_tok_W"].T), "tok_b": x["L0_tok_b"],
         "tok_cls": x["L0_tok_cls_token"][0], "tok_pos": x["L0_tok_pos_embedding"][0]}
    for n in "qkvp":
        t[f"rff_w{n}"] = matrix(x[f"L0_attn_W{n}"].T)
    t["rff_bp"] = x["L0_attn_bp"][None]
    t["rff_br"] = x["L0_attn_br"].T
    t["rff_wr"] = x["L0_attn_Wr"].transpose(1, 0, 2)
    t["top1_wg"] = matrix(x["L0_ffn_gate_w"].T)
    t["top1_gate_b"], t["top1_expert_bias"] = x["L0_ffn_gate_b"], x["L0_ffn_expert_bias"]
    t["top1_b1"] = x["L0_ffn_b1"].reshape(E, FF // P, P).transpose(0, 2, 1)
    t["top1_b2"] = x["L0_ffn_b2"]
    t["top1_w1"] = matrices(x["L0_ffn_w1"])
    t["top1_w2"] = matrices(x["L0_ffn_w2"])
    for n in "qkvo":
        t[f"tern_w{n}"] = matrix(x[f"L1_attn_w_{n}"].T)
        t[f"tern_s{n}"] = np.reshape(x[f"L1_attn_s_{n}"], (1,))
        t[f"tern_b{n}"] = x[f"L1_attn_b_{n}"]
    t["tern_bq"], t["tern_bk"] = (x[f"L1_attn_b_{n}"].reshape(KD, P).T for n in "qk")
    t["gqa_wq"], t["gqa_wo"] = (matrix(x[f"L1_ffn_w{n}"].T) for n in "qo")
    t["gqa_wk"] = matrix(np.repeat(x["L1_ffn_wk"].reshape(4, DH, D), H // 4, axis=0).reshape(D, D).T)
    t["gqa_wv"] = matrix(x["L1_ffn_wv"].T)
    t["gqa_norm"] = x["L1_ffn_attn_norm_w"].reshape(KD, P).T
    t["top2_norm"] = x["L1_ffn_ffn_norm_w"].reshape(KD, P).T
    t["top2_wg"] = matrix(x["L1_ffn_gate_w"].T)
    t["top2_w"] = x["L1_ffn_expert_w"].transpose(2, 0, 1).reshape(KD, P, E * D).transpose(1, 0, 2)
    for n in "qkvo":
        t[f"diff_w{n}"] = matrix(x[f"L3_attn_W{n}"].T)
    for n in ("q1", "k1", "q2", "k2"):
        t[f"diff_lambda_{n}"] = x[f"L3_attn_lambda_{n}"]
    t["diff_subln"] = x["L3_attn_subln_w"]
    t["xmoe_wg"] = matrix(x["L3_ffn_gate_w"].T)
    t["xmoe_w1"] = matrices(x["L3_ffn_w1"].transpose(0, 2, 1))
    t["xmoe_w2"] = matrices(x["L3_ffn_w2"].transpose(0, 2, 1))
    for n, m in zip("qfvo", "qfio"):
        t[f"gla_w{n}"] = matrix(x[f"L2_attn_W{m}"])
    for n in ("gate", "up", "down"):
        t[f"bit_{n}"] = matrix(x[f"L2_ffn_w_{n}"].T)
    return {n: np.ascontiguousarray(v) for n, v in t.items()}


def build_program(nc, a, out):
    with ExitStack() as stack:
        c = Core(nc, stack)
        constants(c)
        for phase in (tokens, random_feature_attention, top1_experts, scaled_attention, grouped_block,
                      gated_linear_attention, ternary_network, differential_attention, capacity_experts):
            phase(c, a)
            c.end_of_phase()
        store(c, out)


def kernel(**inputs):
    import concourse.bacc as bacc
    from concourse.bass_utils import run_bass_kernel_spmd

    arrays = {f"in_{n}": v for n, v in layouts({n: np.asarray(v) for n, v in inputs.items()}).items()}
    nc = bacc.Bacc("TRN2", target_bir_lowering=False, num_devices=1)
    a = {n[3:]: nc.dram_tensor(n, v.shape, mybir.dt.from_np(v.dtype), kind="ExternalInput").ap()
         for n, v in arrays.items()}
    out = nc.dram_tensor("out", (B, T, D), F32, kind="ExternalOutput").ap()
    build_program(nc, a, out)
    result = run_bass_kernel_spmd(nc, [arrays], core_ids=[0])
    return result.results[0]["out"]
```

```python
import math
from contextlib import ExitStack

import numpy as np

import concourse.bass as bass
from concourse import mybir

F32 = mybir.dt.float32
BF16 = mybir.dt.bfloat16
I32 = mybir.dt.int32
ALU = mybir.AluOpType
ACT = mybir.ActivationFunctionType
AX = mybir.AxisListType

P = 128
NI = 96
PATCH = 16
NPATCH = (NI // PATCH) ** 2
CLS = 1 + NPATCH
NTXT = 77
T = CLS + NTXT
B = 32
D = 256
KD = D // P
G = 4
NG = B // G
N = G * T
H = 16
DH = D // H
E = 8
FF = 1024
KT = 3 * PATCH * PATCH // P
BANK = 512
ROUND = 1.5 * 2.0 ** 23


def flat(ap):
    return ap.rearrange("p a b -> p (a b)")


class Link:

    def __init__(self, eng, sem, i=0, per=0):
        self.eng, self.sem, self.base, self.per, self.n = eng, sem, i * per, per, 0

    def after(self, ins):
        ins.then_inc(self.sem, 1)
        self.n += 1
        self.eng.wait_ge(self.sem, self.base + self.n)

    def end(self):
        assert self.per in (0, self.n), (self.per, self.n)


class Core:

    def __init__(self, nc, stack):
        self.nc, self.in_use = nc, []
        self.resid = self.sb(stack, "resid", [P, B, D])
        self.moments = self.sb(stack, "moments", [P, B, 2])
        self.rstd = self.sb(stack, "rstd", [P, B])
        self.ident = self.sb(stack, "ident", [P, P])
        self.ones = self.sb(stack, "ones", [P, P])

    def sb(self, stack, name, shape, dt=F32):
        return stack.enter_context(self.nc.sbuf_tensor(name, shape, dt))

    def banks(self, stack, name, n, dt=F32):
        return stack.enter_context(self.nc.psum_tensor(name, [P, n, BANK], dt))

    def sems(self, names, phase):
        made = [self.nc.alloc_semaphore(f"{phase}_{n}") for n in names.split()]
        self.in_use += made
        return made

    def end_of_phase(self):
        self.nc.clear_and_free_semaphores(self.in_use)
        self.in_use = []
        self.nc.all_engine_barrier()

    def tile(self, b):
        return flat(self.resid[:T, bass.ds(b, 1), :])

    def mean(self, b):
        return flat(self.moments[:T, bass.ds(b, 1), 0:1])

    def scale(self, b):
        return self.rstd[:T, bass.ds(b, 1)]


def row(ap, parts):
    return bass.AP(ap.tensor, ap.offset, [[0, parts]] + [list(x) for x in ap.ap])


def stats(eng, link, six, tiles):
    eng.memset(six[0:1, 0, 8:9], 0.0)
    for n, (src, _) in enumerate(tiles):
        last = eng.bn_stats(six[:T, n, 0:6], src)
    link.after(last)
    eng.memset(six[0:1, 0, 8:9], 0.0)
    for n in range(len(tiles)):
        last = eng.bn_aggr(six[:T, n, 6:8], six[:T, n, 0:6])
    link.after(last)
    eng.memset(six[0:1, 0, 8:9], 0.0)
    for n, (_, dst) in enumerate(tiles):
        last = eng.tensor_copy(dst, six[:T, n, 6:8])
    return last


def constants(c):
    (zero, made) = c.sems("zero made", "const")
    with c.nc.Block() as block:
        @block.vector
        def _(dve):
            dve.memset(c.ones[:], 1.0)

        @block.gpsimd
        def _(pool):
            pool.memset(c.ident[:], 0.0).then_inc(zero, 1)
            pool.wait_ge(zero, 1)
            pool.affine_select(out=c.ident[:], in_=c.ident[:], compare_op=ALU.not_equal, fill=1.0,
                               base=0, pattern=[[-1, P]], channel_multiplier=1).then_inc(made, 1)
            pool.wait_ge(made, 1)


def inverse_deviation(c, eps, ph):
    added, rooted, inverted = c.sems("added rooted inverted", ph + "_rstd")
    with c.nc.Block() as block:
        @block.vector
        def _(dve):
            dve.tensor_scalar(c.rstd[:T, :], c.moments[:T, :, 1], eps, None, ALU.add).then_inc(added, 1)
            dve.wait_ge(rooted, 1)
            dve.reciprocal(c.rstd[:T, :], c.rstd[:T, :]).then_inc(inverted, 1)
            dve.wait_ge(inverted, 1)

        @block.scalar
        def _(act):
            act.wait_ge(added, 1)
            act.activation(c.rstd[:T, :], c.rstd[:T, :], ACT.Sqrt).then_inc(rooted, 1)


def tokens(c, a):
    nc = c.nc
    with ExitStack() as st:
        patches = c.sb(st, "patches", [P, 2, KT, G, CLS])
        weight = c.sb(st, "tok_w", [P, KT, D])
        base = c.sb(st, "tok_base", [P, D])
        first = c.sb(st, "tok_first", [P, D])
        six = c.sb(st, "tok_six", [P, G, 9])
        acc = c.banks(st, "tok_acc", 4)
        (text_in, fixed_in, cls_in, patch_in0, patch_in1, summed, based, acc_free, link_s) = c.sems(
            "text_in fixed_in cls_in patch_in0 patch_in1 summed based acc_free link", "tok")
        patch_in = (patch_in0, patch_in1)
        with nc.Block() as block:
            @block.sync
            def _(sp):
                sp.dma_start(weight[:], a["tok_w"]).then_inc(fixed_in, 16)
                sp.dma_start(base[:CLS, :], a["tok_pos"]).then_inc(fixed_in, 16)
                sp.dma_start(first[:CLS, :], row(a["tok_b"], CLS)).then_inc(fixed_in, 16)
                sp.wait_ge(fixed_in, 48)
                sp.dma_start(first[0:1, :], a["tok_cls"]).then_inc(cls_in, 16)
                with sp.Fori(0, NG // 2) as i:
                    for u in range(2):
                        sp.wait_ge(summed, 2 * i + u + 1)
                        sp.dma_start(patches[:, u], a["patches"][bass.ds(2 * i + u, 1)].rearrange(
                            "a p k g c -> p (a k) g c")).then_inc(patch_in[u], 16)

            @block.scalar
            def _(act):
                act.dma_start(c.resid[CLS:T, :, :], a["txt"]).then_inc(text_in, 16)

            @block.tensor
            def _(pe):
                pe.sem_inc(summed, 2)
                pe.wait_ge(cls_in, 16)
                with pe.Fori(0, NG // 2) as i:
                    for u in range(2):
                        pe.wait_ge(patch_in[u], 16 * (i + 1))
                        pe.wait_ge(acc_free, 2 * i + u + 1)
                        for j in range(G):
                            for k in range(KT):
                                last = pe.matmul(acc[:CLS, 2 * u + j // 2, j % 2 * D:(j % 2 + 1) * D],
                                                 patches[:, u, k, j, :], weight[:, k, :],
                                                 start=k == 0, stop=k == KT - 1)
                        last.then_inc(summed, 1)

            @block.vector
            def _(dve):
                dve.sem_inc(acc_free, 2)
                dve.wait_ge(cls_in, 16)
                dve.tensor_tensor(base[:CLS, :], base[:CLS, :], first[:CLS, :], ALU.add).then_inc(based, 1)
                dve.wait_ge(based, 1)
                dve.wait_ge(text_in, 16)
                with dve.Fori(0, NG // 2) as i:
                    link = Link(dve, link_s, i, 6)
                    for u in range(2):
                        dve.wait_ge(summed, 2 * i + u + 3)
                        for j in range(G):
                            last = dve.tensor_tensor(
                                flat(c.resid[:CLS, bass.ds(8 * i + 4 * u + j, 1), :]),
                                acc[:CLS, 2 * u + j // 2, j % 2 * D:(j % 2 + 1) * D], base[:CLS, :], ALU.add)
                        link.after(last)
                        last = stats(dve, link, six, [
                            (c.tile(8 * i + 4 * u + j), flat(c.moments[:T, bass.ds(8 * i + 4 * u + j, 1), :]))
                            for j in range(G)])
                        last.then_inc(acc_free, 1)
                        dve.wait_ge(acc_free, 2 * i + u + 3)
                    link.end()


def store(c, out):
    (stored,) = c.sems("stored", "out")
    with c.nc.Block() as block:
        @block.sync
        def _(sp):
            sp.dma_start(out.rearrange("b t d -> t b d"), c.resid[:T, :, :]).then_inc(stored, 16)
            sp.wait_ge(stored, 16)



def normalize(dve, c, z, g, scale=None):
    for j in range(G):
        b = G * g + j
        last = dve.tensor_scalar(z[:T, j, :], c.tile(b), c.mean(b),
                                 c.scale(b) if scale is None else scale[:T, bass.ds(b, 1)],
                                 ALU.subtract, ALU.mult)
    return last


def to_features(pe, c, out, x):
    for k in range(KD):
        for j in range(G):
            last = pe.transpose(out[:, k, j * T:(j + 1) * T], x[:T, j, k * P:(k + 1) * P], c.ident[:T, :T])
    return last


def feature_product(pe, out, weight, xt):
    for m in range(KD):
        for k in range(KD):
            last = pe.matmul(out[:, m, :N], weight[:, k, m * P:(m + 1) * P], xt[:, k, :],
                             start=k == 0, stop=k == KD - 1)
    return last


def token_product(pe, out, xt, weight, bias=None, ones=None):
    for j in range(G):
        dst = out[:T, j // 2, j % 2 * D:(j % 2 + 1) * D]
        for k in range(KD):
            last = pe.matmul(dst, xt[:, k, j * T:(j + 1) * T], weight[:, k, :],
                             start=k == 0, stop=k == KD - 1 and bias is None)
        if bias is not None:
            last = pe.matmul(dst, ones[0:1, :T], bias[0:1, :], start=False, stop=True)
    return last


def add_to_residual(dve, c, y, g):
    for j in range(G):
        b = G * g + j
        last = dve.tensor_tensor(c.tile(b), y[:T, j // 2, j % 2 * D:(j % 2 + 1) * D], c.tile(b), ALU.add)
    return last


def tile_stats(dve, c, link, six, g):
    return stats(dve, link, six, [(c.tile(G * g + j), flat(c.moments[:T, bass.ds(G * g + j, 1), :]))
                                  for j in range(G)])


NEXT = ("z0", "z1", "q0", "q1", "k0", "k1", "v0", "v1")
LAST = ("o0", "o1", "y0", "y1")
ORDER = ("z0", "z1", "q0", "q1", "k0", "k1", "o0", "o1", "v0", "v1", "y0", "y1")


def steps(part):
    return [x for x in ORDER if not (part == "first" and x in LAST or part == "last" and x in NEXT)]


def first_step(g, part):
    return len(NEXT) if part == "first" else len(ORDER) * g + 4


BEFORE_LAST = first_step(NG - 1, "last") + len(LAST)

RFF = 128
TAU_1 = 6.28125
TAU_2 = float(np.float32(round((2 * math.pi - TAU_1) * 2.0 ** 22) / 2.0 ** 22))
TAU_3 = 2 * math.pi - TAU_1 - TAU_2
TAU_IN = 2 * math.pi * (1 - 2.0 ** -22)


def random_feature_attention(c, a):
    nc = c.nc
    inverse_deviation(c, 1e-5, "rff")
    with ExitStack() as st:
        wq, wk, wv, wp = (c.sb(st, f"rff_w{n}", [P, KD, D]) for n in "qkvp")
        wr = c.sb(st, "rff_wr", [P, H, RFF])
        br = c.sb(st, "rff_br", [P, H])
        brs = c.sb(st, "rff_brs", [P, H])
        turns = c.sb(st, "rff_turns", [P, H])
        bp = c.sb(st, "rff_bp", [1, D])
        quarter = c.sb(st, "rff_quarter", [P, 1])
        z = c.sb(st, "rff_z", [P, G, D])
        zt = c.sb(st, "rff_zt", [P, KD, N])
        qt = c.sb(st, "rff_qt", [P, 2, KD, N])
        kt = c.sb(st, "rff_kt", [P, 2, KD, N])
        v1 = c.sb(st, "rff_v1", [P, 2, G, H, DH + 1])
        rounded = c.sb(st, "rff_rounded", [P, 2, 2, N])
        less = c.sb(st, "rff_less", [P, 2, 2, N])
        size = c.sb(st, "rff_size", [P, 2, 2, N])
        sines = c.sb(st, "rff_sines", [P, 2, 2, N])
        cosines = c.sb(st, "rff_cosines", [P, 2, 2, N])
        pair = c.sb(st, "rff_pair", [P, 2, N])
        mixed = c.sb(st, "rff_mixed", [P, H, G, DH + 1])
        inverse = c.sb(st, "rff_inverse", [P, H, G])
        o = c.sb(st, "rff_o", [P, 2, G, D])
        ot = c.sb(st, "rff_ot", [P, KD, N])
        six = c.sb(st, "rff_six", [P, G, 9])
        pg = c.banks(st, "rff_pg", 1)
        px = c.banks(st, "rff_px", 1)
        pp = c.banks(st, "rff_pp", 4)
        pa = c.banks(st, "rff_pa", 2)
        (w_in, wr_in, cleared, fixed, prep_s, z_ready, step_sum, step_done, angle_sum, less_ready,
         size_ready, waves_ready, pair_sum, pair_ready, mix_sum, mix_ready, o_ready, link_first, link_pairs,
         link_last) = c.sems(
            "w_in wr_in cleared fixed prep z_ready step_sum step_done angle_sum less_ready "
            "size_ready waves_ready pair_sum pair_ready mix_sum mix_ready o_ready link_first link_pairs "
            "link_last", "rff")

        def carried(part, h):
            if h < len(ORDER) and ORDER[h] in steps(part):
                return [(ORDER[h], steps(part).index(ORDER[h]))]
            return []

        with nc.Block() as block:
            @block.sync
            def _(sp):
                for w, name in ((wq, "rff_wq"), (wk, "rff_wk"), (wv, "rff_wv"), (wp, "rff_wp"),
                                (br, "rff_br"), (bp, "rff_bp")):
                    sp.dma_start(w[:], a[name]).then_inc(w_in, 16)
                sp.wait_ge(cleared, 1)
                for s in range(P // DH):
                    sp.dma_start(wr[DH * s:DH * (s + 1), s:H:P // DH, :], a["rff_wr"][:, s:H:P // DH, :])\
                      .then_inc(wr_in, 16)

            @block.tensor
            def _(pe):
                pe.sem_inc(pair_sum, 2)
                pe.sem_inc(mix_sum, 2)
                pe.wait_ge(w_in, 96)
                pe.wait_ge(fixed, 1)

                def step(x, g, q, count):
                    if not (isinstance(count, int) and count == 0):
                        pe.wait_ge(step_done, count)
                    k = int(x[1])
                    if x == "z0":
                        pe.wait_ge(z_ready, g + 1)
                    if x == "o0":
                        pe.wait_ge(o_ready, g + 1)
                    if x[0] in "zo":
                        src = z if x[0] == "z" else o[:, q]
                        for j in range(G):
                            last = pe.transpose(px[:, 0, j * T:(j + 1) * T], src[:T, j, k * P:(k + 1) * P],
                                                c.ident[:T, :T])
                    elif x[0] in "qk":
                        w = wq if x[0] == "q" else wk
                        for m in range(KD):
                            last = pe.matmul(px[:, 0, :N], w[:, m, k * P:(k + 1) * P], zt[:, m, :],
                                             start=m == 0, stop=m == KD - 1)
                    else:
                        src, w = (zt, wv) if x[0] == "v" else (ot, wp)
                        for j in (2 * k, 2 * k + 1):
                            dst = px[:T, 0, j % 2 * D:(j % 2 + 1) * D]
                            for m in range(KD):
                                last = pe.matmul(dst, src[:, m, j * T:(j + 1) * T], w[:, m, :],
                                                 start=m == 0, stop=m == KD - 1 and x[0] == "v")
                            if x[0] == "y":
                                last = pe.matmul(dst, c.ones[0:1, :T], bp[0:1, :], start=False, stop=True)
                    last.then_inc(step_sum, 1)

                def angles(g, parity, h):
                    r = H * g + h
                    if not (isinstance(g, int) and r < 2):
                        pe.wait_ge(less_ready, r - 1)
                    for s, src in enumerate((qt, kt)):
                        last = pe.matmul(pp[:, 2 * (h % 2) + s, :N], wr[:, h, :], src[:, parity, h // 8, :],
                                         start=True, stop=True)
                    last.then_inc(angle_sum, 1)

                def pairs(r, h):
                    pe.wait_ge(waves_ready, r + 3)
                    pe.wait_ge(pair_ready, r + 1)
                    for j in range(G):
                        t = slice(j * T, (j + 1) * T)
                        for n, waves in enumerate((cosines, sines)):
                            last = pe.matmul(pa[:T, h % 2, t], waves[:, h % 2, 1, t], waves[:, h % 2, 0, t],
                                             start=n == 0, stop=n == 1)
                    last.then_inc(pair_sum, 1)

                def mix(g, parity, h):
                    pe.wait_ge(pair_ready, H * g + h + 3)
                    if h % 4 == 0:
                        pe.wait_ge(mix_ready, 4 * g + h // 4 + 1)
                    for j in range(G):
                        at = (DH + 1) * (G * (h % 4) + j)
                        last = pe.matmul(pg[:T, 0, at:at + DH + 1], pair[:T, h % 2, j * T:(j + 1) * T],
                                         v1[:T, parity, j, h, :], start=True, stop=True)
                    last.then_inc(mix_sum, 1)

                def group(g, q, part):
                    pe.wait_ge(step_done, first_step(g, part))
                    for h in range(H):
                        if h + 2 < H:
                            angles(g, q, h + 2)
                        elif part != "last":
                            angles(g + 1, 1 - q, h + 2 - H)
                        pairs(H * g + h, h)
                        if h >= 1:
                            mix(g, q, h - 1)
                        elif part != "first":
                            mix(g - 1, 1 - q, H - 1)
                        for x, count in carried(part, h):
                            step(x, g - 1 if x in LAST else g + 1, 1 - q, first_step(g, part) + count)

                for count, x in enumerate(NEXT):
                    step(x, 0, 0, count)
                    if x == "k1":
                        pe.wait_ge(step_done, count + 1)
                        angles(0, 0, 0)
                        angles(0, 0, 1)
                group(0, 0, "first")
                with pe.Fori(0, NG // 2 - 1) as i:
                    for u in range(2):
                        group(2 * i + 1 + u, (1 + u) % 2, "pairs")
                group(NG - 1, 1, "last")
                mix(NG - 1, 1, H - 1)
                for count, x in enumerate(LAST):
                    step(x, NG - 1, 1, BEFORE_LAST + count)

            @block.scalar
            def _(act):
                act.sem_inc(waves_ready, 2)
                act.wait_ge(fixed, 1)

                def read(x, q, count):
                    if x[0] not in "zqko":
                        return
                    k = int(x[1])
                    act.wait_ge(step_sum, count + 1)
                    dst = {"z": zt, "q": qt[:, q], "k": kt[:, q], "o": ot}[x[0]]
                    act.activation(dst[:, k, :], px[:, 0, :N], ACT.Copy).then_inc(step_done, 1)

                def group(g, q, part):
                    for h in range(H):
                        r = H * g + h
                        act.wait_ge(less_ready, r + 1)
                        act.activation(size[:, h % 2], less[:, h % 2], ACT.Abs, bias=br[:, h:h + 1],
                                       scale=-1.0).then_inc(size_ready, 1)
                        act.wait_ge(pair_sum, r + 1)
                        act.activation(sines[:, h % 2], less[:, h % 2], ACT.Sin, bias=brs[:, h:h + 1],
                                       scale=-TAU_IN)
                        act.wait_ge(size_ready, r + 1)
                        act.activation(cosines[:, h % 2], size[:, h % 2], ACT.Sin, bias=quarter[:, 0:1],
                                       scale=-TAU_IN).then_inc(waves_ready, 1)
                        if h:
                            for x, count in carried(part, h - 1):
                                read(x, 1 - q, first_step(g, part) + count)

                for count, x in enumerate(NEXT):
                    read(x, 0, count)
                group(0, 0, "first")
                with act.Fori(0, NG // 2 - 1) as i:
                    for u in range(2):
                        group(2 * i + 1 + u, (1 + u) % 2, "pairs")
                group(NG - 1, 1, "last")
                for count, x in enumerate(LAST):
                    read(x, 1, BEFORE_LAST + count)

            @block.vector
            def _(dve):
                dve.memset(wr[:], 0.0).then_inc(cleared, 1)
                dve.memset(v1[:, :, :, :, DH:DH + 1], 1.0)
                dve.memset(quarter[:], math.pi / 2)
                prep = Link(dve, prep_s)
                dve.wait_ge(w_in, 96)
                prep.after(dve.tensor_scalar(turns[:], br[:], 1 / (2 * math.pi), ROUND, ALU.mult, ALU.add))
                prep.after(dve.tensor_scalar(turns[:], turns[:], ROUND, None, ALU.subtract))
                for part in (TAU_1, TAU_2, TAU_3):
                    prep.after(dve.scalar_tensor_tensor(br[:], turns[:], -part, br[:], ALU.mult, ALU.add))
                prep.after(dve.tensor_scalar(br[:], br[:], 1 / (2 * math.pi), None, ALU.mult))
                dve.tensor_scalar(brs[:], br[:], TAU_IN, None, ALU.mult)
                dve.wait_ge(wr_in, 16 * (P // DH))
                dve.tensor_scalar(wr[:], wr[:], 1 / (2 * math.pi), None, ALU.mult).then_inc(fixed, 1)
                dve.sem_inc(pair_ready, 2)
                dve.sem_inc(mix_ready, 1)

                def read(link, x, g, parity, count):
                    if x[0] not in "vy":
                        return
                    k = int(x[1])
                    pair_of = (2 * k, 2 * k + 1)
                    dve.wait_ge(step_sum, count + 1)
                    if x[0] == "v":
                        dve.tensor_copy(v1[:T, parity, 2 * k:2 * k + 2, :, 0:DH],
                                        px[:T, 0, :].rearrange("p (j h d) -> p j h d", j=2, h=H))\
                           .then_inc(step_done, 1)
                        return
                    for j in pair_of:
                        last = dve.tensor_tensor(c.tile(G * g + j), px[:T, 0, j % 2 * D:(j % 2 + 1) * D],
                                                 c.tile(G * g + j), ALU.add)
                    last.then_inc(step_done, 1)
                    dve.wait_ge(step_done, count + 1)
                    if k == 1:
                        link.after(tile_stats(dve, c, link, six, g))

                def keep_pair(r, h):
                    dve.wait_ge(pair_sum, r + 3)
                    dve.wait_ge(mix_sum, r + 1)
                    dve.tensor_copy(pair[:T, h % 2, :], pa[:T, h % 2, :N]).then_inc(pair_ready, 1)

                def keep_mix(g, q):
                    dve.wait_ge(mix_sum, H * g + 4 * q + 3 + 3)
                    dve.tensor_copy(mixed[:T, 4 * q:4 * q + 4].rearrange("p h j d -> p (h j d)"),
                                    pg[:T, 0, :4 * G * (DH + 1)]).then_inc(mix_ready, 1)

                def divide(link, g, parity):
                    dve.wait_ge(mix_ready, 4 * g + 5)
                    link.after(dve.tensor_scalar(inverse[:T], mixed[:T, :, :, DH], 1e-6 * RFF, None, ALU.add))
                    link.after(dve.reciprocal(inverse[:T], inverse[:T]))
                    dve.tensor_tensor(o[:T, parity].rearrange("p j (h d) -> p h j d", h=H), mixed[:T, :, :, 0:DH],
                                      inverse[:T].unsqueeze(3).to_broadcast([T, H, G, DH]), ALU.mult)\
                       .then_inc(o_ready, 1)

                def group(link, g, q, part):
                    if part != "last":
                        normalize(dve, c, z, g + 1).then_inc(z_ready, 1)
                    for h in range(H):
                        r = H * g + h
                        angle = pp[:, 2 * (h % 2):2 * (h % 2) + 2, :N]
                        dve.wait_ge(angle_sum, r + 1)
                        dve.wait_ge(waves_ready, r + 1)
                        link.after(dve.tensor_scalar(rounded[:, h % 2], angle, br[:, h:h + 1], ROUND,
                                                     ALU.add, ALU.add))
                        dve.scalar_tensor_tensor(less[:, h % 2], rounded[:, h % 2], ROUND, angle,
                                                 ALU.subtract, ALU.subtract).then_inc(less_ready, 1)
                        if h >= 1:
                            keep_pair(r - 1, h - 1)
                            if h % 4 == 1 and h >= 5:
                                keep_mix(g, h // 4 - 1)
                            for x, count in carried(part, h - 1):
                                read(link, x, g - 1 if x in LAST else g + 1, 1 - q, first_step(g, part) + count)
                        elif part != "first":
                            keep_pair(r - 1, H - 1)
                        if h == 1 and part != "first":
                            keep_mix(g - 1, H // 4 - 1)
                            divide(link, g - 1, 1 - q)

                normalize(dve, c, z, 0).then_inc(z_ready, 1)
                link = Link(dve, link_first)
                for count, x in enumerate(NEXT):
                    read(link, x, 0, 0, count)
                group(link, 0, 0, "first")
                with dve.Fori(0, NG // 2 - 1) as i:
                    link = Link(dve, link_pairs, i, 2 * (H + 2 + 3))
                    for u in range(2):
                        group(link, 2 * i + 1 + u, (1 + u) % 2, "pairs")
                    link.end()
                link = Link(dve, link_last)
                group(link, NG - 1, 1, "last")
                keep_pair(H * NG - 1, H - 1)
                keep_mix(NG - 1, H // 4 - 1)
                divide(link, NG - 1, 1)
                for count, x in enumerate(LAST):
                    read(link, x, NG - 1, 1, BEFORE_LAST + count)


class Routing:

    def __init__(self, c, st, ph, rows=False):
        self.ph, self.rows = ph, rows
        if rows:
            self.z = c.sb(st, ph + "_zr", [P, B, D])
        else:
            self.zt = c.sb(st, ph + "_zta", [P, KD, B * T])
        self.share = c.sb(st, ph + "_share", [P, B, E])


def gather_tokens(c, r, z_of, w_gate, gate_biases, w_norm, a):
    nc = c.nc
    with ExitStack() as st:
        wg = c.sb(st, r.ph + "_wg", [P, KD, E])
        extra = c.sb(st, r.ph + "_extra", [P, 2, E])
        norm = c.sb(st, r.ph + "_norm", [P, KD])
        z = c.sb(st, r.ph + "_z", [P, 2, G, D])
        zt = c.sb(st, r.ph + "_zt", [P, 2, KD, N])
        pt = c.banks(st, r.ph + "_pt", 4)
        pl = c.banks(st, r.ph + "_pl", 2)
        (w_in, z_ready, zt_sum, zt_ready, copied, logits_sum, logits_ready, link_s) = c.sems(
            "w_in z_ready zt_sum zt_ready copied logits_sum logits_ready link", r.ph + "_gather")
        names = [w_gate] + list(gate_biases) + ([w_norm] if w_norm else [])

        with nc.Block() as block:
            @block.sync
            def _(sp):
                sp.dma_start(wg[:], a[w_gate]).then_inc(w_in, 16)
                for n, name in enumerate(gate_biases):
                    sp.dma_start(extra[:T, n, :], row(a[name], T)).then_inc(w_in, 16)
                if w_norm:
                    sp.dma_start(norm[:], a[w_norm]).then_inc(w_in, 16)

            @block.tensor
            def _(pe):
                pe.sem_inc(zt_sum, 2)
                pe.sem_inc(logits_sum, 2)
                pe.wait_ge(w_in, 16 * len(names))
                with pe.Fori(0, NG // 2) as i:
                    for u in range(2):
                        n = 2 * i + u
                        pe.wait_ge(z_ready, n + 1)
                        pe.wait_ge(zt_ready, n + 1)
                        to_features(pe, c, pt[:, 2 * u:2 * u + 2], z[:, u]).then_inc(zt_sum, 1)
                        pe.wait_ge(zt_ready, n + 3)
                        pe.wait_ge(logits_ready, n + 1)
                        for j in range(G):
                            for k in range(KD):
                                last = pe.matmul(pl[:T, u, j * E:(j + 1) * E], zt[:, u, k, j * T:(j + 1) * T],
                                                 wg[:, k, :], start=k == 0, stop=k == KD - 1)
                        last.then_inc(logits_sum, 1)

            @block.scalar
            def _(act):
                act.sem_inc(zt_ready, 2)
                act.wait_ge(w_in, 16 * len(names))
                with act.Fori(0, NG // 2) as i:
                    for u in range(2):
                        n = 2 * i + u
                        act.wait_ge(zt_sum, n + 3)
                        act.wait_ge(logits_sum, n + 1)
                        if not r.rows:
                            act.wait_ge(copied, n + 1)
                        for k in range(KD):
                            last = act.activation(zt[:, u, k, :], pt[:, 2 * u + k, :N], ACT.Copy,
                                                  scale=norm[:, k:k + 1] if w_norm else 1.0)
                        last.then_inc(zt_ready, 1)

            @block.gpsimd
            def _(pool):
                pool.sem_inc(copied, 2)
                with pool.Fori(0, NG // 2) as i:
                    for u in range(2):
                        n = 2 * i + u
                        if r.rows:
                            pool.wait_ge(z_ready, n + 1)
                            pool.tensor_copy(r.z[:T, bass.ds(G * n, G), :], z[:T, u]).then_inc(copied, 1)
                        else:
                            pool.wait_ge(zt_ready, n + 3)
                            pool.tensor_copy(r.zt[:, :, bass.ds(N * n, N)], zt[:, u]).then_inc(copied, 1)

            @block.vector
            def _(dve):
                dve.sem_inc(logits_ready, 2)
                dve.wait_ge(w_in, 16 * len(names))
                link = Link(dve, link_s)

                def logits(n, u):
                    dve.wait_ge(logits_sum, n + 3)
                    dst = r.share[:T, bass.ds(G * n, G), :]
                    src = pl[:T, u, :G * E].rearrange("p (j e) -> p j e", j=G)
                    bias = [extra[:T, m:m + 1, :].to_broadcast([T, G, E]) for m in range(len(gate_biases))]
                    if bias:
                        dve.tensor_tensor(dst, src, bias[0], ALU.add).then_inc(logits_ready, 1)
                        dve.wait_ge(logits_ready, n + 3)
                        for m in bias[1:]:
                            dve.tensor_tensor(dst, dst, m, ALU.add)
                    else:
                        dve.tensor_scalar(dst, src, 0.0, None, ALU.add).then_inc(logits_ready, 1)

                with dve.Fori(0, NG // 2) as i:
                    for u in range(2):
                        dve.wait_ge(zt_sum, 2 * i + u + 1)
                        if r.rows:
                            dve.wait_ge(copied, 2 * i + u + 1)
                        z_of(dve, z[:, u], 2 * i + u).then_inc(z_ready, 1)
                    for u in range(2):
                        logits(2 * i + u, u)


def ranks(dve, link, r, above, tie, before, rank):
    mine = r.share[:T].unsqueeze(3).to_broadcast([T, B, E, E])
    other = r.share[:T].unsqueeze(2).to_broadcast([T, B, E, E])
    dve.tensor_tensor(above[:T], other, mine, ALU.is_gt)
    link.after(dve.tensor_tensor(tie[:T], other, mine, ALU.is_equal))
    link.after(dve.tensor_tensor(tie[:T], tie[:T],
                                 before[:T].unsqueeze(1).to_broadcast([T, B, E, E]), ALU.mult))
    link.after(dve.tensor_tensor(above[:T], above[:T], tie[:T], ALU.add))
    link.after(dve.tensor_reduce(rank[:T], above[:T], AX.X, ALU.add))


def lower_index(pool, made, before):
    pool.memset(before[:], 1.0).then_inc(made, 1)
    pool.wait_ge(made, 1)
    pool.affine_select(out=before[:], in_=before[:], compare_op=ALU.is_gt, fill=0.0, base=0,
                       pattern=[[1, E], [-1, E]], channel_multiplier=0).then_inc(made, 1)


S = 256
NS = S // P
NB = (B * T + E * (S - 1)) // S
SMALLEST = 0.5 - 0.5 / S


class Dispatch:

    def __init__(self, c, st, ph):
        self.slot = c.sb(st, ph + "_slot", [P, B], I32)
        self.expert = c.sb(st, ph + "_expert", [1, NB], I32)
        self.x = c.nc.dram_tensor(ph + "_xd", (NB * S, D), F32, kind="Internal").ap()
        self.y = c.nc.dram_tensor(ph + "_yd", (NB * S, D), F32, kind="Internal").ap()


def route_first(c, r, d):
    with ExitStack() as st:
        above, tie = (c.sb(st, f"first_{n}", [P, B, E, E]) for n in ("above", "tie"))
        rank, chosen, place = (c.sb(st, f"first_{n}", [P, B, E]) for n in ("rank", "chosen", "place"))
        runs, totals, places = (c.sb(st, f"first_{n}", [P, E, B]) for n in ("runs", "totals", "places"))
        before = c.sb(st, "first_before", [P, E, E])
        earlier = c.sb(st, "first_earlier", [P, P])
        blocks, start, end, total = (c.sb(st, f"first_{n}", [P, E]) for n in ("blocks", "start", "end", "total"))
        number = c.sb(st, "first_number", [1, NB], I32)
        block_of = c.sb(st, "first_block_of", [1, NB])
        passed = c.sb(st, "first_passed", [1, NB, E])
        slot = c.sb(st, "first_slot", [P, B])
        zero = c.sb(st, "first_zero", [P, D])
        pc = c.banks(st, "first_pc", 2)
        (made, link_s, shared, prefixed, zero_made, cleared, slotted, sent) = c.sems(
            "made link shared prefixed zero_made cleared slotted sent", "first")
        with c.nc.Block() as block:
            @block.sync
            def _(sp):
                sp.wait_ge(zero_made, 1)
                sp.dma_start(d.x.rearrange("(p a) f -> p a f", p=P),
                             zero[:].unsqueeze(1).to_broadcast([P, NB * NS, D])).then_inc(cleared, 16)

            @block.gpsimd
            def _(pool):
                pool.memset(zero[:], 0.0).then_inc(zero_made, 1)
                lower_index(pool, made, before)
                pool.memset(earlier[:], 1.0).then_inc(made, 1)
                pool.wait_ge(made, 3)
                pool.affine_select(out=earlier[:], in_=earlier[:], compare_op=ALU.is_gt, fill=0.0, base=0,
                                   pattern=[[1, P]], channel_multiplier=-1).then_inc(made, 1)
                pool.iota(number[:], [[1, NB]], base=0, channel_multiplier=0).then_inc(made, 1)
                pool.wait_ge(cleared, 16)
                pool.wait_ge(slotted, 1)
                for b in range(B):
                    pool.indirect_dma_start(d.x, bass.IndirectOffsetOnAxis(ap=d.slot[:T, b:b + 1], axis=0),
                                            r.z[:T, b, :], None).then_inc(sent, 16)
                pool.wait_ge(sent, 16 * B)

            @block.tensor
            def _(pe):
                pe.wait_ge(made, 4)
                pe.wait_ge(shared, 1)
                marks = chosen[:T].rearrange("p b e -> p (b e)")
                pe.matmul(pc[:T, 0, :B * E], earlier[:T, :T], marks, start=True, stop=True)
                pe.matmul(pc[:T, 1, :B * E], c.ones[:T, :T], marks, start=True, stop=True).then_inc(prefixed, 1)

            @block.vector
            def _(dve):
                link = Link(dve, link_s)
                dve.wait_ge(made, 5)
                dve.memset(runs[:], 1.0)
                link.after(dve.tensor_copy(block_of[:], number[:]))
                ranks(dve, link, r, above, tie, before, rank)
                dve.memset(runs[:, :, 0:1], 0.0)
                dve.tensor_scalar(chosen[:T], rank[:T], 0.0, None, ALU.is_equal).then_inc(shared, 1)
                dve.wait_ge(prefixed, 1)
                link.after(dve.tensor_copy(totals[:T], pc[:T, 1, :B * E].rearrange("p (b e) -> p e b", e=E)))
                link.after(dve.tensor_tensor_scan(places[:T].rearrange("p e b -> p (e b)"),
                                                  runs[:T].rearrange("p e b -> p (e b)"),
                                                  totals[:T].rearrange("p e b -> p (e b)"), 0.0, ALU.mult, ALU.add))
                link.after(dve.tensor_copy(total[:T, :], places[:T, :, B - 1]))
                link.after(dve.tensor_tensor(places[:T], places[:T], totals[:T], ALU.subtract))
                link.after(dve.tensor_scalar(blocks[:T, :], total[:T, :], 1.0 / S, SMALLEST, ALU.mult, ALU.add))
                link.after(dve.tensor_scalar(blocks[:T, :], blocks[:T, :], ROUND, None, ALU.add))
                link.after(dve.tensor_scalar(blocks[:T, :], blocks[:T, :], ROUND, None, ALU.subtract))
                link.after(dve.tensor_tensor(above[:T, 0], before[:T],
                                             blocks[:T, :].unsqueeze(1).to_broadcast([T, E, E]), ALU.mult))
                link.after(dve.tensor_reduce(start[:T, :], above[:T, 0], AX.X, ALU.add))
                dve.tensor_tensor(end[:T, :], start[:T, :], blocks[:T, :], ALU.add)
                link.after(dve.tensor_tensor(place[:T], places[:T].rearrange("p e b -> p b e"),
                                             pc[:T, 0, :B * E].rearrange("p (b e) -> p b e", e=E), ALU.add))
                link.after(dve.tensor_scalar(start[:T, :], start[:T, :], float(S), None, ALU.mult))
                link.after(dve.tensor_tensor(place[:T], place[:T],
                                             start[:T, :].unsqueeze(1).to_broadcast([T, B, E]), ALU.add))
                link.after(dve.tensor_tensor(place[:T], place[:T], chosen[:T], ALU.mult))
                link.after(dve.tensor_reduce(slot[:T, :], place[:T], AX.X, ALU.add))
                dve.tensor_copy(d.slot[:T, :], slot[:T, :]).then_inc(slotted, 1)
                link.after(dve.tensor_tensor(passed[:], block_of[:].unsqueeze(2).to_broadcast([1, NB, E]),
                                             end[0:1, :].unsqueeze(1).to_broadcast([1, NB, E]), ALU.is_ge))
                link.after(dve.tensor_reduce(block_of[:], passed[:], AX.X, ALU.add))
                link.after(dve.tensor_scalar(block_of[:], block_of[:], float(E - 1), None, ALU.min))
                dve.tensor_copy(d.expert[:], block_of[:])


def expert_blocks(c, d, a):
    nf = FF // P
    with ExitStack() as st:
        x = c.sb(st, "blocks_x", [P, 2, NS, D])
        xt = c.sb(st, "blocks_xt", [P, 2, KD, S])
        w1 = c.sb(st, "blocks_w1", [P, 2, KD, FF])
        w2 = c.sb(st, "blocks_w2", [P, 2, nf, D])
        b1 = c.sb(st, "blocks_b1", [P, 2, nf])
        b2 = c.sb(st, "blocks_b2", [P, 2, D])
        inner = c.sb(st, "blocks_inner", [P, 2, nf, S])
        y = c.sb(st, "blocks_y", [P, 2, NS, D])
        pt = c.banks(st, "blocks_pt", 2)
        ph = c.banks(st, "blocks_ph", 4)
        py = c.banks(st, "blocks_py", 2)
        (x_in0, x_in1, w_in0, w_in1, turned, xt_ready, inner_sum, inner_ready, y_sum, y_ready, y_out0,
         y_out1, stored) = c.sems("x_in0 x_in1 w_in0 w_in1 turned xt_ready inner_sum inner_ready y_sum "
                                  "y_ready y_out0 y_out1 stored", "top1_blocks")
        x_in, w_in, y_out = (x_in0, x_in1), (w_in0, w_in1), (y_out0, y_out1)
        x_blocks, y_blocks = (t.rearrange("(k s p) f -> k p s f", s=NS, p=P) for t in (d.x, d.y))

        with c.nc.Block() as block:
            @block.sync
            def _(sp):
                with sp.Fori(0, NB // 2) as i:
                    for u in range(2):
                        k = 2 * i + u
                        sp.wait_ge(turned, k + 1)
                        sp.dma_start(x[:, u], x_blocks[bass.ds(k, 1)].rearrange(
                            "a p s f -> p (a s) f")).then_inc(x_in[u], 16)
                        e = sp.value_load(d.expert[0:1, bass.ds(k, 1)], min_val=0, max_val=E - 1)
                        sp.wait_ge(y_ready, k + 1)
                        sp.dma_start(w1[:, u], a["top1_w1"][bass.ds(e, 1)].rearrange(
                            "a p k f -> p (a k) f")).then_inc(w_in[u], 16)
                        sp.dma_start(b1[:, u], a["top1_b1"][bass.ds(e, 1)].rearrange(
                            "a p f -> p (a f)")).then_inc(w_in[u], 16)
                        sp.dma_start(w2[:, u], a["top1_w2"][bass.ds(e, 1)].rearrange(
                            "a p k f -> p (a k) f")).then_inc(w_in[u], 16)
                        sp.dma_start(b2[:, u], a["top1_b2"][bass.ds(e, 1)].to_broadcast([P, D])).then_inc(
                            w_in[u], 16)

            @block.tensor
            def _(pe):
                pe.sem_inc(turned, 2)

                def turn(k, u, i):
                    pe.wait_ge(x_in[u], 16 * (i + 1))
                    pe.wait_ge(xt_ready, k + 1)
                    for m in range(KD):
                        for s in range(NS):
                            last = pe.transpose(pt[:, u, m * S + s * P:m * S + (s + 1) * P],
                                                x[:, u, s, m * P:(m + 1) * P], c.ident[:])
                    last.then_inc(turned, 1)

                with pe.Fori(0, NB // 2) as i:
                    for u in range(2):
                        k = 2 * i + u
                        turn(k, u, i)
                        pe.wait_ge(xt_ready, k + 3)
                        pe.wait_ge(w_in[u], 64 * (i + 1))
                        for f in range(nf):
                            if f % 2 == 0:
                                pe.wait_ge(inner_ready, nf // 2 * k + f // 2 + 1)
                            for m in range(KD):
                                last = pe.matmul(ph[:, f // 2, f % 2 * S:(f % 2 + 1) * S],
                                                 w1[:, u, m, f * P:(f + 1) * P], xt[:, u, m, :],
                                                 start=m == 0, stop=m == KD - 1)
                            if f % 2 == 1:
                                last.then_inc(inner_sum, 1)
                        pe.wait_ge(y_ready, k + 1)
                        for s in range(NS):
                            for f in range(nf):
                                if s == 0 and f % 2 == 0:
                                    pe.wait_ge(inner_ready, nf // 2 * k + f // 2 + 5)
                                last = pe.matmul(py[:, u, s * D:(s + 1) * D],
                                                 inner[:, u, f, s * P:(s + 1) * P], w2[:, u, f, :],
                                                 start=f == 0, stop=f == nf - 1)
                        last.then_inc(y_sum, 1)

            @block.scalar
            def _(act):
                act.sem_inc(inner_ready, 4)
                with act.Fori(0, NB // 2) as i:
                    for u in range(2):
                        k = 2 * i + u
                        act.wait_ge(w_in[u], 64 * (i + 1))
                        act.wait_ge(y_ready, k + 1)
                        for f in range(0, nf, 2):
                            act.wait_ge(inner_sum, nf // 2 * k + f // 2 + 1)
                            act.activation(inner[:, u, f, :], ph[:, f // 2, :S], ACT.Relu, bias=b1[:, u, f:f + 1])
                            act.activation(inner[:, u, f + 1, :], ph[:, f // 2, S:], ACT.Relu,
                                           bias=b1[:, u, f + 1:f + 2]).then_inc(inner_ready, 1)

            @block.vector
            def _(dve):
                dve.sem_inc(xt_ready, 2)
                dve.sem_inc(y_ready, 2)
                with dve.Fori(0, NB // 2) as i:
                    for u in range(2):
                        k = 2 * i + u
                        dve.wait_ge(turned, k + 3)
                        dve.tensor_scalar(xt[:, u].rearrange("p m t -> p (m t)"), pt[:, u, :], 0.0, None,
                                          ALU.add).then_inc(xt_ready, 1)
                        dve.wait_ge(y_sum, k + 1)
                        dve.wait_ge(stored, k + 1)
                        for s in range(NS):
                            last = dve.tensor_tensor(y[:, u, s, :], py[:, u, s * D:(s + 1) * D], b2[:, u], ALU.add)
                        last.then_inc(y_ready, 1)

            @block.gpsimd
            def _(pool):
                pool.sem_inc(stored, 2)
                with pool.Fori(0, NB // 2) as i:
                    for u in range(2):
                        k = 2 * i + u
                        pool.wait_ge(y_ready, k + 3)
                        pool.dma_start(y_blocks[bass.ds(k, 1)].rearrange("a p s f -> p (a s) f"),
                                       y[:, u]).then_inc(y_out[u], 16)
                        pool.wait_ge(y_out[u], 16 * (i + 1))
                        pool.sem_inc(stored, 1)


def collect_rows(c, d, ph):
    with ExitStack() as st:
        y = c.sb(st, ph + "_row", [P, 2, G, D])
        six = c.sb(st, ph + "_rsix", [P, G, 9])
        fetched0, fetched1, link_s, done = c.sems("fetched0 fetched1 link done", ph + "_collect")
        fetched = (fetched0, fetched1)
        with c.nc.Block() as block:
            @block.gpsimd
            def _(pool):
                for g in range(NG):
                    if g >= 2:
                        pool.wait_ge(done, g - 1)
                    for j in range(G):
                        pool.indirect_dma_start(y[:T, g % 2, j, :], None, d.y, bass.IndirectOffsetOnAxis(
                            ap=d.slot[:T, G * g + j:G * g + j + 1], axis=0)).then_inc(fetched[g % 2], 16)

            @block.vector
            def _(dve):
                link = Link(dve, link_s)
                for g in range(NG):
                    if g >= 1:
                        dve.wait_ge(done, g)
                    dve.wait_ge(fetched[g % 2], 16 * G * (g // 2 + 1))
                    tiles = c.resid[:T, G * g:G * (g + 1), :]
                    link.after(dve.tensor_tensor(tiles, y[:T, g % 2], tiles, ALU.add))
                    stats(dve, link, six, [(c.resid[:T, G * g + j, :], c.moments[:T, G * g + j, :])
                                           for j in range(G)]).then_inc(done, 1)


def experts(c, r, a, names, nf, func, bias):
    nc = c.nc
    w1n, w2n = names
    flat_share = r.share[:T].rearrange("p b e -> p (b e)")
    with ExitStack() as st:
        w1 = c.sb(st, r.ph + "_w1", [P, 2, KD, nf * P])
        w2 = c.sb(st, r.ph + "_w2", [P, 2, nf, D])
        b1 = c.sb(st, r.ph + "_b1", [P, 2, nf])
        loads = 3 if bias else 2
        inner = c.sb(st, r.ph + "_inner", [P, 2, nf, N])
        ph = c.banks(st, r.ph + "_ph", 4)
        py = c.banks(st, r.ph + "_py", 4)
        (w_in0, w_in1, inner_sum, inner_ready, y_sum, added) = c.sems(
            "w_in0 w_in1 inner_sum inner_ready y_sum added", r.ph + "_experts")
        w_in = (w_in0, w_in1)

        with nc.Block() as block:
            @block.sync
            def _(sp):
                with sp.Fori(0, E // 2) as i:
                    for v in range(2):
                        sp.wait_ge(y_sum, NG * (2 * i + v + 1))
                        sp.dma_start(w1[:, v], a[w1n][bass.ds(2 * i + v, 1)].rearrange(
                            "a p k f -> p (a k) f")).then_inc(w_in[v], 16)
                        if bias:
                            sp.dma_start(b1[:, v], a[bias][bass.ds(2 * i + v, 1)].rearrange(
                                "a p f -> p (a f)")).then_inc(w_in[v], 16)
                        sp.dma_start(w2[:, v], a[w2n][bass.ds(2 * i + v, 1)].rearrange(
                            "a p k f -> p (a k) f")).then_inc(w_in[v], 16)

            @block.tensor
            def _(pe):
                pe.sem_inc(y_sum, 2 * NG)
                with pe.Fori(0, E // 2) as i:
                    for v in range(2):
                        with pe.Fori(0, NG // 2) as q:
                            for u in range(2):
                                n = NG * (2 * i + v) + 2 * q + u
                                if u == 0:
                                    pe.wait_ge(w_in[v], 16 * loads * (i + 1))
                                for f in range(nf):
                                    bank = (nf * u + f) % 4
                                    pe.wait_ge(inner_ready, nf * n + f + 1)
                                    for k in range(KD):
                                        last = pe.matmul(ph[:, bank, :N], w1[:, v, k, f * P:(f + 1) * P],
                                                         r.zt[:, k, bass.ds(N * (2 * q + u), N)],
                                                         start=k == 0, stop=k == KD - 1)
                                    last.then_inc(inner_sum, 1)
                                pe.wait_ge(added, n + 1)
                                for j in range(G):
                                    for f in range(nf):
                                        if j == 0:
                                            pe.wait_ge(inner_ready, nf * n + f + 5)
                                        last = pe.matmul(py[:T, 2 * u + j // 2, j % 2 * D:(j % 2 + 1) * D],
                                                         inner[:, u, f, j * T:(j + 1) * T], w2[:, v, f, :],
                                                         start=f == 0, stop=f == nf - 1)
                                last.then_inc(y_sum, 1)

            @block.scalar
            def _(act):
                act.sem_inc(inner_ready, 4)
                with act.Fori(0, E // 2) as i:
                    for v in range(2):
                        with act.Fori(0, NG // 2) as q:
                            for u in range(2):
                                n = NG * (2 * i + v) + 2 * q + u
                                if bias and u == 0:
                                    act.wait_ge(w_in[v], 16 * loads * (i + 1))
                                act.wait_ge(y_sum, 2 * NG + n - 1)
                                for f in range(nf):
                                    act.wait_ge(inner_sum, nf * n + f + 1)
                                    act.activation(inner[:, u, f, :], ph[:, (nf * u + f) % 4, :N], func,
                                                   bias=b1[:, v, f:f + 1] if bias else 0.0).then_inc(inner_ready, 1)

            @block.vector
            def _(dve):
                dve.sem_inc(added, 2)
                with dve.Fori(0, E // 2) as i:
                    for v in range(2):
                        with dve.Fori(0, NG // 2) as q:
                            for u in range(2):
                                n = NG * (2 * i + v) + 2 * q + u
                                dve.wait_ge(y_sum, 2 * NG + n + 1)
                                dve.wait_ge(added, n + 2)
                                for j in range(G):
                                    b = G * (2 * q + u) + j
                                    last = dve.scalar_tensor_tensor(
                                        c.tile(b), py[:T, 2 * u + j // 2, j % 2 * D:(j % 2 + 1) * D],
                                        flat_share[:, bass.ds(E * b + 2 * i + v, 1)], c.tile(b),
                                        ALU.mult, ALU.add)
                                last.then_inc(added, 1)


def all_stats(c, ph):
    with ExitStack() as st:
        six = c.sb(st, ph + "_six", [P, G, 9])
        link_s, done = c.sems("link done", ph + "_stats")
        with c.nc.Block() as block:
            @block.vector
            def _(dve):
                dve.sem_inc(done, 1)
                with dve.Fori(0, NG) as g:
                    link = Link(dve, link_s, g, 2)
                    dve.wait_ge(done, g + 1)
                    tile_stats(dve, c, link, six, g).then_inc(done, 1)
                    link.end()


def top1_experts(c, a):
    inverse_deviation(c, 1e-5, "top1")
    with ExitStack() as st:
        d = Dispatch(c, st, "top1")
        with ExitStack() as st2:
            r = Routing(c, st2, "top1", rows=True)
            gather_tokens(c, r, lambda dve, z, g: normalize(dve, c, z, g), "top1_wg",
                          ("top1_gate_b", "top1_expert_bias"), None, a)
            route_first(c, r, d)
        expert_blocks(c, d, a)
        collect_rows(c, d, "top1")


class Attention:

    def __init__(self, ph, dm=DH, kv=H, scale=DH ** -0.5, causal=False, affine=False, norm=None,
                 differential=False, keep=None):
        self.ph, self.dm, self.kv, self.scale, self.causal = ph, dm, kv, scale, causal
        self.affine, self.norm, self.differential, self.keep = affine, norm, differential, keep


NX = 16
LAMBDA_INIT = 0.8 - 0.6 * math.exp(-0.3 * 12)
LARGEST = float(np.finfo(np.float32).max)


def softmax_attention(c, a, s):
    nc = c.nc
    ph, dm = s.ph, s.dm
    maps = D // dm
    nr = G * maps // NX
    nh = P // dm
    share = maps // H
    with ExitStack() as st:
        wq, wk, wo = (c.sb(st, f"{ph}_w{n}", [P, KD, D]) for n in "qko")
        wv = c.sb(st, ph + "_wv", [P, KD, s.kv * DH])
        fore = c.sb(st, ph + "_fore", [P, 2, KD])
        factors = c.sb(st, ph + "_factors", [P, 4])
        vbias = c.sb(st, ph + "_vbias", [P, D])
        obias = c.sb(st, ph + "_obias", [P, D])
        norm = c.sb(st, ph + "_norm", [P, KD])
        lam = c.sb(st, ph + "_lam", [P, 4, 8])
        lams = c.sb(st, ph + "_lams", [P, 2])
        neglam = c.sb(st, ph + "_neglam", [P, 1])
        subln = c.sb(st, ph + "_subln", [P, DH])
        own = c.sb(st, ph + "_own", [P, nh])
        future = c.sb(st, ph + "_future", [P, 4, T], BF16)
        identh = c.sb(st, ph + "_identh", [P, P], BF16)
        scale2 = c.sb(st, ph + "_scale2", [P, B])
        z = c.sb(st, ph + "_z", [P, G, D])
        temp = c.sb(st, ph + "_temp", [P, G, D])
        zt = c.sb(st, ph + "_zt", [P, KD, N])
        qt = c.sb(st, ph + "_qt", [P, 2, KD, N])
        kt = c.sb(st, ph + "_kt", [P, 2, KD, N])
        km = c.sb(st, ph + "_km", [P, 2, NX, T])
        v1 = c.sb(st, ph + "_v1", [P, 2, G, s.kv, DH + 1])
        most = c.sb(st, ph + "_most", [P, 2, NX])
        p = c.sb(st, ph + "_p", [P, 2, NX, T])
        pt = c.sb(st, ph + "_pt", [P, 2, NX, T])
        inverse = c.sb(st, ph + "_inverse", [P, NX])
        two = c.sb(st, ph + "_two", [P, NX, DH])
        o = c.sb(st, ph + "_o", [P, 2, G, D])
        squares = c.sb(st, ph + "_squares", [P, G, D])
        roots = c.sb(st, ph + "_roots", [P, G * H])
        ot = c.sb(st, ph + "_ot", [P, KD, N])
        six = c.sb(st, ph + "_six", [P, G, 9])
        ps = c.banks(st, ph + "_ps", 4)
        pp = c.banks(st, ph + "_pp", 2)
        px = c.banks(st, ph + "_px", 1)
        po = c.banks(st, ph + "_po", 1)
        (w_in, own_made, prep_s, lam_sum, lam_exp, z_ready, step_sum, step_done, masked, score_sum,
         less_ready, exp_ready, turned, kept, mix_sum, mix_ready, square_ready, root_ready, o_ready,
         link_first, link_pairs, link_last) = c.sems(
            "w_in own_made prep lam_sum lam_exp z_ready step_sum step_done masked score_sum "
            "less_ready exp_ready turned kept mix_sum mix_ready square_ready root_ready o_ready "
            "link_first link_pairs link_last", ph)
        loads = [(wq[:], a[ph + "_wq"]), (wk[:], a[ph + "_wk"]), (wv[:], a[ph + "_wv"]), (wo[:], a[ph + "_wo"])]
        if s.affine:
            loads += [(fore[:, 0, :], a[ph + "_bq"]), (fore[:, 1, :], a[ph + "_bk"]),
                      (vbias[:T, :], row(a[ph + "_bv"], T)), (obias[:T, :], row(a[ph + "_bo"], T))]
            loads += [(factors[:, n:n + 1], row(a[f"{ph}_s{x}"], P)) for n, x in enumerate("qkvo")]
        if s.norm:
            loads += [(norm[:], a[s.norm])]
        if s.differential:
            loads += [(lam[:T, n, :], row(a[f"{ph}_lambda_{x}"], T)) for n, x in enumerate(("q1", "k1", "q2", "k2"))]
            loads += [(subln[:T, :], row(a[ph + "_subln"], T))]

        per_slot = 3 if nr == 4 else 2

        def carried(part, n, slot):
            at = per_slot * n + slot
            if slot < per_slot and at < len(ORDER) and ORDER[at] in steps(part):
                return [(ORDER[at], steps(part).index(ORDER[at]))]
            return []

        def half(x):
            return x // nh

        def at(n):
            return n * NX // maps, n % (maps // NX)

        with nc.Block() as block:
            @block.sync
            def _(sp):
                for dst, src in loads:
                    sp.dma_start(dst, src).then_inc(w_in, 16)

            @block.gpsimd
            def _(pool):
                pool.memset(own[:], 1.0).then_inc(own_made, 1)
                pool.memset(future[:], 0.0).then_inc(own_made, 1)
                pool.tensor_copy(identh[:], c.ident[:]).then_inc(own_made, 1)
                pool.wait_ge(own_made, 3)
                pool.affine_select(out=own[:], in_=own[:], compare_op=ALU.is_ge, fill=0.0, base=0,
                                   pattern=[[-dm, nh]], channel_multiplier=1).then_inc(own_made, 1)
                pool.affine_select(out=future[:], in_=future[:], compare_op=ALU.is_ge, fill=-1e30, base=0,
                                   pattern=[[0, 4], [-1, T]], channel_multiplier=1).then_inc(own_made, 1)
                pool.wait_ge(own_made, 5)
                pool.affine_select(out=own[:], in_=own[:], compare_op=ALU.is_ge, fill=0.0, base=dm - 1,
                                   pattern=[[dm, nh]], channel_multiplier=-1).then_inc(own_made, 1)
                pool.wait_ge(own_made, 6)

                def mask(g, q, n, ready):
                    j, m0 = at(n)
                    if n == 0:
                        pool.wait_ge(step_done, ready)
                    pool.wait_ge(score_sum, nr * g + n + 1)
                    for x in range(0, NX, nh):
                        src = kt[:, q, m0 + x // nh, j * T:(j + 1) * T]
                        last = pool.tensor_tensor(
                            km[:, n % 2, x:x + nh, :], src.unsqueeze(1).to_broadcast([P, nh, T]),
                            own[:].unsqueeze(2).to_broadcast([P, nh, T]), ALU.mult)
                    last.then_inc(masked, 1)

                def group(g, q, part):
                    for n in range(1, nr):
                        mask(g, q, n, None)
                    if part != "last":
                        mask(g + 1, 1 - q, 0, first_step(g, part) + 6)

                mask(0, 0, 0, 6)
                group(0, 0, "first")
                with pool.Fori(0, NG // 2 - 1) as i:
                    for u in range(2):
                        group(2 * i + 1 + u, (1 + u) % 2, "pairs")
                group(NG - 1, 1, "last")

            @block.tensor
            def _(pe):
                pe.sem_inc(score_sum, 2)
                pe.sem_inc(mix_sum, 2)
                pe.wait_ge(w_in, 16 * len(loads))
                pe.wait_ge(own_made, 6)

                def step(x, g, q, count):
                    if not (isinstance(count, int) and count == 0):
                        pe.wait_ge(step_done, count)
                    k = int(x[1])
                    bank = px[:, 0, :N]
                    if x[0] == "z":
                        if k == 0:
                            pe.wait_ge(z_ready, g + 1)
                        for j in range(G):
                            last = pe.transpose(px[:, 0, j * T:(j + 1) * T], z[:T, j, k * P:(k + 1) * P],
                                                c.ident[:T, :T])
                    elif x[0] in "qk":
                        w = wq if x[0] == "q" else wk
                        for m in range(KD):
                            last = pe.matmul(bank, w[:, m, k * P:(k + 1) * P], zt[:, m, :],
                                             start=m == 0, stop=m == KD - 1)
                    elif x[0] == "o":
                        if k == 0 and s.differential:
                            pe.wait_ge(o_ready, g + 1)
                        elif k == 0:
                            pe.wait_ge(mix_ready, nr * (g + 1) + 1)
                        for j in range(G):
                            last = pe.transpose(px[:, 0, j * T:(j + 1) * T], o[:T, q, j, k * P:(k + 1) * P],
                                                c.ident[:T, :T])
                    else:
                        src, w, width = (zt, wv, s.kv * DH) if x[0] == "v" else (ot, wo, D)
                        for j in (2 * k, 2 * k + 1):
                            for m in range(KD):
                                last = pe.matmul(px[:T, 0, j % 2 * D:j % 2 * D + width],
                                                 src[:, m, j * T:(j + 1) * T], w[:, m, :],
                                                 start=m == 0, stop=m == KD - 1)
                    last.then_inc(step_sum, 1)

                def scores(g, q, n):
                    j, m0 = at(n)
                    pe.wait_ge(masked, nr * g + n + 1)
                    if not (isinstance(g, int) and nr * g + n == 0):
                        pe.wait_ge(less_ready, nr * g + n)
                    for x in range(0, NX, 4):
                        if s.causal:
                            pe.matmul(ps[:T, x // 4, :N], identh[:T, :T],
                                      future[:T].rearrange("p x t -> p (x t)"), start=True, stop=False)
                        last = pe.matmul(ps[:T, x // 4, :N], qt[:, q, m0 + half(x), j * T:(j + 1) * T],
                                         km[:, n % 2, x:x + 4, :].rearrange("p x t -> p (x t)"),
                                         start=not s.causal, stop=True)
                    last.then_inc(score_sum, 1)

                def turn(g, n, q):
                    r = nr * g + n
                    if q == 0:
                        pe.wait_ge(exp_ready, r + 1)
                    pe.wait_ge(kept, 4 * r + q + 1)
                    for x in range(4):
                        last = pe.transpose(pp[:T, q % 2, x * T:(x + 1) * T], p[:T, n % 2, 4 * q + x, :],
                                            c.ident[:T, :T])
                    last.then_inc(turned, 1)

                def mix(g, parity, n, q):
                    j, m0 = at(n)
                    r = nr * g + n
                    pe.wait_ge(kept, 4 * r + q + 3)
                    if q == 0:
                        pe.wait_ge(mix_ready, r + 1)
                    for x in range(4 * q, 4 * q + 4):
                        head = (m0 * NX + x) // share // (H // s.kv)
                        last = pe.matmul(po[:T, 0, x * (DH + 1):(x + 1) * (DH + 1)], pt[:T, n % 2, x, :],
                                         v1[:T, parity, j, head, :], start=True, stop=True)
                    if q == 3:
                        last.then_inc(mix_sum, 1)

                def group(g, q, part):
                    def carry(n, slot):
                        for x, count in carried(part, n, slot):
                            late = x in LAST
                            step(x, g - 1 if late else g + 1, 1 - q, first_step(g, part) + count)

                    pe.wait_ge(step_done, first_step(g, part))
                    for n in range(nr):
                        if n + 1 < nr:
                            scores(g, q, n + 1)
                        elif part != "last":
                            scores(g + 1, 1 - q, 0)
                        carry(n, 0)
                        turn(g, n, 0)
                        turn(g, n, 1)
                        mix(g, q, n, 0)
                        carry(n, 1)
                        turn(g, n, 2)
                        mix(g, q, n, 1)
                        turn(g, n, 3)
                        mix(g, q, n, 2)
                        carry(n, 2)
                        mix(g, q, n, 3)

                for count, x in enumerate(NEXT):
                    step(x, 0, 0, count)
                scores(0, 0, 0)
                group(0, 0, "first")
                with pe.Fori(0, NG // 2 - 1) as i:
                    for u in range(2):
                        group(2 * i + 1 + u, (1 + u) % 2, "pairs")
                group(NG - 1, 1, "last")
                for count, x in enumerate(LAST):
                    step(x, NG - 1, 1, BEFORE_LAST + count)

            @block.scalar
            def _(act):
                act.sem_inc(kept, 2)
                act.wait_ge(w_in, 16 * len(loads))
                if s.differential:
                    act.wait_ge(lam_sum, 1)
                    act.activation(lams[:T, :], lams[:T, :], ACT.Exp).then_inc(lam_exp, 1)
                if s.keep is not None:
                    act.wait_ge(lam_sum, 1)
                    act.activation(scale2[:T, :], scale2[:T, :], ACT.Sqrt).then_inc(lam_exp, 1)

                def read(x, q, count):
                    if x[0] not in "zqko":
                        return
                    k = int(x[1])
                    bank = px[:, 0, :N]
                    act.wait_ge(step_sum, count + 1)
                    if x[0] == "z":
                        last = act.activation(zt[:, k, :], bank, ACT.Copy, scale=norm[:, k:k + 1] if s.norm else 1.0)
                    elif x[0] == "o":
                        last = act.activation(ot[:, k, :], bank, ACT.Copy)
                    else:
                        n, dst = (0, qt) if x[0] == "q" else (1, kt)
                        if s.affine:
                            last = act.activation(dst[:, q, k, :], bank, ACT.Identity,
                                                  bias=fore[:, n, k:k + 1], scale=factors[:, n:n + 1])
                        else:
                            last = act.activation(dst[:, q, k, :], bank, ACT.Copy)
                    last.then_inc(step_done, 1)

                def root(g):
                    act.wait_ge(square_ready, g + 1)
                    act.activation(roots[:T, :], roots[:T, :], ACT.Sqrt).then_inc(root_ready, 1)

                def group(g, q, part):
                    def carry(n, slot):
                        for x, count in carried(part, n, slot):
                            read(x, 1 - q, first_step(g, part) + count)

                    for n in range(nr):
                        r = nr * g + n
                        act.wait_ge(less_ready, r + 1)
                        act.activation(p[:T, n % 2], p[:T, n % 2], ACT.Exp, scale=s.scale).then_inc(exp_ready, 1)
                        act.wait_ge(mix_sum, r + 1)
                        carry(n, 0)
                        for q4 in range(4):
                            if q4 == 2:
                                carry(n, 1)
                            act.wait_ge(turned, 4 * r + q4 + 1)
                            act.activation(pt[:T, n % 2, 4 * q4:4 * q4 + 4, :].rearrange("p x t -> p (x t)"),
                                           pp[:T, q4 % 2, :N], ACT.Copy).then_inc(kept, 1)
                        carry(n, 2)
                        if s.differential and part != "first" and n == 0:
                            root(g - 1)

                for count, x in enumerate(NEXT):
                    read(x, 0, count)
                group(0, 0, "first")
                with act.Fori(0, NG // 2 - 1) as i:
                    for u in range(2):
                        group(2 * i + 1 + u, (1 + u) % 2, "pairs")
                group(NG - 1, 1, "last")
                if s.differential:
                    root(NG - 1)
                for count, x in enumerate(LAST):
                    read(x, 1, BEFORE_LAST + count)

            @block.vector
            def _(dve):
                dve.memset(v1[:], 1.0)
                prep = Link(dve, prep_s)
                dve.wait_ge(w_in, 16 * len(loads))
                if s.differential:
                    for n in range(2):
                        last = dve.tensor_tensor(lam[:T, 2 * n, :], lam[:T, 2 * n, :], lam[:T, 2 * n + 1, :], ALU.mult)
                    prep.after(last)
                    dve.tensor_reduce(lams[:T, :], lam[:T, 0:4:2, :], AX.X, ALU.add).then_inc(lam_sum, 1)
                    dve.wait_ge(lam_exp, 1)
                    prep.after(dve.tensor_tensor(neglam[:T, :], lams[:T, 1:2], lams[:T, 0:1], ALU.subtract))
                    dve.tensor_scalar(neglam[:T, :], neglam[:T, :], -LAMBDA_INIT, None, ALU.add)
                    dve.tensor_scalar(subln[:T, :], subln[:T, :], 1.0 - LAMBDA_INIT, None, ALU.mult)
                if s.keep is not None:
                    prep.after(dve.tensor_tensor(scale2[:T, :], c.rstd[:T, :], c.rstd[:T, :], ALU.mult))
                    prep.after(dve.tensor_tensor(scale2[:T, :], scale2[:T, :], c.moments[:T, :, 1], ALU.mult))
                    dve.tensor_scalar(scale2[:T, :], scale2[:T, :], 1e-6, None, ALU.add).then_inc(lam_sum, 1)
                    dve.wait_ge(lam_exp, 1)
                    prep.after(dve.reciprocal(scale2[:T, :], scale2[:T, :]))
                    prep.after(dve.tensor_tensor(scale2[:T, :], scale2[:T, :], c.rstd[:T, :], ALU.mult))
                prep.after(dve.memset(six[:], 0.0))
                dve.sem_inc(mix_ready, 1)

                def start(g):
                    normalize(dve, c, z, g, scale2 if s.keep is not None else None).then_inc(z_ready, 1)

                def subtract_most(link, r, n):
                    score = ps[:T, :, :N].rearrange("p c (x t) -> p c x t", x=4)
                    high = most[:T, n % 2, :]
                    dve.wait_ge(score_sum, r + 3)
                    link.after(dve.tensor_reduce(high.rearrange("p (c x) -> p c x", c=4), score, AX.X, ALU.max))
                    if s.differential:
                        link.after(dve.tensor_scalar(high, high, LARGEST, -LARGEST, ALU.min, ALU.max))
                        for q in range(4):
                            last = dve.scalar_tensor_tensor(
                                p[:T, n % 2, 4 * q:4 * q + 4, :], score[:, q], LARGEST,
                                high[:, 4 * q:4 * q + 4].unsqueeze(2).to_broadcast([T, 4, T]),
                                ALU.min, ALU.subtract)
                        last.then_inc(less_ready, 1)
                        return
                    dve.tensor_tensor(p[:T, n % 2].rearrange("p (c x) t -> p c x t", c=4), score,
                                      high.rearrange("p (c x) -> p c x", c=4).unsqueeze(3)
                                      .to_broadcast([T, 4, 4, T]), ALU.subtract).then_inc(less_ready, 1)

                def divide(link, r, parity, n):
                    j, m0 = at(n)
                    sums = po[:T, 0, :NX * (DH + 1)].rearrange("p (x d) -> p x d", x=NX)
                    dve.wait_ge(mix_sum, r + 3)
                    link.after(dve.reciprocal(inverse[:T, :], sums[:, :, DH]))
                    if s.differential:
                        link.after(dve.tensor_scalar(inverse[:T, 1:NX:2], inverse[:T, 1:NX:2],
                                                     neglam[:T, 0:1], None, ALU.mult))
                    out = o[:T, parity, j, :].rearrange("p (h d) -> p h d", d=DH) if not s.differential else two[:T]
                    last = dve.tensor_tensor(out, sums[:, :, 0:DH],
                                             inverse[:T, :].unsqueeze(2).to_broadcast([T, NX, DH]), ALU.mult)
                    last.then_inc(mix_ready, 1)
                    if s.differential:
                        dve.wait_ge(mix_ready, r + 2)
                        last = dve.tensor_tensor(
                            o[:T, parity, j, m0 * P:(m0 + 1) * P].rearrange("p (h d) -> p h d", d=DH),
                            two[:T, 0:NX:2, :], two[:T, 1:NX:2, :], ALU.add)
                    return last

                def square(link, parity):
                    flat_o = o[:T, parity].rearrange("p j d -> p (j d)")
                    flat_s = squares[:T].rearrange("p j d -> p (j d)")
                    link.after(dve.tensor_tensor(flat_s, flat_o, flat_o, ALU.mult))
                    link.after(dve.tensor_reduce(roots[:T, :], flat_s.rearrange("p (x d) -> p x d", d=DH),
                                                 AX.X, ALU.add))
                    dve.tensor_scalar(roots[:T, :], roots[:T, :], 1 / DH, 1e-5, ALU.mult,
                                      ALU.add).then_inc(square_ready, 1)

                def norm_heads(link, g, parity):
                    heads = o[:T, parity].rearrange("p j (h d) -> p (j h) d", d=DH)
                    dve.wait_ge(root_ready, g + 1)
                    link.after(dve.reciprocal(roots[:T, :], roots[:T, :]))
                    link.after(dve.tensor_tensor(heads, heads, roots[:T, :].unsqueeze(2)
                                                 .to_broadcast([T, G * H, DH]), ALU.mult))
                    last = dve.tensor_tensor(heads, heads, subln[:T, :].unsqueeze(1)
                                             .to_broadcast([T, G * H, DH]), ALU.mult)
                    last.then_inc(o_ready, 1)

                def read(link, x, g, parity, count):
                    if x[0] not in "vy":
                        return
                    k = int(x[1])
                    pair = (2 * k, 2 * k + 1)
                    dve.wait_ge(step_sum, count + 1)
                    if x[0] == "v":
                        for j in pair:
                            src = px[:T, 0, j % 2 * D:j % 2 * D + s.kv * DH].rearrange("p (h d) -> p h d", d=DH)
                            dst = v1[:T, parity, j, :, 0:DH]
                            if s.affine:
                                last = dve.scalar_tensor_tensor(
                                    dst, src, factors[:T, 2:3],
                                    vbias[:T, :].rearrange("p (h d) -> p h d", d=DH), ALU.mult, ALU.add)
                            else:
                                last = dve.tensor_copy(dst, src)
                        last.then_inc(step_done, 1)
                        return
                    y = [px[:T, 0, j % 2 * D:(j % 2 + 1) * D] for j in pair]
                    tiles = [c.tile(G * g + j) for j in pair]
                    if s.affine:
                        for j in pair:
                            last = dve.scalar_tensor_tensor(temp[:T, j, :], y[j % 2], factors[:T, 3:4],
                                                            obias[:T, :], ALU.mult, ALU.add)
                        last.then_inc(step_done, 1)
                        dve.wait_ge(step_done, count + 1)
                        for j in pair:
                            last = dve.tensor_tensor(tiles[j % 2], temp[:T, j, :], tiles[j % 2], ALU.add)
                        link.after(last)
                    elif s.keep is not None:
                        for j in pair:
                            last = dve.tensor_scalar(temp[:T, j, :], tiles[j % 2], c.mean(G * g + j),
                                                     c.scale(G * g + j), ALU.subtract, ALU.mult)
                        link.after(last)
                        for j in pair:
                            last = dve.tensor_tensor(flat(s.keep[:T, bass.ds(G * g + j, 1), :]),
                                                     y[j % 2], temp[:T, j, :], ALU.add)
                        last.then_inc(step_done, 1)
                        dve.wait_ge(step_done, count + 1)
                        for j in pair:
                            last = dve.tensor_tensor(tiles[j % 2], flat(s.keep[:T, bass.ds(G * g + j, 1), :]),
                                                     tiles[j % 2], ALU.add)
                        link.after(last)
                    else:
                        for j in pair:
                            last = dve.tensor_tensor(tiles[j % 2], y[j % 2], tiles[j % 2], ALU.add)
                        last.then_inc(step_done, 1)
                        dve.wait_ge(step_done, count + 1)
                    if k == 1:
                        of = (lambda j: c.tile(G * g + j)) if s.keep is None else (
                            lambda j: flat(s.keep[:T, bass.ds(G * g + j, 1), :]))
                        link.after(stats(dve, link, six, [
                            (of(j), flat(c.moments[:T, bass.ds(G * g + j, 1), :])) for j in range(G)]))

                def group(link, g, q, part):
                    def carry(n, slot):
                        for x, count in carried(part, n, slot):
                            read(link, x, g - 1 if x in LAST else g + 1, 1 - q, first_step(g, part) + count)

                    if part != "last":
                        start(g + 1)
                    for n in range(nr):
                        r = nr * g + n
                        if not (part == "last" and n == nr - 1):
                            subtract_most(link, r + 1, n + 1)
                        if s.differential and n == 1 and part != "first":
                            norm_heads(link, g - 1, 1 - q)
                        carry(n, 0)
                        carry(n, 1)
                        carry(n, 2)
                        last = divide(link, r, q, n)
                    if s.differential:
                        link.after(last)
                        square(link, q)

                per_round = 4 if s.differential else 2
                per_pairs = 2 * (nr * per_round + (5 if s.differential else 0) + 2 * bool(s.affine)
                                 + 4 * (s.keep is not None) + 3)
                start(0)
                link = Link(dve, link_first)
                for count, x in enumerate(NEXT):
                    read(link, x, 0, 0, count)
                subtract_most(link, 0, 0)
                group(link, 0, 0, "first")
                with dve.Fori(0, NG // 2 - 1) as i:
                    link = Link(dve, link_pairs, i, per_pairs)
                    for u in range(2):
                        group(link, 2 * i + 1 + u, (1 + u) % 2, "pairs")
                    link.end()
                link = Link(dve, link_last)
                group(link, NG - 1, 1, "last")
                if s.differential:
                    norm_heads(link, NG - 1, 1)
                for count, x in enumerate(LAST):
                    read(link, x, NG - 1, 1, BEFORE_LAST + count)


def scaled_attention(c, a):
    inverse_deviation(c, 1e-5, "tern")
    softmax_attention(c, a, Attention("tern", affine=True))


def weigh_two(c, r):
    with ExitStack() as st:
        above, tie = (c.sb(st, f"two_{n}", [P, B, E, E]) for n in ("above", "tie"))
        rank, taken = (c.sb(st, f"two_{n}", [P, B, E]) for n in ("rank", "taken"))
        before = c.sb(st, "two_before", [P, E, E])
        most, total = (c.sb(st, f"two_{n}", [P, B]) for n in ("most", "total"))
        made, link_s, less_ready, exp_ready = c.sems("made link less_ready exp_ready", "two")
        with c.nc.Block() as block:
            @block.gpsimd
            def _(pool):
                lower_index(pool, made, before)

            @block.scalar
            def _(act):
                act.wait_ge(less_ready, 1)
                act.activation(r.share[:T], r.share[:T], ACT.Exp).then_inc(exp_ready, 1)

            @block.vector
            def _(dve):
                link = Link(dve, link_s)
                dve.wait_ge(made, 2)
                ranks(dve, link, r, above, tie, before, rank)
                dve.tensor_scalar(taken[:T], rank[:T], 2.0, None, ALU.is_lt)
                link.after(dve.tensor_reduce(most[:T, :], r.share[:T], AX.X, ALU.max))
                dve.tensor_tensor(r.share[:T], r.share[:T], most[:T, :].unsqueeze(2).to_broadcast([T, B, E]),
                                  ALU.subtract).then_inc(less_ready, 1)
                dve.wait_ge(exp_ready, 1)
                link.after(dve.tensor_tensor(r.share[:T], r.share[:T], taken[:T], ALU.mult))
                link.after(dve.tensor_reduce(total[:T, :], r.share[:T], AX.X, ALU.add))
                link.after(dve.reciprocal(total[:T, :], total[:T, :]))
                link.after(dve.tensor_tensor(r.share[:T], r.share[:T],
                                             total[:T, :].unsqueeze(2).to_broadcast([T, B, E]), ALU.mult))


def linear_experts(c, r, a, name):
    nc = c.nc
    flat_share = r.share[:T].rearrange("p b e -> p (b e)")
    pairs = B // 2
    with ExitStack() as st:
        w = c.sb(st, r.ph + "_w", [P, KD, E * D])
        py = c.banks(st, r.ph + "_py", 8)
        w_in, y_sum, added = c.sems("w_in y_sum added", r.ph + "_experts")
        with nc.Block() as block:
            @block.sync
            def _(sp):
                sp.dma_start(w[:], a[name]).then_inc(w_in, 16)

            @block.tensor
            def _(pe):
                pe.wait_ge(w_in, 16)
                with pe.Fori(0, E) as e:
                    for n in range(pairs):
                        pe.wait_ge(added, pairs * e + n + 1)
                        for j in range(2):
                            b = 2 * n + j
                            for k in range(KD):
                                last = pe.matmul(py[:T, n % 8, j * D:(j + 1) * D], r.zt[:, k, b * T:(b + 1) * T],
                                                 w[:, k, bass.ds(D * e, D)], start=k == 0, stop=k == KD - 1)
                        last.then_inc(y_sum, 1)

            @block.vector
            def _(dve):
                dve.sem_inc(added, 8)
                with dve.Fori(0, E) as e:
                    for n in range(pairs):
                        dve.wait_ge(y_sum, pairs * e + n + 1)
                        dve.wait_ge(added, pairs * e + n + 1)
                        for j in range(2):
                            b = 2 * n + j
                            last = dve.scalar_tensor_tensor(
                                c.resid[:T, b, :], py[:T, n % 8, j * D:(j + 1) * D],
                                flat_share[:, bass.ds(E * b + e, 1)], c.resid[:T, b, :], ALU.mult, ALU.add)
                        last.then_inc(added, 1)


def grouped_block(c, a):
    inverse_deviation(c, 1e-5, "gqa")
    with ExitStack() as st:
        inner = c.sb(st, "gqa_inner", [P, B, D])
        softmax_attention(c, a, Attention("gqa", kv=4, causal=True, norm="gqa_norm", keep=inner))
        (squared,) = c.sems("squared", "gqa_square")
        with c.nc.Block() as block:
            @block.vector
            def _(dve):
                dve.tensor_tensor(c.rstd[:T, :], c.moments[:T, :, 0], c.moments[:T, :, 0], ALU.mult).then_inc(squared, 1)
                dve.wait_ge(squared, 1)
                dve.tensor_tensor(c.moments[:T, :, 1], c.moments[:T, :, 1], c.rstd[:T, :], ALU.add)\
                   .then_inc(squared, 1)
                dve.wait_ge(squared, 2)
        inverse_deviation(c, 1e-6, "gqa_rms")
        r = Routing(c, st, "top2")

        def rms(dve, z, g):
            for j in range(G):
                b = G * g + j
                last = dve.tensor_scalar(z[:T, j, :], flat(inner[:T, bass.ds(b, 1), :]), c.scale(b), None, ALU.mult)
            return last

        gather_tokens(c, r, rms, "top2_wg", (), "top2_norm", a)
        weigh_two(c, r)
        linear_experts(c, r, a, "top2_w")
    all_stats(c, "top2")


def differential_attention(c, a):
    inverse_deviation(c, 1e-5, "diff")
    softmax_attention(c, a, Attention("diff", dm=DH // 2, scale=(DH // 2) ** -0.5, differential=True))


CAPACITY = math.ceil(B * T / E)
ENOUGH = 0.9


def route_by_threshold(c, r):
    nc = c.nc
    with ExitStack() as st:
        above, tie = (c.sb(st, f"cap_{n}", [P, B, E, E]) for n in ("above", "tie"))
        rank, value, at_least, equal = (c.sb(st, f"cap_{n}", [P, B, E]) for n in ("rank", "value", "at_least", "equal"))
        places, runs, totals = (c.sb(st, f"cap_{n}", [P, E, B]) for n in ("places", "runs", "totals"))
        before = c.sb(st, "cap_before", [P, E, E])
        earlier = c.sb(st, "cap_earlier", [P, P])
        most = c.sb(st, "cap_most", [P, B])
        count, level, step, trial, room = (c.sb(st, f"cap_{n}", [P, E]) for n in ("count", "level", "step", "trial", "room"))
        pc = c.banks(st, "cap_pc", 3)
        made, link_s, less_ready, exp_ready, counted, summed, counted2, summed2, marked, prefixed, scan_s = c.sems(
            "made link less_ready exp_ready counted summed counted2 summed2 marked prefixed scan", "cap")
        steps = 27

        def per_expert(x):
            return x[:T].unsqueeze(1).to_broadcast([T, B, E])

        with nc.Block() as block:
            @block.gpsimd
            def _(pool):
                lower_index(pool, made, before)
                pool.memset(earlier[:], 1.0).then_inc(made, 1)
                pool.wait_ge(made, 3)
                pool.affine_select(out=earlier[:], in_=earlier[:], compare_op=ALU.is_gt, fill=0.0, base=0,
                                   pattern=[[1, P]], channel_multiplier=-1).then_inc(made, 1)

            @block.scalar
            def _(act):
                act.wait_ge(less_ready, 1)
                act.activation(r.share[:T], r.share[:T], ACT.Exp).then_inc(exp_ready, 1)

            @block.tensor
            def _(pe):
                with pe.Fori(0, steps) as i:
                    pe.wait_ge(counted, i + 1)
                    pe.matmul(pc[:, 0, :E], c.ones[:T, :], count[:T, :], start=True, stop=True).then_inc(summed, 1)
                pe.wait_ge(counted2, 1)
                pe.matmul(pc[:, 0, :E], c.ones[:T, :], count[:T, :], start=True, stop=True).then_inc(summed2, 1)
                pe.wait_ge(made, 4)
                pe.wait_ge(marked, 1)
                marks = equal[:T].rearrange("p b e -> p (b e)")
                pe.matmul(pc[:T, 1, :B * E], earlier[:T, :T], marks, start=True, stop=True)
                pe.matmul(pc[:T, 2, :B * E], c.ones[:T, :T], marks, start=True, stop=True).then_inc(prefixed, 1)

            @block.vector
            def _(dve):
                link = Link(dve, link_s)
                link.after(dve.tensor_reduce(most[:T, :], r.share[:T], AX.X, ALU.max))
                dve.tensor_tensor(r.share[:T], r.share[:T], most[:T, :].unsqueeze(2).to_broadcast([T, B, E]),
                                  ALU.subtract).then_inc(less_ready, 1)
                dve.wait_ge(exp_ready, 1)
                link.after(dve.tensor_reduce(most[:T, :], r.share[:T], AX.X, ALU.add))
                link.after(dve.reciprocal(most[:T, :], most[:T, :]))
                link.after(dve.tensor_tensor(r.share[:T], r.share[:T],
                                             most[:T, :].unsqueeze(2).to_broadcast([T, B, E]), ALU.mult))
                dve.wait_ge(made, 2)
                ranks(dve, link, r, above, tie, before, rank)
                link.after(dve.tensor_tensor(above[:T], above[:T],
                                             r.share[:T].unsqueeze(2).to_broadcast([T, B, E, E]), ALU.mult))
                link.after(dve.tensor_reduce(equal[:T], above[:T], AX.X, ALU.add))
                dve.tensor_scalar(at_least[:T], equal[:T], ENOUGH, None, ALU.is_lt)
                link.after(dve.tensor_scalar(rank[:T], rank[:T], 1.0, None, ALU.add))
                link.after(dve.tensor_tensor(value[:T], r.share[:T], rank[:T], ALU.subtract))
                dve.tensor_tensor(value[:T], value[:T], at_least[:T], ALU.mult)
                link.after(dve.tensor_scalar(equal[:T], at_least[:T], 1.0, 1e9, ALU.subtract, ALU.mult))
                dve.memset(level[:], -8.0)
                dve.memset(step[:], 4.0)
                link.after(dve.tensor_tensor(value[:T], value[:T], equal[:T], ALU.add))

                with dve.Fori(0, steps) as i:
                    loop = Link(dve, scan_s, i, 5)
                    loop.after(dve.tensor_tensor(trial[:T, :], level[:T, :], step[:T, :], ALU.add))
                    loop.after(dve.tensor_tensor(at_least[:T], value[:T], per_expert(trial), ALU.is_ge))
                    dve.tensor_reduce(count[:T, :], at_least[:T].rearrange("p b e -> p e b"), AX.X,
                                      ALU.add).then_inc(counted, 1)
                    dve.wait_ge(summed, i + 1)
                    loop.after(dve.scalar_tensor_tensor(trial[:T, :], pc[:T, 0, :E], float(CAPACITY), step[:T, :],
                                                        ALU.is_ge, ALU.mult))
                    dve.tensor_scalar(step[:T, :], step[:T, :], 0.5, None, ALU.mult)
                    loop.after(dve.tensor_tensor(level[:T, :], level[:T, :], trial[:T, :], ALU.add))
                    loop.after(dve.memset(room[:], 0.0))
                    loop.end()
                link.after(dve.tensor_tensor(at_least[:T], value[:T], per_expert(level), ALU.is_gt))
                dve.tensor_tensor(equal[:T], value[:T], per_expert(level), ALU.is_equal).then_inc(marked, 1)
                dve.tensor_reduce(count[:T, :], at_least[:T].rearrange("p b e -> p e b"), AX.X,
                                  ALU.add).then_inc(counted2, 1)
                dve.wait_ge(summed2, 1)
                dve.tensor_scalar(room[:T, :], pc[:T, 0, :E], -1.0, float(CAPACITY), ALU.mult, ALU.add)
                dve.memset(runs[:], 1.0)
                dve.wait_ge(prefixed, 1)
                link.after(dve.tensor_copy(totals[:T], pc[:T, 2, :B * E].rearrange("p (b e) -> p e b", e=E)))
                link.after(dve.memset(runs[:, :, 0:1], 0.0))
                link.after(dve.tensor_tensor_scan(places[:T].rearrange("p e b -> p (e b)"),
                                                  runs[:T].rearrange("p e b -> p (e b)"),
                                                  totals[:T].rearrange("p e b -> p (e b)"), 0.0, ALU.mult, ALU.add))
                link.after(dve.tensor_tensor(places[:T], places[:T], totals[:T], ALU.subtract))
                link.after(dve.tensor_tensor(rank[:T], places[:T].rearrange("p e b -> p b e"),
                                             pc[:T, 1, :B * E].rearrange("p (b e) -> p b e", e=E), ALU.add))
                link.after(dve.tensor_tensor(rank[:T], rank[:T], per_expert(room), ALU.is_lt))
                link.after(dve.tensor_tensor(rank[:T], rank[:T], equal[:T], ALU.mult))
                link.after(dve.tensor_tensor(rank[:T], rank[:T], at_least[:T], ALU.add))
                link.after(dve.tensor_tensor(r.share[:T], r.share[:T], rank[:T], ALU.mult))


def capacity_experts(c, a):
    inverse_deviation(c, 1e-5, "xmoe")
    with ExitStack() as st:
        r = Routing(c, st, "xmoe")
        gather_tokens(c, r, lambda dve, z, g: normalize(dve, c, z, g), "xmoe_wg", (), None, a)
        route_by_threshold(c, r)
        experts(c, r, a, ("xmoe_w1", "xmoe_w2"), D // P, ACT.Gelu, None)


def gated_linear_attention(c, a):
    nc = c.nc
    inverse_deviation(c, 1e-5, "gla")
    L = T + 1
    NH2 = P // DH
    with ExitStack() as st:
        wqf = c.sb(st, "gla_wqf", [P, KD, 2 * D])
        wv, wo = (c.sb(st, f"gla_w{n}", [P, KD, D]) for n in "vo")
        own = c.sb(st, "gla_own", [P, NH2])
        falls = c.sb(st, "gla_falls", [P, L])
        nexts = c.sb(st, "gla_nexts", [P, T])
        z = c.sb(st, "gla_z", [P, G, D])
        zt = c.sb(st, "gla_zt", [P, KD, N])
        rows = c.sb(st, "gla_rows", [P, G, 2, D])
        high, total = (c.sb(st, f"gla_{n}", [P, G * 2]) for n in ("high", "total"))
        v = c.sb(st, "gla_v", [P, G, D])
        fall = c.sb(st, "gla_fall", [P, G, D])
        after = c.sb(st, "gla_after", [P, G, D])
        wide = c.sb(st, "gla_wide", [P, 4, G, P])
        weight = c.sb(st, "gla_weight", [P, G, H])
        qt = c.sb(st, "gla_qt", [P, KD, G, T])
        at = c.sb(st, "gla_at", [P, KD, G, L])
        state = c.sb(st, "gla_state", [P, 2, G, L])
        read = c.sb(st, "gla_read", [P, 2, G, T])
        o = c.sb(st, "gla_o", [P, G, D])
        ot = c.sb(st, "gla_ot", [P, KD, N])
        six = c.sb(st, "gla_six", [P, G, 9])
        ps = c.banks(st, "gla_ps", 4)
        pp = c.banks(st, "gla_pp", 2)
        po = c.banks(st, "gla_po", 2)
        (w_in, made, z_ready, zt_sum, zt_ready, rows_sum, less_ready, exp_ready, rows_ready, v_sum, v_ready,
         fall_sum, fall_ready, after_sum, after_ready, turned, turned_ready, spread, state_ready, read_ready, repeated,
         o_sum, o_ready, ot_sum, ot_ready, y_sum, done, link_s) = c.sems(
            "w_in made z_ready zt_sum zt_ready rows_sum less_ready exp_ready rows_ready v_sum v_ready "
            "fall_sum fall_ready after_sum after_ready turned turned_ready spread state_ready read_ready repeated "
            "o_sum o_ready ot_sum ot_ready y_sum done link", "gla")
        nu = KD * DH

        with nc.Block() as block:
            @block.sync
            def _(sp):
                for dst, name in ((wqf[:, :, :D], "gla_wq"), (wqf[:, :, D:], "gla_wf"), (wv[:], "gla_wv"),
                                  (wo[:], "gla_wo")):
                    sp.dma_start(dst, a[name]).then_inc(w_in, 16)

            @block.gpsimd
            def _(pool):
                def band(x, base, value, width, ready):
                    pool.affine_select(out=x, in_=x, compare_op=ALU.not_equal, fill=value, base=-base,
                                       pattern=[[-1, width]], channel_multiplier=1).then_inc(made, 1)
                    pool.wait_ge(made, ready)

                pool.memset(own[:], 1.0).then_inc(made, 1)
                pool.memset(falls[:], 0.0).then_inc(made, 1)
                pool.memset(nexts[:], 0.0).then_inc(made, 1)
                pool.wait_ge(made, 3)
                pool.affine_select(out=own[:], in_=own[:], compare_op=ALU.is_ge, fill=0.0, base=0,
                                   pattern=[[-DH, NH2]], channel_multiplier=1).then_inc(made, 1)
                pool.wait_ge(made, 4)
                pool.affine_select(out=own[:], in_=own[:], compare_op=ALU.is_ge, fill=0.0, base=DH - 1,
                                   pattern=[[DH, NH2]], channel_multiplier=-1).then_inc(made, 1)
                band(falls[:], -1, 1.0, L, 6)
                band(falls[:], 0, -1.0, L, 7)
                band(nexts[:], 1, 1.0, T, 8)
                pool.sem_inc(read_ready, 2)
                with pool.Fori(0, NG) as g:
                    for w in range(nu):
                        pool.wait_ge(state_ready, nu * g + w + 1)
                        pool.wait_ge(o_sum, nu * g + w + 1)
                        pool.tensor_tensor(read[:, w % 2], state[:, w % 2, :, 1:], qt[:, w // DH],
                                           ALU.mult).then_inc(read_ready, 1)

            @block.tensor
            def _(pe):
                pe.sem_inc(o_sum, 2)
                pe.sem_inc(spread, 4)
                pe.wait_ge(w_in, 64)
                pe.wait_ge(made, 8)
                with pe.Fori(0, NG) as g:
                    pe.wait_ge(z_ready, g + 1)
                    to_features(pe, c, pp, z).then_inc(zt_sum, 1)
                    pe.wait_ge(zt_ready, g + 1)
                    pe.wait_ge(done, g + 1)
                    for j in range(G):
                        for k in range(KD):
                            last = pe.matmul(ps[:T, j, :], zt[:, k, j * T:(j + 1) * T], wqf[:, k, :],
                                             start=k == 0, stop=k == KD - 1)
                    last.then_inc(rows_sum, 1)
                    token_product(pe, pp, zt, wv).then_inc(v_sum, 1)
                    pe.wait_ge(v_ready, g + 1)
                    for n in range(2):
                        last = pe.matmul(pp[:L, n, :], falls[:T, :], v[:T, 2 * n:2 * n + 2, :].rearrange(
                            "p j d -> p (j d)"), start=True, stop=True)
                    last.then_inc(fall_sum, 1)
                    pe.wait_ge(fall_ready, g + 1)
                    for n in range(2):
                        last = pe.matmul(pp[:T, n, :], nexts[:T, :], v[:T, 2 * n:2 * n + 2, :].rearrange(
                            "p j d -> p (j d)"), start=True, stop=True)
                    last.then_inc(after_sum, 1)
                    pe.wait_ge(rows_ready, g + 1)
                    for n in range(2):
                        for k in range(KD):
                            for j in range(G):
                                last = pe.transpose(ps[:, 2 * n + k, j * T:(j + 1) * T],
                                                    rows[:T, j, n, k * P:(k + 1) * P], c.ident[:T, :T])
                    last.then_inc(turned, 1)
                    pe.wait_ge(turned_ready, g + 1)
                    pe.wait_ge(after_ready, g + 1)

                    def increments(w):
                        if w >= 4:
                            pe.wait_ge(state_ready, nu * g + w - 3)
                        pe.wait_ge(repeated, nu * g + w + 1)
                        for j in range(G):
                            last = pe.transpose(ps[:, w % 4, j * L:(j + 1) * L], wide[:L, w % 4, j, :],
                                                c.ident[:L, :L])
                        last.then_inc(spread, 1)

                    def contract(w):
                        m, e = w // DH, w % DH
                        pe.wait_ge(read_ready, nu * g + w + 3)
                        for j in range(G):
                            out = po[:T, j // 2, j % 2 * D + m * P:j % 2 * D + (m + 1) * P]
                            last = pe.matmul(out.rearrange("p (h d) -> p h d", d=DH)[:, :, e],
                                             read[:, w % 2, j, :], own[:], start=True, stop=True)
                        last.then_inc(o_sum, 1)

                    for w in range(4):
                        increments(w)
                    for w in range(nu):
                        contract(w)
                        if w + 4 < nu:
                            increments(w + 4)
                    pe.wait_ge(o_ready, g + 1)
                    to_features(pe, c, pp, o).then_inc(ot_sum, 1)
                    pe.wait_ge(ot_ready, g + 1)
                    token_product(pe, ps[:, 0:2], ot, wo).then_inc(y_sum, 1)

            @block.scalar
            def _(act):
                with act.Fori(0, NG) as g:
                    act.wait_ge(zt_sum, g + 1)
                    act.activation(zt[:], pp[:, :, :N], ACT.Copy).then_inc(zt_ready, 1)
                    act.wait_ge(v_sum, g + 1)
                    act.activation(v[:T].rearrange("p j d -> p (j d)"),
                                   pp[:T, :, :].rearrange("p n d -> p (n d)"), ACT.Copy).then_inc(v_ready, 1)
                    act.wait_ge(less_ready, g + 1)
                    act.activation(rows[:T].rearrange("p j n d -> p (j n d)"),
                                   rows[:T].rearrange("p j n d -> p (j n d)"), ACT.Exp).then_inc(exp_ready, 1)
                    act.wait_ge(fall_sum, g + 1)
                    act.activation(fall[:L].rearrange("p j d -> p (j d)"),
                                   pp[:L, :, :].rearrange("p n d -> p (n d)"), ACT.Copy).then_inc(fall_ready, 1)
                    act.wait_ge(after_sum, g + 1)
                    act.activation(after[:T].rearrange("p j d -> p (j d)"),
                                   pp[:T, :, :].rearrange("p n d -> p (n d)"), ACT.Copy).then_inc(after_ready, 1)
                    act.wait_ge(turned, g + 1)
                    for k in range(KD):
                        act.activation(qt[:, k], ps[:, k, :N].rearrange("p (j t) -> p j t", j=G), ACT.Copy)
                        last = act.activation(at[:, k, :, 1:], ps[:, 2 + k, :N].rearrange("p (j t) -> p j t", j=G),
                                              ACT.Copy)
                    last.then_inc(turned_ready, 1)
                    for w in range(nu):
                        m, e = w // DH, w % DH
                        act.wait_ge(spread, nu * g + w + 1)
                        column = fall[:L, :, m * P:(m + 1) * P].rearrange("p j (h d) -> p j h d", d=DH)[:, :, :, e:e + 1]
                        act.activation(wide[:L, w % 4].rearrange("p j (h k) -> p j h k", k=DH),
                                       column.to_broadcast([L, G, NH2, DH]), ACT.Copy).then_inc(repeated, 1)
                    act.wait_ge(ot_sum, g + 1)
                    act.activation(ot[:], pp[:, :, :N], ACT.Copy).then_inc(ot_ready, 1)

            @block.vector
            def _(dve):
                dve.memset(at[:, :, :, 0:1], 0.0)
                dve.sem_inc(done, 1)
                with dve.Fori(0, NG) as g:
                    link = Link(dve, link_s, g, 9)
                    normalize(dve, c, z, g).then_inc(z_ready, 1)
                    dve.wait_ge(rows_sum, g + 1)
                    both = ps[:T].rearrange("p j (n d) -> p (j n) d", n=2)
                    rows8 = rows[:T].rearrange("p j n d -> p (j n) d")
                    link.after(dve.tensor_reduce(high[:T, :], both, AX.X, ALU.max))
                    dve.tensor_tensor(rows8, both, high[:T, :].unsqueeze(2).to_broadcast([T, 2 * G, D]),
                                      ALU.subtract).then_inc(less_ready, 1)
                    dve.wait_ge(exp_ready, g + 1)
                    link.after(dve.tensor_reduce(total[:T, :], rows8, AX.X, ALU.add))
                    link.after(dve.reciprocal(total[:T, :], total[:T, :]))
                    for j in range(G):
                        dve.tensor_scalar(rows[:T, j, 0, :], rows[:T, j, 0, :], total[:T, 2 * j:2 * j + 1],
                                          DH ** -0.5, ALU.mult, ALU.mult)
                        last = dve.tensor_scalar(rows[:T, j, 1, :], rows[:T, j, 1, :], total[:T, 2 * j + 1:2 * j + 2],
                                                 None, ALU.mult)
                    last.then_inc(rows_ready, 1)
                    dve.wait_ge(rows_ready, g + 1)
                    link.after(dve.tensor_reduce(weight[:T], rows[:T, :, 0, :].rearrange("p j (h d) -> p j h d", d=DH),
                                                 AX.X, ALU.add))
                    dve.wait_ge(after_ready, g + 1)
                    dve.tensor_tensor(after[:T].rearrange("p j (h d) -> p (j h) d", d=DH),
                                      after[:T].rearrange("p j (h d) -> p (j h) d", d=DH),
                                      weight[:T].rearrange("p j h -> p (j h)").unsqueeze(2)
                                      .to_broadcast([T, G * H, DH]), ALU.mult)
                    dve.wait_ge(turned_ready, g + 1)
                    for w in range(nu):
                        dve.wait_ge(spread, nu * g + w + 5)
                        dve.wait_ge(read_ready, nu * g + w + 1)
                        dve.tensor_tensor_scan(state[:, w % 2].rearrange("p j t -> p (j t)"),
                                               at[:, w // DH].rearrange("p j t -> p (j t)"),
                                               ps[:, w % 4, :G * L], 0.0, ALU.mult, ALU.add).then_inc(state_ready, 1)
                    dve.wait_ge(o_sum, nu * (g + 1) + 2)
                    dve.tensor_tensor(o[:T].rearrange("p j d -> p (j d)"), po[:T].rearrange("p n d -> p (n d)"),
                                      after[:T].rearrange("p j d -> p (j d)"), ALU.add).then_inc(o_ready, 1)
                    dve.wait_ge(y_sum, g + 1)
                    link.after(add_to_residual(dve, c, ps[:, 0:2], g))
                    link.after(tile_stats(dve, c, link, six, g))
                    link.after(dve.memset(six[:, 0, 8:9], 0.0))
                    dve.tensor_copy(six[:, 1, 8:9], six[:, 0, 8:9]).then_inc(done, 1)
                    link.end()


LEVELS = 127.0
TINY = 1e-5


def ternary_network(c, a):
    nc = c.nc
    inverse_deviation(c, 1e-5, "bit")
    NF = FF // P
    with ExitStack() as st:
        w = c.sb(st, "bit_w", [P, 3, KD * FF])
        wt = c.sb(st, "bit_wt", [P, 3, KD * FF], BF16)
        gate, up = (wt[:, n, :].rearrange("p (k f) -> p k f", k=KD) for n in range(2))
        down = wt[:, 2, :].rearrange("p (f d) -> p f d", f=NF)
        mean = c.sb(st, "bit_mean", [P, 3])
        factor = c.sb(st, "bit_factor", [P, 3])
        identh = c.sb(st, "bit_identh", [P, P], BF16)
        z = c.sb(st, "bit_z", [P, G, D])
        xh = c.sb(st, "bit_xh", [P, G, D], BF16)
        xt = c.sb(st, "bit_xt", [P, KD, N], BF16)
        size, grid, back, back2 = (c.sb(st, f"bit_{n}", [P, G]) for n in ("size", "grid", "back", "back2"))
        swish = c.sb(st, "bit_swish", [P, 2, FF])
        inner = c.sb(st, "bit_inner", [P, 2, FF])
        ih = c.sb(st, "bit_ih", [P, 2, FF], BF16)
        it = c.sb(st, "bit_it", [P, 2, NF, T], BF16)
        isize, igrid, iback = (c.sb(st, f"bit_{n}", [P, 2]) for n in ("isize", "igrid", "iback"))
        six = c.sb(st, "bit_six", [P, G, 9])
        pg = c.banks(st, "bit_pg", 4)
        px = st.enter_context(nc.psum_tensor("bit_px", [P, 1, 2 * BANK], BF16))
        pi = st.enter_context(nc.psum_tensor("bit_pi", [P, 1, 2 * BANK], BF16))
        py = c.banks(st, "bit_py", 2)
        (w_in, means, mean_sum, prep_s, ready, x_ready, xt_sum, xt_ready, gate_sum, swish_ready, inner_used,
         i_ready, it_sum, it_ready, y_sum, done, link_s) = c.sems(
            "w_in means mean_sum prep ready x_ready xt_sum xt_ready gate_sum swish_ready inner_used "
            "i_ready it_sum it_ready y_sum done link", "bit")

        with nc.Block() as block:
            @block.sync
            def _(sp):
                for n, name in enumerate(("bit_gate", "bit_up", "bit_down")):
                    sp.dma_start(w[:, n, :], a[name].rearrange("p k f -> p (k f)")).then_inc(w_in, 16)

            @block.tensor
            def _(pe):
                pe.sem_inc(y_sum, 2)
                pe.wait_ge(means, 1)
                pe.matmul(pg[:, 0, :3], c.ones[:], mean[:], start=True, stop=True).then_inc(mean_sum, 1)
                pe.wait_ge(ready, 1)
                with pe.Fori(0, NG) as g:
                    pe.wait_ge(x_ready, g + 1)
                    for k in range(KD):
                        for j in range(G):
                            last = pe.transpose(px[:, 0, k * BANK + j * T:k * BANK + (j + 1) * T],
                                                xh[:T, j, k * P:(k + 1) * P], identh[:T, :T])
                    last.then_inc(xt_sum, 1)
                    pe.wait_ge(xt_ready, g + 1)

                    def open_up(j):
                        if j:
                            pe.wait_ge(inner_used, G * g + j + 1)
                        for n, weight in enumerate((gate, up)):
                            for f in range(2):
                                for k in range(KD):
                                    last = pe.matmul(pg[:T, 2 * n + f, :], xt[:, k, j * T:(j + 1) * T],
                                                     weight[:, k, f * BANK:(f + 1) * BANK],
                                                     start=k == 0, stop=k == KD - 1)
                        last.then_inc(gate_sum, 1)

                    def turn(j):
                        pe.wait_ge(i_ready, G * g + j + 1)
                        pe.wait_ge(it_ready, G * g + j + 1)
                        for f in range(NF):
                            last = pe.transpose(pi[:, 0, f * P:f * P + T], ih[:T, j % 2, f * P:(f + 1) * P],
                                                identh[:T, :T])
                        last.then_inc(it_sum, 1)

                    def close(j):
                        pe.wait_ge(it_ready, G * g + j + 2)
                        pe.wait_ge(done, G * g + j + 1)
                        for f in range(NF):
                            last = pe.matmul(py[:T, j % 2, :D], it[:, j % 2, f, :], down[:, f, :],
                                             start=f == 0, stop=f == NF - 1)
                        last.then_inc(y_sum, 1)

                    open_up(0)
                    for j in range(G):
                        if j + 1 < G:
                            open_up(j + 1)
                        turn(j)
                        close(j)

            @block.scalar
            def _(act):
                act.sem_inc(it_ready, 1)
                act.activation(identh[:], c.ident[:], ACT.Copy).then_inc(ready, 1)
                with act.Fori(0, NG) as g:
                    act.wait_ge(xt_sum, g + 1)
                    act.activation(xt[:], px[:, 0, :].rearrange("p (k n) -> p k n", k=KD)[:, :, :N],
                                   ACT.Copy).then_inc(xt_ready, 1)

                    def swishes(j):
                        act.wait_ge(gate_sum, G * g + j + 1)
                        act.wait_ge(inner_used, G * g + j + 1)
                        act.activation(swish[:T, j % 2, :], pg[:T, 0:2, :].rearrange("p n d -> p (n d)"), ACT.Silu,
                                       scale=back[:T, j:j + 1]).then_inc(swish_ready, 1)

                    for j in range(G):
                        swishes(j)
                        if j:
                            act.wait_ge(it_sum, G * g + j)
                            act.wait_ge(y_sum, G * g + j)
                            act.activation(it[:, (j - 1) % 2], pi[:, 0, :].rearrange("p (f n) -> p f n", n=P)[:, :, :T],
                                           ACT.Copy).then_inc(it_ready, 1)
                    act.wait_ge(it_sum, G * g + G)
                    act.wait_ge(y_sum, G * g + G)
                    act.activation(it[:, (G - 1) % 2], pi[:, 0, :].rearrange("p (f n) -> p f n", n=P)[:, :, :T],
                                   ACT.Copy).then_inc(it_ready, 1)

            @block.vector
            def _(dve):
                prep = Link(dve, prep_s)
                for n in range(3):
                    dve.wait_ge(w_in, 48)
                    last = dve.tensor_reduce(mean[:, n:n + 1], w[:, n, :], AX.X, ALU.add, apply_absolute_value=True)
                last.then_inc(means, 1)
                dve.wait_ge(mean_sum, 1)
                prep.after(dve.tensor_scalar(mean[:], pg[:, 0, :3], 1.0 / (D * FF), TINY, ALU.mult, ALU.max))
                prep.after(dve.reciprocal(factor[:], mean[:]))
                for n in range(3):
                    last = dve.tensor_scalar(w[:, n, :], w[:, n, :], factor[:, n:n + 1], ROUND, ALU.mult, ALU.add)
                prep.after(last)
                flat_w = w[:].rearrange("p n f -> p (n f)")
                prep.after(dve.tensor_scalar(flat_w, flat_w, ROUND, -1.0, ALU.subtract, ALU.max))
                prep.after(dve.tensor_scalar(wt[:].rearrange("p n f -> p (n f)"), flat_w, 1.0, None, ALU.min))
                dve.tensor_scalar(factor[:], mean[:], 1.0 / LEVELS, None, ALU.mult)
                dve.memset(size[:], 0.0)
                dve.wait_ge(ready, 1)
                dve.memset(grid[:], 0.0).then_inc(ready, 1)
                dve.wait_ge(ready, 2)
                dve.sem_inc(done, 2)
                dve.sem_inc(inner_used, 1)
                with dve.Fori(0, NG) as g:
                    link = Link(dve, link_s, g, 6 + G * 9)
                    link.after(normalize(dve, c, z, g))
                    link.after(dve.tensor_reduce(size[:T, :], z[:T], AX.X, ALU.max, apply_absolute_value=True))
                    link.after(dve.tensor_scalar(size[:T, :], size[:T, :], TINY, None, ALU.max))
                    dve.tensor_scalar(back[:T, :], size[:T, :], factor[:T, 0:1], None, ALU.mult)
                    dve.tensor_scalar(back2[:T, :], size[:T, :], factor[:T, 1:2], None, ALU.mult)
                    link.after(dve.reciprocal(grid[:T, :], size[:T, :]))
                    link.after(dve.tensor_scalar(grid[:T, :], grid[:T, :], LEVELS, None, ALU.mult))
                    for j in range(G):
                        last = dve.tensor_scalar(z[:T, j, :], z[:T, j, :], grid[:T, j:j + 1], ROUND, ALU.mult, ALU.add)
                    link.after(last)
                    dve.tensor_scalar(xh[:T].rearrange("p j d -> p (j d)"), z[:T].rearrange("p j d -> p (j d)"),
                                      ROUND, None, ALU.subtract).then_inc(x_ready, 1)
                    for j in range(G):
                        x = inner[:T, j % 2, :]
                        n = j % 2
                        dve.wait_ge(swish_ready, G * g + j + 1)
                        dve.scalar_tensor_tensor(x, pg[:T, 2:4, :].rearrange("p n d -> p (n d)"),
                                                 back2[:T, j:j + 1], swish[:T, j % 2, :], ALU.mult,
                                                 ALU.mult).then_inc(inner_used, 1)
                        dve.wait_ge(inner_used, G * g + j + 2)
                        link.after(dve.tensor_reduce(isize[:T, n:n + 1], x, AX.X, ALU.max, apply_absolute_value=True))
                        link.after(dve.tensor_scalar(isize[:T, n:n + 1], isize[:T, n:n + 1], TINY, None, ALU.max))
                        dve.tensor_scalar(iback[:T, n:n + 1], isize[:T, n:n + 1], factor[:T, 2:3], None, ALU.mult)
                        link.after(dve.reciprocal(igrid[:T, n:n + 1], isize[:T, n:n + 1]))
                        link.after(dve.tensor_scalar(igrid[:T, n:n + 1], igrid[:T, n:n + 1], LEVELS, None, ALU.mult))
                        link.after(dve.tensor_scalar(x, x, igrid[:T, n:n + 1], ROUND, ALU.mult, ALU.add))
                        dve.tensor_scalar(ih[:T, j % 2, :], x, ROUND, None, ALU.subtract).then_inc(i_ready, 1)
                        dve.wait_ge(y_sum, G * g + j + 3)
                        b = G * g + j
                        link.after(dve.scalar_tensor_tensor(c.tile(b), py[:T, j % 2, :D], iback[:T, n:n + 1],
                                                            c.tile(b), ALU.mult, ALU.add))
                        link.after(stats(dve, link, six, [(c.tile(b), flat(c.moments[:T, bass.ds(b, 1), :]))]))
                        dve.memset(six[:, 0, 8:9], 0.0).then_inc(done, 1)
                    link.end()


def matrix(w):
    return w.reshape(-1, P, w.shape[1]).transpose(1, 0, 2)


def matrices(w):
    return w.reshape(w.shape[0], -1, P, w.shape[2]).transpose(0, 2, 1, 3)


def layouts(x):
    image = x["x"].reshape(NG, G, 3, NI // PATCH, PATCH, NI // PATCH, PATCH)
    image = image.transpose(0, 2, 4, 6, 1, 3, 5).reshape(NG, KT, P, G, NPATCH).transpose(0, 2, 1, 3, 4)
    patches = np.zeros((NG, P, KT, G, CLS), image.dtype)
    patches[..., 1:] = image
    t = {"patches": patches, "txt": x["txt"].transpose(1, 0, 2),
         "tok_w": matrix(x["L0_tok_W"].T), "tok_b": x["L0_tok_b"],
         "tok_cls": x["L0_tok_cls_token"][0], "tok_pos": x["L0_tok_pos_embedding"][0]}
    for n in "qkvp":
        t[f"rff_w{n}"] = matrix(x[f"L0_attn_W{n}"].T)
    t["rff_bp"] = x["L0_attn_bp"][None]
    t["rff_br"] = x["L0_attn_br"].T
    t["rff_wr"] = x["L0_attn_Wr"].transpose(1, 0, 2)
    t["top1_wg"] = matrix(x["L0_ffn_gate_w"].T)
    t["top1_gate_b"], t["top1_expert_bias"] = x["L0_ffn_gate_b"], x["L0_ffn_expert_bias"]
    t["top1_b1"] = x["L0_ffn_b1"].reshape(E, FF // P, P).transpose(0, 2, 1)
    t["top1_b2"] = x["L0_ffn_b2"]
    t["top1_w1"] = matrices(x["L0_ffn_w1"])
    t["top1_w2"] = matrices(x["L0_ffn_w2"])
    for n in "qkvo":
        t[f"tern_w{n}"] = matrix(x[f"L1_attn_w_{n}"].T)
        t[f"tern_s{n}"] = np.reshape(x[f"L1_attn_s_{n}"], (1,))
        t[f"tern_b{n}"] = x[f"L1_attn_b_{n}"]
    t["tern_bq"], t["tern_bk"] = (x[f"L1_attn_b_{n}"].reshape(KD, P).T for n in "qk")
    t["gqa_wq"], t["gqa_wo"] = (matrix(x[f"L1_ffn_w{n}"].T) for n in "qo")
    t["gqa_wk"] = matrix(np.repeat(x["L1_ffn_wk"].reshape(4, DH, D), H // 4, axis=0).reshape(D, D).T)
    t["gqa_wv"] = matrix(x["L1_ffn_wv"].T)
    t["gqa_norm"] = x["L1_ffn_attn_norm_w"].reshape(KD, P).T
    t["top2_norm"] = x["L1_ffn_ffn_norm_w"].reshape(KD, P).T
    t["top2_wg"] = matrix(x["L1_ffn_gate_w"].T)
    t["top2_w"] = x["L1_ffn_expert_w"].transpose(2, 0, 1).reshape(KD, P, E * D).transpose(1, 0, 2)
    for n in "qkvo":
        t[f"diff_w{n}"] = matrix(x[f"L3_attn_W{n}"].T)
    for n in ("q1", "k1", "q2", "k2"):
        t[f"diff_lambda_{n}"] = x[f"L3_attn_lambda_{n}"]
    t["diff_subln"] = x["L3_attn_subln_w"]
    t["xmoe_wg"] = matrix(x["L3_ffn_gate_w"].T)
    t["xmoe_w1"] = matrices(x["L3_ffn_w1"].transpose(0, 2, 1))
    t["xmoe_w2"] = matrices(x["L3_ffn_w2"].transpose(0, 2, 1))
    for n, m in zip("qfvo", "qfio"):
        t[f"gla_w{n}"] = matrix(x[f"L2_attn_W{m}"])
    for n in ("gate", "up", "down"):
        t[f"bit_{n}"] = matrix(x[f"L2_ffn_w_{n}"].T)
    return {n: np.ascontiguousarray(v) for n, v in t.items()}


def build_program(nc, a, out):
    with ExitStack() as stack:
        c = Core(nc, stack)
        constants(c)
        for phase in (tokens, random_feature_attention, top1_experts, scaled_attention, grouped_block,
                      gated_linear_attention, ternary_network, differential_attention, capacity_experts):
            phase(c, a)
            c.end_of_phase()
        store(c, out)


def kernel(**inputs):
    import concourse.bacc as bacc
    from concourse.bass_utils import run_bass_kernel_spmd

    arrays = {f"in_{n}": v for n, v in layouts({n: np.asarray(v) for n, v in inputs.items()}).items()}
    nc = bacc.Bacc("TRN2", target_bir_lowering=False, num_devices=1)
    a = {n[3:]: nc.dram_tensor(n, v.shape, mybir.dt.from_np(v.dtype), kind="ExternalInput").ap()
         for n, v in arrays.items()}
    out = nc.dram_tensor("out", (B, T, D), F32, kind="ExternalOutput").ap()
    build_program(nc, a, out)
    result = run_bass_kernel_spmd(nc, [arrays], core_ids=[0])
    return result.results[0]["out"]
```

```python
import math
from contextlib import ExitStack

import numpy as np

import concourse.bass as bass
from concourse import mybir

F32 = mybir.dt.float32
F32R = mybir.dt.float32r
BF16 = mybir.dt.bfloat16
I32 = mybir.dt.int32
ALU = mybir.AluOpType
ACT = mybir.ActivationFunctionType
AX = mybir.AxisListType

P = 128
NI = 96
PATCH = 16
NPATCH = (NI // PATCH) ** 2
CLS = 1 + NPATCH
NTXT = 77
T = CLS + NTXT
B = 32
D = 256
KD = D // P
G = 4
NG = B // G
N = G * T
H = 16
DH = D // H
E = 8
FF = 1024
KT = 3 * PATCH * PATCH // P
BANK = 512
ROUND = 1.5 * 2.0 ** 23


def flat(ap):
    return ap.rearrange("p a b -> p (a b)")


class Link:

    def __init__(self, eng, sem, i=0, per=0):
        self.eng, self.sem, self.base, self.per, self.n = eng, sem, i * per, per, 0

    def after(self, ins):
        ins.then_inc(self.sem, 1)
        self.n += 1
        self.eng.wait_ge(self.sem, self.base + self.n)

    def end(self):
        assert self.per in (0, self.n), (self.per, self.n)


class Core:

    def __init__(self, nc, stack):
        self.nc, self.in_use = nc, []
        self.resid = self.sb(stack, "resid", [P, B, D])
        self.moments = self.sb(stack, "moments", [P, B, 2])
        self.rstd = self.sb(stack, "rstd", [P, B])
        self.ident = self.sb(stack, "ident", [P, P])
        self.ones = self.sb(stack, "ones", [P, P])

    def sb(self, stack, name, shape, dt=F32):
        return stack.enter_context(self.nc.sbuf_tensor(name, shape, dt))

    def banks(self, stack, name, n, dt=F32):
        return stack.enter_context(self.nc.psum_tensor(name, [P, n, BANK], dt))

    def sems(self, names, phase):
        made = [self.nc.alloc_semaphore(f"{phase}_{n}") for n in names.split()]
        self.in_use += made
        return made

    def end_of_phase(self):
        self.nc.clear_and_free_semaphores(self.in_use)
        self.in_use = []
        self.nc.all_engine_barrier()

    def tile(self, b):
        return flat(self.resid[:T, bass.ds(b, 1), :])

    def mean(self, b):
        return flat(self.moments[:T, bass.ds(b, 1), 0:1])

    def scale(self, b):
        return self.rstd[:T, bass.ds(b, 1)]


def row(ap, parts):
    return bass.AP(ap.tensor, ap.offset, [[0, parts]] + [list(x) for x in ap.ap])


def stats(eng, link, six, tiles):
    eng.memset(six[0:1, 0, 8:9], 0.0)
    for n, (src, _) in enumerate(tiles):
        last = eng.bn_stats(six[:T, n, 0:6], src)
    link.after(last)
    eng.memset(six[0:1, 0, 8:9], 0.0)
    for n in range(len(tiles)):
        last = eng.bn_aggr(six[:T, n, 6:8], six[:T, n, 0:6])
    link.after(last)
    eng.memset(six[0:1, 0, 8:9], 0.0)
    for n, (_, dst) in enumerate(tiles):
        last = eng.tensor_copy(dst, six[:T, n, 6:8])
    return last


def constants(c):
    (zero, made) = c.sems("zero made", "const")
    with c.nc.Block() as block:
        @block.vector
        def _(dve):
            dve.memset(c.ones[:], 1.0)

        @block.gpsimd
        def _(pool):
            pool.memset(c.ident[:], 0.0).then_inc(zero, 1)
            pool.wait_ge(zero, 1)
            pool.affine_select(out=c.ident[:], in_=c.ident[:], compare_op=ALU.not_equal, fill=1.0,
                               base=0, pattern=[[-1, P]], channel_multiplier=1).then_inc(made, 1)
            pool.wait_ge(made, 1)


def inverse_deviation(c, eps, ph):
    added, rooted, inverted = c.sems("added rooted inverted", ph + "_rstd")
    with c.nc.Block() as block:
        @block.vector
        def _(dve):
            dve.tensor_scalar(c.rstd[:T, :], c.moments[:T, :, 1], eps, None, ALU.add).then_inc(added, 1)
            dve.wait_ge(rooted, 1)
            dve.reciprocal(c.rstd[:T, :], c.rstd[:T, :]).then_inc(inverted, 1)
            dve.wait_ge(inverted, 1)

        @block.scalar
        def _(act):
            act.wait_ge(added, 1)
            act.activation(c.rstd[:T, :], c.rstd[:T, :], ACT.Sqrt).then_inc(rooted, 1)


def tokens(c, a):
    nc = c.nc
    with ExitStack() as st:
        patches = c.sb(st, "patches", [P, 2, KT, G, CLS])
        weight = c.sb(st, "tok_w", [P, KT, D])
        base = c.sb(st, "tok_base", [P, D])
        first = c.sb(st, "tok_first", [P, D])
        six = c.sb(st, "tok_six", [P, G, 9])
        acc = c.banks(st, "tok_acc", 4)
        (text_in, fixed_in, cls_in, patch_in0, patch_in1, summed, based, acc_free, link_s) = c.sems(
            "text_in fixed_in cls_in patch_in0 patch_in1 summed based acc_free link", "tok")
        patch_in = (patch_in0, patch_in1)
        with nc.Block() as block:
            @block.sync
            def _(sp):
                sp.dma_start(weight[:], a["tok_w"]).then_inc(fixed_in, 16)
                sp.dma_start(base[:CLS, :], a["tok_pos"]).then_inc(fixed_in, 16)
                sp.dma_start(first[:CLS, :], row(a["tok_b"], CLS)).then_inc(fixed_in, 16)
                sp.wait_ge(fixed_in, 48)
                sp.dma_start(first[0:1, :], a["tok_cls"]).then_inc(cls_in, 16)
                with sp.Fori(0, NG // 2) as i:
                    for u in range(2):
                        sp.wait_ge(summed, 2 * i + u + 1)
                        sp.dma_start(patches[:, u], a["patches"][bass.ds(2 * i + u, 1)].rearrange(
                            "a p k g c -> p (a k) g c")).then_inc(patch_in[u], 16)

            @block.scalar
            def _(act):
                act.dma_start(c.resid[CLS:T, :, :], a["txt"]).then_inc(text_in, 16)

            @block.tensor
            def _(pe):
                pe.sem_inc(summed, 2)
                pe.wait_ge(cls_in, 16)
                with pe.Fori(0, NG // 2) as i:
                    for u in range(2):
                        pe.wait_ge(patch_in[u], 16 * (i + 1))
                        pe.wait_ge(acc_free, 2 * i + u + 1)
                        for j in range(G):
                            for k in range(KT):
                                last = pe.matmul(acc[:CLS, 2 * u + j // 2, j % 2 * D:(j % 2 + 1) * D],
                                                 patches[:, u, k, j, :], weight[:, k, :],
                                                 start=k == 0, stop=k == KT - 1)
                        last.then_inc(summed, 1)

            @block.vector
            def _(dve):
                dve.sem_inc(acc_free, 2)
                dve.wait_ge(cls_in, 16)
                dve.tensor_tensor(base[:CLS, :], base[:CLS, :], first[:CLS, :], ALU.add).then_inc(based, 1)
                dve.wait_ge(based, 1)
                dve.wait_ge(text_in, 16)
                with dve.Fori(0, NG // 2) as i:
                    link = Link(dve, link_s, i, 6)
                    for u in range(2):
                        dve.wait_ge(summed, 2 * i + u + 3)
                        for j in range(G):
                            last = dve.tensor_tensor(
                                flat(c.resid[:CLS, bass.ds(8 * i + 4 * u + j, 1), :]),
                                acc[:CLS, 2 * u + j // 2, j % 2 * D:(j % 2 + 1) * D], base[:CLS, :], ALU.add)
                        link.after(last)
                        last = stats(dve, link, six, [
                            (c.tile(8 * i + 4 * u + j), flat(c.moments[:T, bass.ds(8 * i + 4 * u + j, 1), :]))
                            for j in range(G)])
                        last.then_inc(acc_free, 1)
                        dve.wait_ge(acc_free, 2 * i + u + 3)
                    link.end()


def store(c, out):
    (stored,) = c.sems("stored", "out")
    with c.nc.Block() as block:
        @block.sync
        def _(sp):
            sp.dma_start(out.rearrange("b t d -> t b d"), c.resid[:T, :, :]).then_inc(stored, 16)
            sp.wait_ge(stored, 16)



def normalize(dve, c, z, g, scale=None):
    for j in range(G):
        b = G * g + j
        last = dve.tensor_scalar(z[:T, j, :], c.tile(b), c.mean(b),
                                 c.scale(b) if scale is None else scale[:T, bass.ds(b, 1)],
                                 ALU.subtract, ALU.mult)
    return last


def to_features(pe, c, out, x):
    for k in range(KD):
        for j in range(G):
            last = pe.transpose(out[:, k, j * T:(j + 1) * T], x[:T, j, k * P:(k + 1) * P], c.ident[:T, :T])
    return last


def feature_product(pe, out, weight, xt):
    for m in range(KD):
        for k in range(KD):
            last = pe.matmul(out[:, m, :N], weight[:, k, m * P:(m + 1) * P], xt[:, k, :],
                             start=k == 0, stop=k == KD - 1)
    return last


PARTS = ((0, 0), (0, 1), (1, 0))


def whole(x):
    return x.bitcast(F32)


def token_product(pe, out, xt, weight, bias=None, ones=None):
    for j in range(G):
        dst = out[:T, j // 2, j % 2 * D:(j % 2 + 1) * D]
        for k in range(KD):
            last = pe.matmul(dst, xt[:, k, j * T:(j + 1) * T], weight[:, k, :],
                             start=k == 0, stop=k == KD - 1 and bias is None)
        if bias is not None:
            last = pe.matmul(dst, ones[0:1, :T], bias[0:1, :], start=False, stop=True)
    return last


def add_to_residual(dve, c, y, g):
    for j in range(G):
        b = G * g + j
        last = dve.tensor_tensor(c.tile(b), y[:T, j // 2, j % 2 * D:(j % 2 + 1) * D], c.tile(b), ALU.add)
    return last


def tile_stats(dve, c, link, six, g):
    return stats(dve, link, six, [(c.tile(G * g + j), flat(c.moments[:T, bass.ds(G * g + j, 1), :]))
                                  for j in range(G)])


NEXT = ("z0", "z1", "q0", "q1", "k0", "k1", "v0", "v1")
LAST = ("o0", "o1", "y0", "y1")
ORDER = ("z0", "z1", "q0", "q1", "k0", "k1", "o0", "o1", "v0", "v1", "y0", "y1")


def steps(part):
    return [x for x in ORDER if not (part == "first" and x in LAST or part == "last" and x in NEXT)]


def first_step(g, part):
    return len(NEXT) if part == "first" else len(ORDER) * g + 4


BEFORE_LAST = first_step(NG - 1, "last") + len(LAST)
SPLIT = ("q0", "q1", "k0", "k1")
SPREAD = 5


def spread(count):
    if count >= NEXT.index("v0"):
        return NEXT.index("v0")
    return max(0 if count < 2 else 2, count - SPREAD + 1)


RFF = 128
TAU_1 = 6.28125
TAU_2 = float(np.float32(round((2 * math.pi - TAU_1) * 2.0 ** 22) / 2.0 ** 22))
TAU_3 = 2 * math.pi - TAU_1 - TAU_2
TAU_IN = 2 * math.pi * (1 - 2.0 ** -22)


def random_feature_attention(c, a):
    nc = c.nc
    inverse_deviation(c, 1e-5, "rff")
    with ExitStack() as st:
        wq, wk, wv, wp = (c.sb(st, f"rff_w{n}", [P, KD, D]) for n in "qkvp")
        wr = c.sb(st, "rff_wr", [P, H, RFF])
        br = c.sb(st, "rff_br", [P, H])
        brs = c.sb(st, "rff_brs", [P, H])
        turns = c.sb(st, "rff_turns", [P, H])
        bp = c.sb(st, "rff_bp", [1, D])
        quarter = c.sb(st, "rff_quarter", [P, 1])
        z = c.sb(st, "rff_z", [P, G, D])
        zt = c.sb(st, "rff_zt", [P, KD, N])
        wrs = [c.sb(st, f"rff_wr{n}", [P, H, RFF], F32R) for n in range(2)]
        qk = c.sb(st, "rff_qk", [P, 2 * KD, N])
        qt, kt = ([c.sb(st, f"rff_{x}t{n}", [P, 2, KD, N], F32R) for n in range(2)] for x in "qk")
        v1 = c.sb(st, "rff_v1", [P, 2, G, H, DH + 1])
        rounded = c.sb(st, "rff_rounded", [P, 2, 2, N])
        less = c.sb(st, "rff_less", [P, 4, 2, N])
        size = c.sb(st, "rff_size", [P, 2, 2, N])
        sines = c.sb(st, "rff_sines", [P, 2, 2, N])
        cosines = c.sb(st, "rff_cosines", [P, 2, 2, N])
        pair = c.sb(st, "rff_pair", [P, 2, N])
        mixed = c.sb(st, "rff_mixed", [P, H, G, DH + 1])
        inverse = c.sb(st, "rff_inverse", [P, H, G])
        o = c.sb(st, "rff_o", [P, 2, G, D])
        ot = c.sb(st, "rff_ot", [P, KD, N])
        six = c.sb(st, "rff_six", [P, G, 9])
        pg = c.banks(st, "rff_pg", 1)
        steps_bank = c.banks(st, "rff_px", 1)
        pp = c.banks(st, "rff_pp", 4)
        pa = c.banks(st, "rff_pa", 2)
        (w_in, wr_in, cleared, fixed, high_made, qk_split, prep_s, z_ready, step_sum, step_done, angle_sum, less_ready,
         size_ready, waves_ready, pair_sum, pair_ready, mix_sum, mix_ready, o_ready, link_first, link_pairs,
         link_last) = c.sems(
            "w_in wr_in cleared fixed high_made qk_split prep z_ready step_sum step_done angle_sum less_ready "
            "size_ready waves_ready pair_sum pair_ready mix_sum mix_ready o_ready link_first link_pairs "
            "link_last", "rff")

        def bank_of(count):
            n = count % SPREAD
            return steps_bank if n == SPREAD - 1 else pp[:, n:n + 1]

        def carried(part, h):
            if h < len(ORDER) and ORDER[h] in steps(part):
                return [(ORDER[h], steps(part).index(ORDER[h]))]
            return []

        with nc.Block() as block:
            @block.sync
            def _(sp):
                for w, name in ((wq, "rff_wq"), (wk, "rff_wk"), (wv, "rff_wv"), (wp, "rff_wp"),
                                (br, "rff_br"), (bp, "rff_bp")):
                    sp.dma_start(w[:], a[name]).then_inc(w_in, 16)
                sp.wait_ge(cleared, 1)
                for s in range(P // DH):
                    sp.dma_start(wr[DH * s:DH * (s + 1), s:H:P // DH, :], a["rff_wr"][:, s:H:P // DH, :])\
                      .then_inc(wr_in, 16)

            @block.gpsimd
            def _(pool):
                pool.memset(wr[:], 0.0).then_inc(cleared, 1)
                pool.sem_inc(qk_split, 1)

                def split(g, q, x):
                    n = SPLIT.index(x)
                    high, low = (part[:, q, n % KD, :] for part in (qt if x[0] == "q" else kt))
                    pool.wait_ge(high_made, len(SPLIT) * g + n + 1)
                    pool.tensor_tensor(low, qk[:, n, :], whole(high), ALU.subtract).then_inc(qk_split, 1)

                def group(g, q):
                    for x in SPLIT:
                        split(g, q, x)

                group(0, 0)
                group(1, 1)
                with pool.Fori(0, NG // 2 - 1) as i:
                    for u in range(2):
                        group(2 * i + 2 + u, u)

            @block.tensor
            def _(pe):
                pe.sem_inc(pair_sum, 2)
                pe.sem_inc(mix_sum, 2)

                def step(x, g, q, count, alone=False):
                    if not alone:
                        pe.wait_ge(step_done, count)
                    elif spread(count):
                        pe.wait_ge(step_done, spread(count))
                    px = bank_of(count) if alone else steps_bank
                    k = int(x[1])
                    if x == "z0":
                        pe.wait_ge(z_ready, g + 1)
                    if x == "o0":
                        pe.wait_ge(o_ready, g + 1)
                    if x[0] in "zo":
                        src = z if x[0] == "z" else o[:, q]
                        for j in range(G):
                            last = pe.transpose(px[:, 0, j * T:(j + 1) * T], src[:T, j, k * P:(k + 1) * P],
                                                c.ident[:T, :T])
                    elif x[0] in "qk":
                        w = wq if x[0] == "q" else wk
                        for m in range(KD):
                            last = pe.matmul(px[:, 0, :N], w[:, m, k * P:(k + 1) * P], zt[:, m, :],
                                             start=m == 0, stop=m == KD - 1)
                    else:
                        src, w = (zt, wv) if x[0] == "v" else (ot, wp)
                        for j in (2 * k, 2 * k + 1):
                            dst = px[:T, 0, j % 2 * D:(j % 2 + 1) * D]
                            for m in range(KD):
                                last = pe.matmul(dst, src[:, m, j * T:(j + 1) * T], w[:, m, :],
                                                 start=m == 0, stop=m == KD - 1 and x[0] == "v")
                            if x[0] == "y":
                                last = pe.matmul(dst, c.ones[0:1, :T], bp[0:1, :], start=False, stop=True)
                    last.then_inc(step_sum, 1)

                def angles(g, parity, h):
                    r = H * g + h
                    if not (isinstance(g, int) and r < 2):
                        pe.wait_ge(less_ready, r - 1)
                    if h == 0:
                        pe.wait_ge(qk_split, len(SPLIT) * (g + 1) + 1)
                    for s, src in enumerate((qt, kt)):
                        for v, y in PARTS:
                            last = pe.matmul(pp[:, 2 * (h % 2) + s, :N], wrs[v][:, h, :], src[y][:, parity, h // 8, :],
                                             start=(v, y) == PARTS[0], stop=(v, y) == PARTS[-1])
                    last.then_inc(angle_sum, 1)

                def pairs(r, h):
                    pe.wait_ge(waves_ready, r + 5)
                    pe.wait_ge(pair_ready, r + 1)
                    for j in range(G):
                        t = slice(j * T, (j + 1) * T)
                        for n, waves in enumerate((cosines, sines)):
                            last = pe.matmul(pa[:T, h % 2, t], waves[:, h % 2, 1, t], waves[:, h % 2, 0, t],
                                             start=n == 0, stop=n == 1)
                    last.then_inc(pair_sum, 1)

                def mix(g, parity, h):
                    pe.wait_ge(pair_ready, H * g + h + 3)
                    if h % 4 == 0:
                        pe.wait_ge(mix_ready, 4 * g + h // 4 + 1)
                    for j in range(G):
                        at = (DH + 1) * (G * (h % 4) + j)
                        last = pe.matmul(pg[:T, 0, at:at + DH + 1], pair[:T, h % 2, j * T:(j + 1) * T],
                                         v1[:T, parity, j, h, :], start=True, stop=True)
                    last.then_inc(mix_sum, 1)

                def group(g, q, part):
                    pe.wait_ge(step_done, first_step(g, part))
                    for h in range(H):
                        if h + 2 < H:
                            angles(g, q, h + 2)
                        elif part != "last":
                            angles(g + 1, 1 - q, h + 2 - H)
                        pairs(H * g + h, h)
                        if h >= 2:
                            mix(g, q, h - 2)
                        elif part != "first":
                            mix(g - 1, 1 - q, H - 2 + h)
                        for x, count in carried(part, h):
                            step(x, g - 1 if x in LAST else g + 1, 1 - q, first_step(g, part) + count)

                for count, x in enumerate(NEXT):
                    if x == "q0":
                        pe.wait_ge(w_in, 96)
                    step(x, 0, 0, count, alone=True)
                pe.wait_ge(fixed, 1)
                pe.wait_ge(step_done, len(NEXT))
                angles(0, 0, 0)
                angles(0, 0, 1)
                group(0, 0, "first")
                with pe.Fori(0, NG // 2 - 1) as i:
                    for u in range(2):
                        group(2 * i + 1 + u, (1 + u) % 2, "pairs")
                group(NG - 1, 1, "last")
                for h in (H - 2, H - 1):
                    mix(NG - 1, 1, h)
                for count, x in enumerate(LAST):
                    step(x, NG - 1, 1, BEFORE_LAST + count)

            @block.scalar
            def _(act):
                act.sem_inc(waves_ready, 4)

                def read(x, g, q, count, px=steps_bank):
                    if x[0] not in "zqko":
                        return
                    k = int(x[1])
                    act.wait_ge(step_sum, count + 1)
                    if x not in SPLIT:
                        act.activation((zt if x[0] == "z" else ot)[:, k, :], px[:, 0, :N], ACT.Copy)\
                           .then_inc(step_done, 1)
                        return
                    m = SPLIT.index(x)
                    act.wait_ge(qk_split, len(SPLIT) * g + 1)
                    act.activation(qk[:, m, :], px[:, 0, :N], ACT.Copy).then_inc(step_done, 1)
                    act.wait_ge(step_done, count + 1)
                    act.activation((qt if x[0] == "q" else kt)[0][:, q, k, :], qk[:, m, :],
                                   ACT.Copy).then_inc(high_made, 1)

                def group(g, q, part):
                    for h in range(H):
                        r = H * g + h
                        act.wait_ge(less_ready, r + 1)
                        act.activation(size[:, h % 2], less[:, h % 4], ACT.Abs, bias=br[:, h:h + 1],
                                       scale=-1.0).then_inc(size_ready, 1)
                        act.wait_ge(pair_sum, r + 1)
                        act.activation(sines[:, h % 2], less[:, h % 4], ACT.Sin, bias=brs[:, h:h + 1],
                                       scale=-TAU_IN)
                        act.wait_ge(size_ready, r + 1)
                        act.activation(cosines[:, h % 2], size[:, h % 2], ACT.Sin, bias=quarter[:, 0:1],
                                       scale=-TAU_IN).then_inc(waves_ready, 1)
                        if h:
                            for x, count in carried(part, h - 1):
                                read(x, g - 1 if x in LAST else g + 1, 1 - q, first_step(g, part) + count)

                for count, x in enumerate(NEXT):
                    read(x, 0, 0, count, bank_of(count))
                act.wait_ge(fixed, 1)
                group(0, 0, "first")
                with act.Fori(0, NG // 2 - 1) as i:
                    for u in range(2):
                        group(2 * i + 1 + u, (1 + u) % 2, "pairs")
                group(NG - 1, 1, "last")
                for count, x in enumerate(LAST):
                    read(x, NG - 1, 1, BEFORE_LAST + count)

            @block.vector
            def _(dve):
                normalize(dve, c, z, 0).then_inc(z_ready, 1)
                dve.memset(v1[:, :, :, :, DH:DH + 1], 1.0)
                dve.memset(quarter[:], math.pi / 2)
                prep = Link(dve, prep_s)
                dve.wait_ge(w_in, 96)
                prep.after(dve.tensor_scalar(turns[:], br[:], 1 / (2 * math.pi), ROUND, ALU.mult, ALU.add))
                prep.after(dve.tensor_scalar(turns[:], turns[:], ROUND, None, ALU.subtract))
                for part in (TAU_1, TAU_2, TAU_3):
                    prep.after(dve.scalar_tensor_tensor(br[:], turns[:], -part, br[:], ALU.mult, ALU.add))
                prep.after(dve.tensor_scalar(br[:], br[:], 1 / (2 * math.pi), None, ALU.mult))
                dve.tensor_scalar(brs[:], br[:], TAU_IN, None, ALU.mult)
                dve.wait_ge(wr_in, 16 * (P // DH))
                prep.after(dve.tensor_scalar(wr[:], wr[:], 1 / (2 * math.pi), None, ALU.mult))
                prep.after(dve.tensor_scalar(wrs[0][:], wr[:], 1.0, None, ALU.mult))
                dve.tensor_tensor(wrs[1][:], wr[:], whole(wrs[0][:]), ALU.subtract).then_inc(fixed, 1)
                dve.sem_inc(pair_ready, 2)
                dve.sem_inc(mix_ready, 1)

                def read(link, x, g, parity, count, px=steps_bank):
                    if x[0] not in "vy":
                        return
                    k = int(x[1])
                    pair_of = (2 * k, 2 * k + 1)
                    dve.wait_ge(step_sum, count + 1)
                    if x[0] == "v":
                        dve.tensor_copy(v1[:T, parity, 2 * k:2 * k + 2, :, 0:DH],
                                        px[:T, 0, :].rearrange("p (j h d) -> p j h d", j=2, h=H))\
                           .then_inc(step_done, 1)
                        return
                    for j in pair_of:
                        last = dve.tensor_tensor(c.tile(G * g + j), px[:T, 0, j % 2 * D:(j % 2 + 1) * D],
                                                 c.tile(G * g + j), ALU.add)
                    last.then_inc(step_done, 1)
                    dve.wait_ge(step_done, count + 1)
                    if k == 1:
                        link.after(tile_stats(dve, c, link, six, g))

                def keep_pair(r, h):
                    dve.wait_ge(pair_sum, r + 3)
                    dve.wait_ge(mix_sum, r + 1)
                    dve.tensor_copy(pair[:T, h % 2, :], pa[:T, h % 2, :N]).then_inc(pair_ready, 1)

                def keep_mix(g, q):
                    dve.wait_ge(mix_sum, H * g + 4 * q + 3 + 3)
                    dve.tensor_copy(mixed[:T, 4 * q:4 * q + 4].rearrange("p h j d -> p (h j d)"),
                                    pg[:T, 0, :4 * G * (DH + 1)]).then_inc(mix_ready, 1)

                def divide(link, g, parity):
                    dve.wait_ge(mix_ready, 4 * g + 5)
                    link.after(dve.tensor_scalar(inverse[:T], mixed[:T, :, :, DH], 1e-6 * RFF, None, ALU.add))
                    link.after(dve.reciprocal(inverse[:T], inverse[:T]))
                    dve.tensor_tensor(o[:T, parity].rearrange("p j (h d) -> p h j d", h=H), mixed[:T, :, :, 0:DH],
                                      inverse[:T].unsqueeze(3).to_broadcast([T, H, G, DH]), ALU.mult)\
                       .then_inc(o_ready, 1)

                def group(link, g, q, part):
                    if part != "last":
                        normalize(dve, c, z, g + 1).then_inc(z_ready, 1)
                    for h in range(H):
                        r = H * g + h
                        angle = pp[:, 2 * (h % 2):2 * (h % 2) + 2, :N]
                        dve.wait_ge(angle_sum, r + 1)
                        dve.wait_ge(waves_ready, r + 1)
                        link.after(dve.tensor_scalar(rounded[:, h % 2], angle, br[:, h:h + 1], ROUND,
                                                     ALU.add, ALU.add))
                        dve.scalar_tensor_tensor(less[:, h % 4], rounded[:, h % 2], ROUND, angle,
                                                 ALU.subtract, ALU.subtract).then_inc(less_ready, 1)
                        if h >= 2:
                            keep_pair(r - 2, h - 2)
                        elif part != "first":
                            keep_pair(r - 2, H - 2 + h)
                        if h % 4 == 2 and h >= 6:
                            keep_mix(g, h // 4 - 1)
                        if h >= 1:
                            for x, count in carried(part, h - 1):
                                read(link, x, g - 1 if x in LAST else g + 1, 1 - q, first_step(g, part) + count)
                        if h == 2 and part != "first":
                            keep_mix(g - 1, H // 4 - 1)
                            divide(link, g - 1, 1 - q)

                link = Link(dve, link_first)
                for count, x in enumerate(NEXT):
                    read(link, x, 0, 0, count, bank_of(count))
                group(link, 0, 0, "first")
                with dve.Fori(0, NG // 2 - 1) as i:
                    link = Link(dve, link_pairs, i, 2 * (H + 2 + 3))
                    for u in range(2):
                        group(link, 2 * i + 1 + u, (1 + u) % 2, "pairs")
                    link.end()
                link = Link(dve, link_last)
                group(link, NG - 1, 1, "last")
                for h in (H - 2, H - 1):
                    keep_pair(H * (NG - 1) + h, h)
                keep_mix(NG - 1, H // 4 - 1)
                divide(link, NG - 1, 1)
                for count, x in enumerate(LAST):
                    read(link, x, NG - 1, 1, BEFORE_LAST + count)


class Routing:

    def __init__(self, c, st, ph, rows=False):
        self.ph, self.rows = ph, rows
        if rows:
            self.z = c.sb(st, ph + "_zr", [P, B, D])
        else:
            self.zt = [c.sb(st, f"{ph}_zt{n}", [P, KD, B * T], F32R) for n in range(2)]
        self.share = c.sb(st, ph + "_share", [P, B, E])


def gather_tokens(c, r, z_of, w_gate, gate_biases, w_norm, a, ahead=None):
    nc = c.nc
    with ExitStack() as st:
        wg = c.sb(st, r.ph + "_wg", [P, KD, E])
        extra = c.sb(st, r.ph + "_extra", [P, 2, E])
        norm = c.sb(st, r.ph + "_norm", [P, KD])
        z = c.sb(st, r.ph + "_z", [P, 2, G, D])
        zt = c.sb(st, r.ph + "_zt", [P, 2, KD, N])
        pt = c.banks(st, r.ph + "_pt", 4)
        pl = c.banks(st, r.ph + "_pl", 2)
        (w_in, z_ready, zt_sum, zt_ready, high_made, copied, logits_sum, logits_ready) = c.sems(
            "w_in z_ready zt_sum zt_ready high_made copied logits_sum logits_ready", r.ph + "_gather")
        (ahead_in,) = c.sems("ahead_in", r.ph + "_ahead")
        names = [w_gate] + list(gate_biases) + ([w_norm] if w_norm else [])

        with nc.Block() as block:
            @block.sync
            def _(sp):
                sp.dma_start(wg[:], a[w_gate]).then_inc(w_in, 16)
                for n, name in enumerate(gate_biases):
                    sp.dma_start(extra[:T, n, :], row(a[name], T)).then_inc(w_in, 16)
                if w_norm:
                    sp.dma_start(norm[:], a[w_norm]).then_inc(w_in, 16)
                if ahead:
                    sp.dma_start(ahead[0][:], a[ahead[1]]).then_inc(ahead_in, 16)
                    sp.wait_ge(ahead_in, 16)

            @block.tensor
            def _(pe):
                pe.sem_inc(zt_sum, 2)
                pe.sem_inc(logits_sum, 2)
                pe.wait_ge(w_in, 16 * len(names))
                with pe.Fori(0, NG // 2) as i:
                    for u in range(2):
                        n = 2 * i + u
                        pe.wait_ge(z_ready, n + 1)
                        pe.wait_ge(zt_ready, n + 1)
                        to_features(pe, c, pt[:, 2 * u:2 * u + 2], z[:, u]).then_inc(zt_sum, 1)
                    for u in range(2):
                        n = 2 * i + u
                        pe.wait_ge(zt_ready, n + 3)
                        pe.wait_ge(logits_ready, n + 1)
                        for j in range(G):
                            for k in range(KD):
                                last = pe.matmul(pl[:T, u, j * E:(j + 1) * E], zt[:, u, k, j * T:(j + 1) * T],
                                                 wg[:, k, :], start=k == 0, stop=k == KD - 1)
                        last.then_inc(logits_sum, 1)

            @block.scalar
            def _(act):
                act.sem_inc(zt_ready, 2)
                act.wait_ge(w_in, 16 * len(names))
                with act.Fori(0, NG // 2) as i:
                    for u in range(2):
                        n = 2 * i + u
                        act.wait_ge(zt_sum, n + 3)
                        act.wait_ge(logits_sum, n + 1)
                        if not r.rows:
                            act.wait_ge(copied, n + 1)
                        for k in range(KD):
                            last = act.activation(zt[:, u, k, :], pt[:, 2 * u + k, :N], ACT.Copy,
                                                  scale=norm[:, k:k + 1] if w_norm else 1.0)
                        last.then_inc(zt_ready, 1)

            @block.gpsimd
            def _(pool):
                pool.sem_inc(copied, 2)
                with pool.Fori(0, NG // 2) as i:
                    for u in range(2):
                        n = 2 * i + u
                        if r.rows:
                            pool.wait_ge(z_ready, n + 1)
                            pool.tensor_copy(r.z[:T, bass.ds(G * n, G), :], z[:T, u]).then_inc(copied, 1)
                        else:
                            high, low = (x[:, :, bass.ds(N * n, N)] for x in r.zt)
                            pool.wait_ge(high_made, n + 1)
                            pool.tensor_tensor(low, zt[:, u], whole(high), ALU.subtract).then_inc(copied, 1)

            @block.vector
            def _(dve):
                dve.sem_inc(logits_ready, 2)

                def logits(n, u):
                    if not r.rows:
                        dve.wait_ge(zt_ready, n + 3)
                        dve.tensor_scalar(r.zt[0][:, :, bass.ds(N * n, N)], zt[:, u], 1.0, None,
                                          ALU.mult).then_inc(high_made, 1)
                    dve.wait_ge(logits_sum, n + 3)
                    dst = r.share[:T, bass.ds(G * n, G), :]
                    src = pl[:T, u, :G * E].rearrange("p (j e) -> p j e", j=G)
                    bias = [extra[:T, m:m + 1, :].to_broadcast([T, G, E]) for m in range(len(gate_biases))]
                    if bias:
                        dve.tensor_tensor(dst, src, bias[0], ALU.add).then_inc(logits_ready, 1)
                        dve.wait_ge(logits_ready, n + 3)
                        for m in bias[1:]:
                            dve.tensor_tensor(dst, dst, m, ALU.add)
                    else:
                        dve.tensor_scalar(dst, src, 0.0, None, ALU.add).then_inc(logits_ready, 1)

                def normalize_pair(first):
                    for u in range(2):
                        dve.wait_ge(zt_sum, first + u + 1)
                        if r.rows:
                            dve.wait_ge(copied, first + u + 1)
                        z_of(dve, z[:, u], first + u).then_inc(z_ready, 1)

                normalize_pair(0)
                dve.wait_ge(w_in, 16 * len(names))
                with dve.Fori(0, NG // 2 - 1) as i:
                    normalize_pair(2 * i + 2)
                    for u in range(2):
                        logits(2 * i + u, u)
                for u in range(2):
                    logits(NG - 2 + u, u)


def ranks(dve, link, r, above, tie, before, rank):
    mine = r.share[:T].unsqueeze(3).to_broadcast([T, B, E, E])
    other = r.share[:T].unsqueeze(2).to_broadcast([T, B, E, E])
    dve.tensor_tensor(above[:T], other, mine, ALU.is_gt)
    link.after(dve.tensor_tensor(tie[:T], other, mine, ALU.is_equal))
    link.after(dve.tensor_tensor(tie[:T], tie[:T],
                                 before[:T].unsqueeze(1).to_broadcast([T, B, E, E]), ALU.mult))
    link.after(dve.tensor_tensor(above[:T], above[:T], tie[:T], ALU.add))
    link.after(dve.tensor_reduce(rank[:T], above[:T], AX.X, ALU.add))


def lower_index(pool, made, before):
    pool.memset(before[:], 1.0).then_inc(made, 1)
    pool.wait_ge(made, 1)
    pool.affine_select(out=before[:], in_=before[:], compare_op=ALU.is_gt, fill=0.0, base=0,
                       pattern=[[1, E], [-1, E]], channel_multiplier=0).then_inc(made, 1)


S = 256
NS = S // P
NB = (B * T + E * (S - 1)) // S
SMALLEST = 0.5 - 0.5 / S


class Dispatch:

    def __init__(self, c, st, ph):
        self.slot = c.sb(st, ph + "_slot", [P, B], I32)
        self.expert = c.sb(st, ph + "_expert", [1, NB], I32)
        self.x = c.nc.dram_tensor(ph + "_xd", (NB * S, D), F32, kind="Internal").ap()
        self.y = c.nc.dram_tensor(ph + "_yd", (NB * S, D), F32, kind="Internal").ap()


def route_first(c, r, d):
    with ExitStack() as st:
        above, tie = (c.sb(st, f"first_{n}", [P, B, E, E]) for n in ("above", "tie"))
        rank, chosen, place = (c.sb(st, f"first_{n}", [P, B, E]) for n in ("rank", "chosen", "place"))
        runs, totals, places = (c.sb(st, f"first_{n}", [P, E, B]) for n in ("runs", "totals", "places"))
        before = c.sb(st, "first_before", [P, E, E])
        earlier = c.sb(st, "first_earlier", [P, P])
        blocks, start, end, total = (c.sb(st, f"first_{n}", [P, E]) for n in ("blocks", "start", "end", "total"))
        number = c.sb(st, "first_number", [1, NB], I32)
        block_of = c.sb(st, "first_block_of", [1, NB])
        passed = c.sb(st, "first_passed", [1, NB, E])
        slot = c.sb(st, "first_slot", [P, B])
        zero = c.sb(st, "first_zero", [P, D])
        pc = c.banks(st, "first_pc", 2)
        (made, link_s, shared, prefixed, zero_made, cleared, slotted, sent) = c.sems(
            "made link shared prefixed zero_made cleared slotted sent", "first")
        with c.nc.Block() as block:
            @block.sync
            def _(sp):
                sp.wait_ge(zero_made, 1)
                sp.dma_start(d.x.rearrange("(p a) f -> p a f", p=P),
                             zero[:].unsqueeze(1).to_broadcast([P, NB * NS, D])).then_inc(cleared, 16)

            @block.gpsimd
            def _(pool):
                pool.memset(zero[:], 0.0).then_inc(zero_made, 1)
                lower_index(pool, made, before)
                pool.memset(earlier[:], 1.0).then_inc(made, 1)
                pool.wait_ge(made, 3)
                pool.affine_select(out=earlier[:], in_=earlier[:], compare_op=ALU.is_gt, fill=0.0, base=0,
                                   pattern=[[1, P]], channel_multiplier=-1).then_inc(made, 1)
                pool.iota(number[:], [[1, NB]], base=0, channel_multiplier=0).then_inc(made, 1)
                pool.wait_ge(cleared, 16)
                pool.wait_ge(slotted, 1)
                for b in range(B):
                    pool.indirect_dma_start(d.x, bass.IndirectOffsetOnAxis(ap=d.slot[:T, b:b + 1], axis=0),
                                            r.z[:T, b, :], None).then_inc(sent, 16)
                pool.wait_ge(sent, 16 * B)

            @block.tensor
            def _(pe):
                pe.wait_ge(made, 4)
                pe.wait_ge(shared, 1)
                marks = chosen[:T].rearrange("p b e -> p (b e)")
                pe.matmul(pc[:T, 0, :B * E], earlier[:T, :T], marks, start=True, stop=True)
                pe.matmul(pc[:T, 1, :B * E], c.ones[:T, :T], marks, start=True, stop=True).then_inc(prefixed, 1)

            @block.vector
            def _(dve):
                link = Link(dve, link_s)
                dve.wait_ge(made, 5)
                dve.memset(runs[:], 1.0)
                link.after(dve.tensor_copy(block_of[:], number[:]))
                ranks(dve, link, r, above, tie, before, rank)
                dve.memset(runs[:, :, 0:1], 0.0)
                dve.tensor_scalar(chosen[:T], rank[:T], 0.0, None, ALU.is_equal).then_inc(shared, 1)
                dve.wait_ge(prefixed, 1)
                link.after(dve.tensor_copy(totals[:T], pc[:T, 1, :B * E].rearrange("p (b e) -> p e b", e=E)))
                link.after(dve.tensor_tensor_scan(places[:T].rearrange("p e b -> p (e b)"),
                                                  runs[:T].rearrange("p e b -> p (e b)"),
                                                  totals[:T].rearrange("p e b -> p (e b)"), 0.0, ALU.mult, ALU.add))
                link.after(dve.tensor_copy(total[:T, :], places[:T, :, B - 1]))
                link.after(dve.tensor_tensor(places[:T], places[:T], totals[:T], ALU.subtract))
                link.after(dve.tensor_scalar(blocks[:T, :], total[:T, :], 1.0 / S, SMALLEST, ALU.mult, ALU.add))
                link.after(dve.tensor_scalar(blocks[:T, :], blocks[:T, :], ROUND, None, ALU.add))
                link.after(dve.tensor_scalar(blocks[:T, :], blocks[:T, :], ROUND, None, ALU.subtract))
                link.after(dve.tensor_tensor(above[:T, 0], before[:T],
                                             blocks[:T, :].unsqueeze(1).to_broadcast([T, E, E]), ALU.mult))
                link.after(dve.tensor_reduce(start[:T, :], above[:T, 0], AX.X, ALU.add))
                dve.tensor_tensor(end[:T, :], start[:T, :], blocks[:T, :], ALU.add)
                link.after(dve.tensor_tensor(place[:T], places[:T].rearrange("p e b -> p b e"),
                                             pc[:T, 0, :B * E].rearrange("p (b e) -> p b e", e=E), ALU.add))
                link.after(dve.tensor_scalar(start[:T, :], start[:T, :], float(S), None, ALU.mult))
                link.after(dve.tensor_tensor(place[:T], place[:T],
                                             start[:T, :].unsqueeze(1).to_broadcast([T, B, E]), ALU.add))
                link.after(dve.tensor_tensor(place[:T], place[:T], chosen[:T], ALU.mult))
                link.after(dve.tensor_reduce(slot[:T, :], place[:T], AX.X, ALU.add))
                dve.tensor_copy(d.slot[:T, :], slot[:T, :]).then_inc(slotted, 1)
                link.after(dve.tensor_tensor(passed[:], block_of[:].unsqueeze(2).to_broadcast([1, NB, E]),
                                             end[0:1, :].unsqueeze(1).to_broadcast([1, NB, E]), ALU.is_ge))
                link.after(dve.tensor_reduce(block_of[:], passed[:], AX.X, ALU.add))
                link.after(dve.tensor_scalar(block_of[:], block_of[:], float(E - 1), None, ALU.min))
                dve.tensor_copy(d.expert[:], block_of[:])


def expert_blocks(c, d, a):
    nf = FF // P
    np_ = nf // 2
    w1_size = KD * FF
    with ExitStack() as st:
        x = c.sb(st, "blocks_x", [P, 2, NS, D])
        xts = [c.sb(st, f"blocks_xt{n}", [P, 2, KD, S], F32R) for n in range(2)]
        w = c.sb(st, "blocks_w", [P, 2, w1_size + nf * D])
        parts = [c.sb(st, f"blocks_w{n}", [P, 2, w1_size + nf * D], F32R) for n in range(2)]
        first_w, second_w = slice(0, w1_size), slice(w1_size, w1_size + nf * D)
        w1, w2 = ([v[:, :, at].rearrange("p v (k f) -> p v k f", k=k) for v in parts]
                  for at, k in ((first_w, KD), (second_w, nf)))
        b1 = c.sb(st, "blocks_b1", [P, 2, nf])
        b2 = c.sb(st, "blocks_b2", [P, 2, D])
        inner = c.sb(st, "blocks_inner", [P, nf, S])
        inners = [c.sb(st, f"blocks_inner{n}", [P, 2, nf, S], F32R) for n in range(2)]
        y = c.sb(st, "blocks_y", [P, 2, NS, D])
        pt = c.banks(st, "blocks_pt", 2)
        ph = c.banks(st, "blocks_ph", 4)
        py = c.banks(st, "blocks_py", 2)
        (x_in0, x_in1, w1_in0, w1_in1, w2_in0, w2_in1, b_in0, b_in1, turned, xt_high, xt_ready, high1, low1, high2, low2,
         inner_sum, inner_made, inner_high, inner_split, y_sum, y_ready, y_out0, y_out1, stored) = c.sems(
            "x_in0 x_in1 w1_in0 w1_in1 w2_in0 w2_in1 b_in0 b_in1 turned xt_high xt_ready high1 low1 high2 low2 "
            "inner_sum inner_made inner_high inner_split y_sum y_ready y_out0 y_out1 stored", "blocks")
        x_in, b_in, y_out = (x_in0, x_in1), (b_in0, b_in1), (y_out0, y_out1)
        w1_in, w2_in = (w1_in0, w1_in1), (w2_in0, w2_in1)
        x_blocks, y_blocks = (t.rearrange("(k s p) f -> k p s f", s=NS, p=P) for t in (d.x, d.y))

        def pipeline(eng, body):
            with eng.Fori(0, NB // 2 - 1) as i:
                for u in range(2):
                    body(2 * i + u, u, i, True)
            for u in range(2):
                body(NB - 2 + u, u, NB // 2 - 1, False)

        with c.nc.Block() as block:
            @block.sync
            def _(sp):

                def expert_of(k):
                    return sp.value_load(d.expert[0:1, bass.ds(k, 1)], min_val=0, max_val=E - 1)

                def operands(k, u):
                    sp.wait_ge(turned, k + 1)
                    sp.dma_start(x[:, u], x_blocks[bass.ds(k, 1)].rearrange(
                        "a p s f -> p (a s) f")).then_inc(x_in[u], 16)
                    e = expert_of(k)
                    sp.wait_ge(low1, k + 1)
                    sp.dma_start(w[:, u, first_w], a["top1_w1"][bass.ds(e, 1)].rearrange(
                        "a p k f -> p (a k f)")).then_inc(w1_in[u], 16)
                    sp.wait_ge(low2, k + 1)
                    sp.dma_start(w[:, u, second_w], a["top1_w2"][bass.ds(e, 1)].rearrange(
                        "a p k f -> p (a k f)")).then_inc(w2_in[u], 16)

                def biases(k, u):
                    e = expert_of(k)
                    sp.wait_ge(y_ready, k + 1)
                    sp.dma_start(b1[:, u], a["top1_b1"][bass.ds(e, 1)].rearrange(
                        "a p f -> p (a f)")).then_inc(b_in[u], 16)
                    sp.dma_start(b2[:, u], a["top1_b2"][bass.ds(e, 1)].to_broadcast([P, D])).then_inc(b_in[u], 16)

                operands(0, 0)
                operands(1, 1)
                biases(0, 0)
                with sp.Fori(1, NB // 2) as i:
                    for u in range(2):
                        operands(2 * i + u, u)
                        biases(2 * i + u - 1, 1 - u)
                biases(NB - 1, 1)

            @block.tensor
            def _(pe):
                pe.sem_inc(turned, 2)
                pe.sem_inc(y_sum, 2)

                def turn(k, u, i):
                    pe.wait_ge(x_in[u], 16 * (i + 1))
                    pe.wait_ge(xt_ready, k + 1)
                    for m in range(KD):
                        for s in range(NS):
                            last = pe.transpose(pt[:, u, m * S + s * P:m * S + (s + 1) * P],
                                                x[:, u, s, m * P:(m + 1) * P], c.ident[:])
                    last.then_inc(turned, 1)

                def first(k, u):
                    pe.wait_ge(xt_ready, k + 3)
                    pe.wait_ge(low1, k + 3)
                    for n in range(np_):
                        pe.wait_ge(inner_made, np_ * k + n + 1)
                        for f in (2 * n, 2 * n + 1):
                            for m in range(KD):
                                for v, z in PARTS:
                                    last = pe.matmul(ph[:, n, f % 2 * S:(f % 2 + 1) * S],
                                                     w1[v][:, u, m, f * P:(f + 1) * P], xts[z][:, u, m, :],
                                                     start=m == 0 and (v, z) == PARTS[0],
                                                     stop=m == KD - 1 and (v, z) == PARTS[-1])
                        last.then_inc(inner_sum, 1)

                def second(k, u):
                    pe.wait_ge(low2, k + 3)
                    pe.wait_ge(y_ready, k + 1)
                    for s in range(NS):
                        for f in range(nf):
                            if s == 0 and f % 2 == 0:
                                pe.wait_ge(inner_split, np_ * k + f // 2 + 1 + np_)
                            for v, z in PARTS:
                                last = pe.matmul(py[:, u, s * D:(s + 1) * D],
                                                 inners[v][:, u, f, s * P:(s + 1) * P], w2[z][:, u, f, :],
                                                 start=f == 0 and (v, z) == PARTS[0],
                                                 stop=f == nf - 1 and (v, z) == PARTS[-1])
                    last.then_inc(y_sum, 1)

                def body(k, u, i, more):
                    if more or u == 0:
                        first(k + 1, 1 - u)
                    if more:
                        turn(k + 2, u, i + 1)
                    second(k, u)

                turn(0, 0, 0)
                first(0, 0)
                turn(1, 1, 0)
                pipeline(pe, body)

            @block.scalar
            def _(act):
                act.sem_inc(inner_made, np_)

                def high(u, part, made):
                    act.activation(parts[0][:, u, part], w[:, u, part], ACT.Copy).then_inc(made, 1)

                def relu(k, u, i):
                    act.wait_ge(b_in[u], 32 * (i + 1))
                    for n in range(np_):
                        act.wait_ge(inner_sum, np_ * k + n + 1)
                        act.wait_ge(inner_split, np_ * k + n + 1)
                        for f in (2 * n, 2 * n + 1):
                            last = act.activation(inner[:, f, :], ph[:, n, f % 2 * S:(f % 2 + 1) * S], ACT.Relu,
                                                  bias=b1[:, u, f:f + 1])
                        last.then_inc(inner_made, 1)

                def body(k, u, i, more):
                    if more:
                        act.wait_ge(w1_in[u], 16 * (i + 2))
                        high(u, first_w, high1)
                    if more or u == 0:
                        relu(k + 1, 1 - u, i + u)
                    if more:
                        act.wait_ge(w2_in[u], 16 * (i + 2))
                        act.wait_ge(y_sum, k + 3)
                        high(u, second_w, high2)

                for u in range(2):
                    act.wait_ge(w1_in[u], 16)
                    high(u, first_w, high1)
                    act.wait_ge(w2_in[u], 16)
                    high(u, second_w, high2)
                    if u == 0:
                        relu(0, 0, 0)
                pipeline(act, body)

            @block.vector
            def _(dve):
                dve.sem_inc(xt_ready, 2)
                dve.sem_inc(y_ready, 2)
                dve.sem_inc(low1, 2)
                dve.sem_inc(inner_split, np_)

                def features(k, u):
                    flat_parts = [v[:, u].rearrange("p m t -> p (m t)") for v in xts]
                    dve.wait_ge(turned, k + 3)
                    dve.tensor_scalar(flat_parts[0], pt[:, u, :], 1.0, None, ALU.mult).then_inc(xt_high, 1)
                    dve.wait_ge(xt_high, k + 1)
                    dve.tensor_tensor(flat_parts[1], pt[:, u, :], whole(flat_parts[0]),
                                      ALU.subtract).then_inc(xt_ready, 1)

                def low(k, u):
                    dve.wait_ge(high1, k + 1)
                    dve.tensor_tensor(parts[1][:, u, first_w], w[:, u, first_w], whole(parts[0][:, u, first_w]),
                                      ALU.subtract).then_inc(low1, 1)

                def split(k, u):
                    dve.wait_ge(y_sum, k + 1)
                    for n in range(np_):
                        pair = slice(2 * n, 2 * n + 2)
                        dve.wait_ge(inner_made, np_ * k + n + 1 + np_)
                        dve.tensor_scalar(inners[0][:, u, pair, :], inner[:, pair, :], 1.0, None,
                                          ALU.mult).then_inc(inner_high, 1)
                        dve.wait_ge(inner_high, np_ * k + n + 1)
                        dve.tensor_tensor(inners[1][:, u, pair, :], inner[:, pair, :], whole(inners[0][:, u, pair, :]),
                                          ALU.subtract).then_inc(inner_split, 1)

                def body(k, u, i, more):
                    if more:
                        low(k + 2, u)
                    if more or u == 0:
                        split(k + 1, 1 - u)
                    if more:
                        features(k + 2, u)
                    dve.wait_ge(y_sum, k + 3)
                    dve.wait_ge(stored, k + 1)
                    for s in range(NS):
                        last = dve.tensor_tensor(y[:, u, s, :], py[:, u, s * D:(s + 1) * D], b2[:, u], ALU.add)
                    last.then_inc(y_ready, 1)

                features(0, 0)
                low(0, 0)
                split(0, 0)
                features(1, 1)
                low(1, 1)
                pipeline(dve, body)

            @block.gpsimd
            def _(pool):
                pool.sem_inc(stored, 2)
                pool.sem_inc(low2, 2)

                def low(k, u):
                    pool.wait_ge(high2, k + 1)
                    pool.tensor_tensor(parts[1][:, u, second_w], w[:, u, second_w],
                                       whole(parts[0][:, u, second_w]), ALU.subtract).then_inc(low2, 1)

                def body(k, u, i, more):
                    pool.wait_ge(y_ready, k + 3)
                    pool.dma_start(y_blocks[bass.ds(k, 1)].rearrange("a p s f -> p (a s) f"),
                                   y[:, u]).then_inc(y_out[u], 16)
                    if more:
                        low(k + 2, u)
                    pool.wait_ge(y_out[u], 16 * (i + 1))
                    pool.sem_inc(stored, 1)

                low(0, 0)
                low(1, 1)
                pipeline(pool, body)


def collect_rows(c, d, ph):
    with ExitStack() as st:
        y = c.sb(st, ph + "_row", [P, 2, G, D])
        six = c.sb(st, ph + "_rsix", [P, G, 9])
        fetched0, fetched1, link_s, done = c.sems("fetched0 fetched1 link done", ph + "_collect")
        fetched = (fetched0, fetched1)
        with c.nc.Block() as block:
            @block.gpsimd
            def _(pool):
                for g in range(NG):
                    if g >= 2:
                        pool.wait_ge(done, g - 1)
                    for j in range(G):
                        pool.indirect_dma_start(y[:T, g % 2, j, :], None, d.y, bass.IndirectOffsetOnAxis(
                            ap=d.slot[:T, G * g + j:G * g + j + 1], axis=0)).then_inc(fetched[g % 2], 16)

            @block.vector
            def _(dve):
                link = Link(dve, link_s)
                for g in range(NG):
                    if g >= 1:
                        dve.wait_ge(done, g)
                    dve.wait_ge(fetched[g % 2], 16 * G * (g // 2 + 1))
                    tiles = c.resid[:T, G * g:G * (g + 1), :]
                    link.after(dve.tensor_tensor(tiles, y[:T, g % 2], tiles, ALU.add))
                    stats(dve, link, six, [(c.resid[:T, G * g + j, :], c.moments[:T, G * g + j, :])
                                           for j in range(G)]).then_inc(done, 1)


def experts(c, r, a, names, nf, func):
    nc = c.nc
    w1n, w2n = names
    flat_share = r.share[:T].rearrange("p b e -> p (b e)")
    w1_size = KD * nf * P
    with ExitStack() as st:
        w = c.sb(st, r.ph + "_w", [P, 2, w1_size + nf * D])
        parts = [c.sb(st, f"{r.ph}_w{n}", [P, 2, w1_size + nf * D], F32R) for n in range(2)]
        w1, w2 = ([x[:, :, at].rearrange("p v (k f) -> p v k f", k=k) for x in parts]
                  for at, k in ((slice(0, w1_size), KD), (slice(w1_size, w1_size + nf * D), nf)))
        inner = c.sb(st, r.ph + "_inner", [P, 2, nf, N])
        inners = [c.sb(st, f"{r.ph}_inner{n}", [P, 2, nf, N], F32R) for n in range(2)]
        ph = c.banks(st, r.ph + "_ph", 2 * nf)
        py = c.banks(st, r.ph + "_py", 4)
        (w_in0, w_in1, w_high, w_split, inner_sum, inner_made, inner_high, inner_split, y_sum, added) = c.sems(
            "w_in0 w_in1 w_high w_split inner_sum inner_made inner_high inner_split y_sum added",
            r.ph + "_experts")
        w_in = (w_in0, w_in1)

        def groups(eng, body):
            with eng.Fori(0, E // 2) as i:
                for v in range(2):
                    with eng.Fori(0, NG // 2) as q:
                        for u in range(2):
                            body(NG * (2 * i + v) + 2 * q + u, i, v, q, u)

        def two_ahead(eng, late, early):
            def expert(i, v, final):
                start = NG * (2 * i + v)
                with eng.Fori(0, NG // 2 - 1) as q:
                    for u in range(2):
                        late(start + 2 * q + u, i, v, q, u)
                        early(start + 2 * q + u + 2, i, v, q + 1, u)
                for u in range(2):
                    late(start + NG - 2 + u, i, v, NG // 2 - 1, u)
                    if not final:
                        early(start + NG + u, i + v, 1 - v, 0, u)

            for u in range(2):
                early(u, 0, 0, 0, u)
            with eng.Fori(0, E // 2 - 1) as i:
                for v in range(2):
                    expert(i, v, False)
            for v in range(2):
                expert(E // 2 - 1, v, v == 1)

        with nc.Block() as block:
            @block.sync
            def _(sp):
                with sp.Fori(0, E // 2) as i:
                    for v in range(2):
                        sp.wait_ge(w_split, 2 * i + v + 1)
                        sp.dma_start(w[:, v, :w1_size], a[w1n][bass.ds(2 * i + v, 1)].rearrange(
                            "a p k f -> p (a k f)")).then_inc(w_in[v], 16)
                        sp.dma_start(w[:, v, w1_size:], a[w2n][bass.ds(2 * i + v, 1)].rearrange(
                            "a p k f -> p (a k f)")).then_inc(w_in[v], 16)

            @block.gpsimd
            def _(pool):
                pool.sem_inc(w_split, 2)
                with pool.Fori(0, E // 2) as i:
                    for v in range(2):
                        pool.wait_ge(w_in[v], 32 * (i + 1))
                        pool.wait_ge(y_sum, NG * (2 * i + v + 1))
                        pool.tensor_tensor(parts[0][:, v], w[:, v], c.ones[:, 0:1].to_broadcast([P, w1_size + nf * D]),
                                           ALU.mult).then_inc(w_high, 1)
                        pool.wait_ge(w_high, 2 * i + v + 1)
                        pool.tensor_tensor(parts[1][:, v], w[:, v], whole(parts[0][:, v]),
                                           ALU.subtract).then_inc(w_split, 1)

            @block.tensor
            def _(pe):
                pe.sem_inc(y_sum, 2 * NG)

                def first(n, i, v, q, u):
                    if u == 0:
                        pe.wait_ge(w_split, 2 * i + v + 3)
                    pe.wait_ge(inner_made, n + 1)
                    for f in range(nf):
                        for k in range(KD):
                            for x, y in PARTS:
                                last = pe.matmul(ph[:, nf * u + f, :N], w1[x][:, v, k, f * P:(f + 1) * P],
                                                 r.zt[y][:, k, bass.ds(N * (2 * q + u), N)],
                                                 start=k == 0 and (x, y) == PARTS[0],
                                                 stop=k == KD - 1 and (x, y) == PARTS[-1])
                    last.then_inc(inner_sum, 1)

                def second(n, i, v, q, u):
                    pe.wait_ge(inner_split, n + 3)
                    pe.wait_ge(added, n + 1)
                    for j in range(G):
                        for f in range(nf):
                            for x, y in PARTS:
                                last = pe.matmul(py[:T, 2 * u + j // 2, j % 2 * D:(j % 2 + 1) * D],
                                                 inners[x][:, u, f, j * T:(j + 1) * T], w2[y][:, v, f, :],
                                                 start=f == 0 and (x, y) == PARTS[0],
                                                 stop=f == nf - 1 and (x, y) == PARTS[-1])
                    last.then_inc(y_sum, 1)

                two_ahead(pe, second, first)

            @block.scalar
            def _(act):
                act.sem_inc(inner_made, 2)

                def body(n, i, v, q, u):
                    act.wait_ge(inner_sum, n + 1)
                    act.wait_ge(inner_split, n + 1)
                    act.activation(inner[:, u], ph[:, nf * u:nf * u + nf, :N], func).then_inc(inner_made, 1)
                    act.wait_ge(inner_made, n + 3)
                    act.wait_ge(y_sum, 2 * NG + n - 1)
                    act.activation(inners[0][:, u], inner[:, u], ACT.Copy).then_inc(inner_high, 1)
                groups(act, body)

            @block.vector
            def _(dve):
                dve.sem_inc(inner_split, 2)
                dve.sem_inc(added, 2)

                def split(n, i, v, q, u):
                    dve.wait_ge(inner_high, n + 1)
                    dve.tensor_tensor(inners[1][:, u], inner[:, u], whole(inners[0][:, u]),
                                      ALU.subtract).then_inc(inner_split, 1)

                def add(n, i, v, q, u):
                    dve.wait_ge(y_sum, 2 * NG + n + 1)
                    dve.wait_ge(added, n + 2)
                    for j in range(G):
                        b = G * (2 * q + u) + j
                        last = dve.scalar_tensor_tensor(
                            c.tile(b), py[:T, 2 * u + j // 2, j % 2 * D:(j % 2 + 1) * D],
                            flat_share[:, bass.ds(E * b + 2 * i + v, 1)], c.tile(b), ALU.mult, ALU.add)
                    last.then_inc(added, 1)

                two_ahead(dve, add, split)


def all_stats(c, ph):
    with ExitStack() as st:
        six = c.sb(st, ph + "_six", [P, G, 9])
        link_s, done = c.sems("link done", ph + "_stats")
        with c.nc.Block() as block:
            @block.vector
            def _(dve):
                dve.sem_inc(done, 1)
                with dve.Fori(0, NG) as g:
                    link = Link(dve, link_s, g, 2)
                    dve.wait_ge(done, g + 1)
                    tile_stats(dve, c, link, six, g).then_inc(done, 1)
                    link.end()


def top1_experts(c, a):
    inverse_deviation(c, 1e-5, "top1")
    with ExitStack() as st:
        d = Dispatch(c, st, "top1")
        with ExitStack() as st2:
            r = Routing(c, st2, "top1", rows=True)
            gather_tokens(c, r, lambda dve, z, g: normalize(dve, c, z, g), "top1_wg",
                          ("top1_gate_b", "top1_expert_bias"), None, a)
            route_first(c, r, d)
        expert_blocks(c, d, a)
        collect_rows(c, d, "top1")


class Attention:

    def __init__(self, ph, dm=DH, kv=H, scale=DH ** -0.5, causal=False, affine=False, norm=None,
                 differential=False, keep=None):
        self.ph, self.dm, self.kv, self.scale, self.causal = ph, dm, kv, scale, causal
        self.affine, self.norm, self.differential, self.keep = affine, norm, differential, keep


NX = 16
LAMBDA_INIT = 0.8 - 0.6 * math.exp(-0.3 * 12)
LARGEST = float(np.finfo(np.float32).max)


def softmax_attention(c, a, s):
    nc = c.nc
    ph, dm = s.ph, s.dm
    maps = D // dm
    nr = G * maps // NX
    nh = P // dm
    share = maps // H
    with ExitStack() as st:
        wq, wk, wo = (c.sb(st, f"{ph}_w{n}", [P, KD, D]) for n in "qko")
        wv = c.sb(st, ph + "_wv", [P, KD, s.kv * DH])
        fore = c.sb(st, ph + "_fore", [P, 2, KD])
        factors = c.sb(st, ph + "_factors", [P, 4])
        vbias = c.sb(st, ph + "_vbias", [P, D])
        obias = c.sb(st, ph + "_obias", [P, D])
        norm = c.sb(st, ph + "_norm", [P, KD])
        lam = c.sb(st, ph + "_lam", [P, 4, 8])
        lams = c.sb(st, ph + "_lams", [P, 2])
        neglam = c.sb(st, ph + "_neglam", [P, 1])
        subln = c.sb(st, ph + "_subln", [P, DH])
        own = c.sb(st, ph + "_own", [P, nh])
        future = c.sb(st, ph + "_future", [P, 4, T], BF16)
        identh = c.sb(st, ph + "_identh", [P, P], BF16)
        scale2 = c.sb(st, ph + "_scale2", [P, B])
        z = c.sb(st, ph + "_z", [P, G, D])
        temp = c.sb(st, ph + "_temp", [P, G, D])
        zt = c.sb(st, ph + "_zt", [P, KD, N])
        qk = c.sb(st, ph + "_qk", [P, 2 * KD, N])
        qt, kt = ([c.sb(st, f"{ph}_{x}t{n}", [P, 2, KD, N], F32R) for n in range(2)] for x in "qk")
        km = [c.sb(st, f"{ph}_km{n}", [P, 2, NX, T], F32R) for n in range(2)]
        v1 = c.sb(st, ph + "_v1", [P, 2, G, s.kv, DH + 1])
        most = c.sb(st, ph + "_most", [P, 2, NX])
        p = c.sb(st, ph + "_p", [P, 2, NX, T])
        pt = c.sb(st, ph + "_pt", [P, 2, NX, T])
        inverse = c.sb(st, ph + "_inverse", [P, NX])
        two = c.sb(st, ph + "_two", [P, NX, DH])
        o = c.sb(st, ph + "_o", [P, 2, G, D])
        squares = c.sb(st, ph + "_squares", [P, G, D])
        roots = c.sb(st, ph + "_roots", [P, G * H])
        ot = c.sb(st, ph + "_ot", [P, KD, N])
        six = c.sb(st, ph + "_six", [P, G, 9])
        ps = c.banks(st, ph + "_ps", 4)
        pp = c.banks(st, ph + "_pp", 2)
        steps_bank = c.banks(st, ph + "_px", 1)
        po = c.banks(st, ph + "_po", 1)
        (matrices_in, w_in, own_made, prep_s, lam_sum, lam_exp, z_ready, step_sum, step_done, masked, score_sum,
         high_made, qk_split, less_ready, exp_ready, turned, kept, mix_sum, mix_ready, square_ready, root_ready, o_ready,
         link_first, link_pairs, link_last) = c.sems(
            "matrices_in w_in own_made prep lam_sum lam_exp z_ready step_sum step_done masked score_sum "
            "high_made qk_split less_ready exp_ready turned kept mix_sum mix_ready square_ready root_ready o_ready "
            "link_first link_pairs link_last", ph)
        loads = []
        if s.affine:
            loads += [(fore[:, 0, :], a[ph + "_bq"]), (fore[:, 1, :], a[ph + "_bk"]),
                      (vbias[:T, :], row(a[ph + "_bv"], T)), (obias[:T, :], row(a[ph + "_bo"], T))]
            loads += [(factors[:, n:n + 1], row(a[f"{ph}_s{x}"], P)) for n, x in enumerate("qkvo")]
        if s.norm:
            loads += [(norm[:], a[s.norm])]
        if s.differential:
            loads += [(lam[:T, n, :], row(a[f"{ph}_lambda_{x}"], T)) for n, x in enumerate(("q1", "k1", "q2", "k2"))]
            loads += [(subln[:T, :], row(a[ph + "_subln"], T))]

        per_slot = 3 if nr == 4 else 2

        def bank_of(count):
            n = count % SPREAD
            return steps_bank if n == SPREAD - 1 else ps[:, n:n + 1]

        def carried(part, n, slot):
            at = per_slot * n + slot
            if slot < per_slot and at < len(ORDER) and ORDER[at] in steps(part):
                return [(ORDER[at], steps(part).index(ORDER[at]))]
            return []

        def half(x):
            return x // nh

        def at(n):
            return n * NX // maps, n % (maps // NX)

        with nc.Block() as block:
            @block.sync
            def _(sp):
                for w, n in ((wq, "q"), (wk, "k"), (wv, "v"), (wo, "o")):
                    sp.dma_start(w[:], a[f"{ph}_w{n}"]).then_inc(matrices_in, 16)
                for dst, src in loads:
                    sp.dma_start(dst, src).then_inc(w_in, 16)

            @block.gpsimd
            def _(pool):
                pool.memset(own[:], 1.0).then_inc(own_made, 1)
                pool.memset(future[:], 0.0).then_inc(own_made, 1)
                pool.tensor_copy(identh[:], c.ident[:]).then_inc(own_made, 1)
                pool.wait_ge(own_made, 3)
                pool.affine_select(out=own[:], in_=own[:], compare_op=ALU.is_ge, fill=0.0, base=0,
                                   pattern=[[-dm, nh]], channel_multiplier=1).then_inc(own_made, 1)
                pool.affine_select(out=future[:], in_=future[:], compare_op=ALU.is_ge, fill=-1e30, base=0,
                                   pattern=[[0, 4], [-1, T]], channel_multiplier=1).then_inc(own_made, 1)
                pool.wait_ge(own_made, 5)
                pool.affine_select(out=own[:], in_=own[:], compare_op=ALU.is_ge, fill=0.0, base=dm - 1,
                                   pattern=[[dm, nh]], channel_multiplier=-1).then_inc(own_made, 1)
                pool.wait_ge(own_made, 6)

                def split(g, q, x):
                    n = SPLIT.index(x)
                    part = (qt if x[0] == "q" else kt)[0][:, q, n % KD, :]
                    low_part = (qt if x[0] == "q" else kt)[1][:, q, n % KD, :]
                    pool.wait_ge(high_made, len(SPLIT) * g + n + 1)
                    pool.tensor_tensor(low_part, qk[:, n, :], whole(part), ALU.subtract).then_inc(qk_split, 1)

                def mask(g, q, n):
                    j, m0 = at(n)
                    if n == 0:
                        pool.wait_ge(qk_split, len(SPLIT) * (g + 1) + 1)
                    pool.wait_ge(score_sum, nr * g + n + 1)
                    for part, masked_part in zip(kt, km):
                        for x in range(0, NX, nh):
                            src = whole(part[:, q, m0 + x // nh, j * T:(j + 1) * T])
                            last = pool.tensor_tensor(
                                masked_part[:, n % 2, x:x + nh, :], src.unsqueeze(1).to_broadcast([P, nh, T]),
                                own[:].unsqueeze(2).to_broadcast([P, nh, T]), ALU.mult)
                    last.then_inc(masked, 1)

                def group(g, q, part):
                    for n in range(1, nr):
                        mask(g, q, n)
                        if part != "last" and n >= 2:
                            for slot in range(3):
                                for x, _ in carried(part, n - 2, slot):
                                    if x in SPLIT:
                                        split(g + 1, 1 - q, x)
                    if part != "last":
                        mask(g + 1, 1 - q, 0)

                pool.sem_inc(qk_split, 1)
                for x in SPLIT:
                    split(0, 0, x)
                mask(0, 0, 0)
                group(0, 0, "first")
                with pool.Fori(0, NG // 2 - 1) as i:
                    for u in range(2):
                        group(2 * i + 1 + u, (1 + u) % 2, "pairs")
                group(NG - 1, 1, "last")

            @block.tensor
            def _(pe):
                pe.sem_inc(score_sum, 2)
                pe.sem_inc(mix_sum, 2)

                def step(x, g, q, count, alone=False):
                    if not alone:
                        pe.wait_ge(step_done, count)
                    elif spread(count):
                        pe.wait_ge(step_done, spread(count))
                    px = bank_of(count) if alone else steps_bank
                    k = int(x[1])
                    bank = px[:, 0, :N]
                    if x[0] == "z":
                        if k == 0:
                            pe.wait_ge(z_ready, g + 1)
                        for j in range(G):
                            last = pe.transpose(px[:, 0, j * T:(j + 1) * T], z[:T, j, k * P:(k + 1) * P],
                                                c.ident[:T, :T])
                    elif x[0] in "qk":
                        w = wq if x[0] == "q" else wk
                        for m in range(KD):
                            last = pe.matmul(bank, w[:, m, k * P:(k + 1) * P], zt[:, m, :],
                                             start=m == 0, stop=m == KD - 1)
                    elif x[0] == "o":
                        if k == 0 and s.differential:
                            pe.wait_ge(o_ready, g + 1)
                        elif k == 0:
                            pe.wait_ge(mix_ready, nr * (g + 1) + 1)
                        for j in range(G):
                            last = pe.transpose(px[:, 0, j * T:(j + 1) * T], o[:T, q, j, k * P:(k + 1) * P],
                                                c.ident[:T, :T])
                    else:
                        src, w, width = (zt, wv, s.kv * DH) if x[0] == "v" else (ot, wo, D)
                        for j in (2 * k, 2 * k + 1):
                            for m in range(KD):
                                last = pe.matmul(px[:T, 0, j % 2 * D:j % 2 * D + width],
                                                 src[:, m, j * T:(j + 1) * T], w[:, m, :],
                                                 start=m == 0, stop=m == KD - 1)
                    last.then_inc(step_sum, 1)

                def scores(g, q, n):
                    j, m0 = at(n)
                    pe.wait_ge(masked, nr * g + n + 1)
                    if not (isinstance(g, int) and nr * g + n == 0):
                        pe.wait_ge(less_ready, nr * g + n)
                    for x in range(0, NX, 4):
                        if s.causal:
                            pe.matmul(ps[:T, x // 4, :N], identh[:T, :T],
                                      future[:T].rearrange("p x t -> p (x t)"), start=True, stop=False)
                        for v, z in PARTS:
                            last = pe.matmul(ps[:T, x // 4, :N], qt[v][:, q, m0 + half(x), j * T:(j + 1) * T],
                                             km[z][:, n % 2, x:x + 4, :].rearrange("p x t -> p (x t)"),
                                             start=not s.causal and (v, z) == PARTS[0], stop=(v, z) == PARTS[-1])
                    last.then_inc(score_sum, 1)

                def turn(g, n, q):
                    r = nr * g + n
                    if q == 0:
                        pe.wait_ge(exp_ready, r + 1)
                    pe.wait_ge(kept, 4 * r + q + 1)
                    for x in range(4):
                        last = pe.transpose(pp[:T, q % 2, x * T:(x + 1) * T], p[:T, n % 2, 4 * q + x, :],
                                            c.ident[:T, :T])
                    last.then_inc(turned, 1)

                def mix(g, parity, n, q):
                    j, m0 = at(n)
                    r = nr * g + n
                    pe.wait_ge(kept, 4 * r + q + 3)
                    if q == 0:
                        pe.wait_ge(mix_ready, r + 1)
                    for x in range(4 * q, 4 * q + 4):
                        head = (m0 * NX + x) // share // (H // s.kv)
                        last = pe.matmul(po[:T, 0, x * (DH + 1):(x + 1) * (DH + 1)], pt[:T, n % 2, x, :],
                                         v1[:T, parity, j, head, :], start=True, stop=True)
                    if q == 3:
                        last.then_inc(mix_sum, 1)

                def group(g, q, part):
                    def carry(n, slot):
                        for x, count in carried(part, n, slot):
                            late = x in LAST
                            step(x, g - 1 if late else g + 1, 1 - q, first_step(g, part) + count)

                    pe.wait_ge(step_done, first_step(g, part))
                    for n in range(nr):
                        if n + 1 < nr:
                            scores(g, q, n + 1)
                        elif part != "last":
                            scores(g + 1, 1 - q, 0)
                        carry(n, 0)
                        turn(g, n, 0)
                        turn(g, n, 1)
                        mix(g, q, n, 0)
                        carry(n, 1)
                        turn(g, n, 2)
                        mix(g, q, n, 1)
                        turn(g, n, 3)
                        mix(g, q, n, 2)
                        carry(n, 2)
                        mix(g, q, n, 3)

                for count, x in enumerate(NEXT):
                    if x == "q0":
                        pe.wait_ge(matrices_in, 64)
                    step(x, 0, 0, count, alone=True)
                pe.wait_ge(own_made, 6)
                pe.wait_ge(step_done, len(NEXT))
                scores(0, 0, 0)
                group(0, 0, "first")
                with pe.Fori(0, NG // 2 - 1) as i:
                    for u in range(2):
                        group(2 * i + 1 + u, (1 + u) % 2, "pairs")
                group(NG - 1, 1, "last")
                for count, x in enumerate(LAST):
                    step(x, NG - 1, 1, BEFORE_LAST + count)

            @block.scalar
            def _(act):
                act.sem_inc(kept, 2)
                if s.keep is not None:
                    act.wait_ge(lam_sum, 1)
                    act.activation(scale2[:T, :], scale2[:T, :], ACT.Sqrt).then_inc(lam_exp, 1)
                if s.norm:
                    act.wait_ge(w_in, 16 * len(loads))
                if s.differential:
                    act.wait_ge(lam_sum, 1)
                    act.activation(lams[:T, :], lams[:T, :], ACT.Exp).then_inc(lam_exp, 1)

                def read(x, g, q, count, px=steps_bank):
                    if x[0] not in "zqko":
                        return
                    k = int(x[1])
                    bank = px[:, 0, :N]
                    act.wait_ge(step_sum, count + 1)
                    if x[0] == "z":
                        last = act.activation(zt[:, k, :], bank, ACT.Copy, scale=norm[:, k:k + 1] if s.norm else 1.0)
                    elif x[0] == "o":
                        last = act.activation(ot[:, k, :], bank, ACT.Copy)
                    else:
                        m = SPLIT.index(x)
                        act.wait_ge(qk_split, len(SPLIT) * g + 1)
                        if s.affine:
                            n = m // KD
                            last = act.activation(qk[:, m, :], bank, ACT.Identity,
                                                  bias=fore[:, n, k:k + 1], scale=factors[:, n:n + 1])
                        else:
                            last = act.activation(qk[:, m, :], bank, ACT.Copy)
                    last.then_inc(step_done, 1)
                    if x in SPLIT:
                        act.wait_ge(step_done, count + 1)
                        act.activation((qt if x[0] == "q" else kt)[0][:, q, k, :], qk[:, m, :],
                                       ACT.Copy).then_inc(high_made, 1)

                def root(g):
                    act.wait_ge(square_ready, g + 1)
                    act.activation(roots[:T, :], roots[:T, :], ACT.Sqrt).then_inc(root_ready, 1)

                def group(g, q, part):
                    def carry(n, slot):
                        for x, count in carried(part, n, slot):
                            read(x, g - 1 if x in LAST else g + 1, 1 - q, first_step(g, part) + count)

                    for n in range(nr):
                        r = nr * g + n
                        act.wait_ge(less_ready, r + 1)
                        act.activation(p[:T, n % 2], p[:T, n % 2], ACT.Exp, scale=s.scale).then_inc(exp_ready, 1)
                        act.wait_ge(mix_sum, r + 1)
                        carry(n, 0)
                        for q4 in range(4):
                            if q4 == 2:
                                carry(n, 1)
                            act.wait_ge(turned, 4 * r + q4 + 1)
                            act.activation(pt[:T, n % 2, 4 * q4:4 * q4 + 4, :].rearrange("p x t -> p (x t)"),
                                           pp[:T, q4 % 2, :N], ACT.Copy).then_inc(kept, 1)
                        carry(n, 2)
                        if s.differential and part != "first" and n == 0:
                            root(g - 1)

                for count, x in enumerate(NEXT):
                    if x == "q0" and s.affine:
                        act.wait_ge(w_in, 16 * len(loads))
                    read(x, 0, 0, count, bank_of(count))
                group(0, 0, "first")
                with act.Fori(0, NG // 2 - 1) as i:
                    for u in range(2):
                        group(2 * i + 1 + u, (1 + u) % 2, "pairs")
                group(NG - 1, 1, "last")
                if s.differential:
                    root(NG - 1)
                for count, x in enumerate(LAST):
                    read(x, NG - 1, 1, BEFORE_LAST + count)

            @block.vector
            def _(dve):
                prep = Link(dve, prep_s)
                if s.keep is not None:
                    prep.after(dve.tensor_tensor(scale2[:T, :], c.rstd[:T, :], c.rstd[:T, :], ALU.mult))
                    prep.after(dve.tensor_tensor(scale2[:T, :], scale2[:T, :], c.moments[:T, :, 1], ALU.mult))
                    dve.tensor_scalar(scale2[:T, :], scale2[:T, :], 1e-6, None, ALU.add).then_inc(lam_sum, 1)
                    dve.wait_ge(lam_exp, 1)
                    prep.after(dve.reciprocal(scale2[:T, :], scale2[:T, :]))
                    prep.after(dve.tensor_tensor(scale2[:T, :], scale2[:T, :], c.rstd[:T, :], ALU.mult))

                def start(g):
                    normalize(dve, c, z, g, scale2 if s.keep is not None else None).then_inc(z_ready, 1)

                start(0)
                dve.memset(v1[:, :, :, :, DH:DH + 1], 1.0)
                if loads:
                    dve.wait_ge(w_in, 16 * len(loads))
                if s.differential:
                    for n in range(2):
                        last = dve.tensor_tensor(lam[:T, 2 * n, :], lam[:T, 2 * n, :], lam[:T, 2 * n + 1, :], ALU.mult)
                    prep.after(last)
                    dve.tensor_reduce(lams[:T, :], lam[:T, 0:4:2, :], AX.X, ALU.add).then_inc(lam_sum, 1)
                    dve.wait_ge(lam_exp, 1)
                    prep.after(dve.tensor_tensor(neglam[:T, :], lams[:T, 1:2], lams[:T, 0:1], ALU.subtract))
                    dve.tensor_scalar(neglam[:T, :], neglam[:T, :], -LAMBDA_INIT, None, ALU.add)
                    dve.tensor_scalar(subln[:T, :], subln[:T, :], 1.0 - LAMBDA_INIT, None, ALU.mult)
                prep.after(dve.memset(six[:], 0.0))
                dve.sem_inc(mix_ready, 1)

                def subtract_most(link, r, n):
                    score = ps[:T, :, :N].rearrange("p c (x t) -> p c x t", x=4)
                    high = most[:T, n % 2, :]
                    dve.wait_ge(score_sum, r + 3)
                    link.after(dve.tensor_reduce(high.rearrange("p (c x) -> p c x", c=4), score, AX.X, ALU.max))
                    if s.differential:
                        link.after(dve.tensor_scalar(high, high, LARGEST, -LARGEST, ALU.min, ALU.max))
                        for q in range(4):
                            last = dve.scalar_tensor_tensor(
                                p[:T, n % 2, 4 * q:4 * q + 4, :], score[:, q], LARGEST,
                                high[:, 4 * q:4 * q + 4].unsqueeze(2).to_broadcast([T, 4, T]),
                                ALU.min, ALU.subtract)
                        last.then_inc(less_ready, 1)
                        return
                    dve.tensor_tensor(p[:T, n % 2].rearrange("p (c x) t -> p c x t", c=4), score,
                                      high.rearrange("p (c x) -> p c x", c=4).unsqueeze(3)
                                      .to_broadcast([T, 4, 4, T]), ALU.subtract).then_inc(less_ready, 1)

                def divide(link, r, parity, n):
                    j, m0 = at(n)
                    sums = po[:T, 0, :NX * (DH + 1)].rearrange("p (x d) -> p x d", x=NX)
                    dve.wait_ge(mix_sum, r + 3)
                    link.after(dve.reciprocal(inverse[:T, :], sums[:, :, DH]))
                    if s.differential:
                        link.after(dve.tensor_scalar(inverse[:T, 1:NX:2], inverse[:T, 1:NX:2],
                                                     neglam[:T, 0:1], None, ALU.mult))
                    out = o[:T, parity, j, :].rearrange("p (h d) -> p h d", d=DH) if not s.differential else two[:T]
                    last = dve.tensor_tensor(out, sums[:, :, 0:DH],
                                             inverse[:T, :].unsqueeze(2).to_broadcast([T, NX, DH]), ALU.mult)
                    last.then_inc(mix_ready, 1)
                    if s.differential:
                        dve.wait_ge(mix_ready, r + 2)
                        last = dve.tensor_tensor(
                            o[:T, parity, j, m0 * P:(m0 + 1) * P].rearrange("p (h d) -> p h d", d=DH),
                            two[:T, 0:NX:2, :], two[:T, 1:NX:2, :], ALU.add)
                    return last

                def square(link, parity):
                    flat_o = o[:T, parity].rearrange("p j d -> p (j d)")
                    flat_s = squares[:T].rearrange("p j d -> p (j d)")
                    link.after(dve.tensor_tensor(flat_s, flat_o, flat_o, ALU.mult))
                    link.after(dve.tensor_reduce(roots[:T, :], flat_s.rearrange("p (x d) -> p x d", d=DH),
                                                 AX.X, ALU.add))
                    dve.tensor_scalar(roots[:T, :], roots[:T, :], 1 / DH, 1e-5, ALU.mult,
                                      ALU.add).then_inc(square_ready, 1)

                def norm_heads(link, g, parity):
                    heads = o[:T, parity].rearrange("p j (h d) -> p (j h) d", d=DH)
                    dve.wait_ge(root_ready, g + 1)
                    link.after(dve.reciprocal(roots[:T, :], roots[:T, :]))
                    link.after(dve.tensor_tensor(heads, heads, roots[:T, :].unsqueeze(2)
                                                 .to_broadcast([T, G * H, DH]), ALU.mult))
                    last = dve.tensor_tensor(heads, heads, subln[:T, :].unsqueeze(1)
                                             .to_broadcast([T, G * H, DH]), ALU.mult)
                    last.then_inc(o_ready, 1)

                def read(link, x, g, parity, count, px=steps_bank):
                    if x[0] not in "vy":
                        return
                    k = int(x[1])
                    pair = (2 * k, 2 * k + 1)
                    dve.wait_ge(step_sum, count + 1)
                    if x[0] == "v":
                        for j in pair:
                            src = px[:T, 0, j % 2 * D:j % 2 * D + s.kv * DH].rearrange("p (h d) -> p h d", d=DH)
                            dst = v1[:T, parity, j, :, 0:DH]
                            if s.affine:
                                last = dve.scalar_tensor_tensor(
                                    dst, src, factors[:T, 2:3],
                                    vbias[:T, :].rearrange("p (h d) -> p h d", d=DH), ALU.mult, ALU.add)
                            else:
                                last = dve.tensor_copy(dst, src)
                        last.then_inc(step_done, 1)
                        return
                    y = [px[:T, 0, j % 2 * D:(j % 2 + 1) * D] for j in pair]
                    tiles = [c.tile(G * g + j) for j in pair]
                    if s.affine:
                        for j in pair:
                            last = dve.scalar_tensor_tensor(temp[:T, j, :], y[j % 2], factors[:T, 3:4],
                                                            obias[:T, :], ALU.mult, ALU.add)
                        last.then_inc(step_done, 1)
                        dve.wait_ge(step_done, count + 1)
                        for j in pair:
                            last = dve.tensor_tensor(tiles[j % 2], temp[:T, j, :], tiles[j % 2], ALU.add)
                        link.after(last)
                    elif s.keep is not None:
                        for j in pair:
                            last = dve.tensor_scalar(temp[:T, j, :], tiles[j % 2], c.mean(G * g + j),
                                                     c.scale(G * g + j), ALU.subtract, ALU.mult)
                        link.after(last)
                        for j in pair:
                            last = dve.tensor_tensor(flat(s.keep[:T, bass.ds(G * g + j, 1), :]),
                                                     y[j % 2], temp[:T, j, :], ALU.add)
                        last.then_inc(step_done, 1)
                        dve.wait_ge(step_done, count + 1)
                        for j in pair:
                            last = dve.tensor_tensor(tiles[j % 2], flat(s.keep[:T, bass.ds(G * g + j, 1), :]),
                                                     tiles[j % 2], ALU.add)
                        link.after(last)
                    else:
                        for j in pair:
                            last = dve.tensor_tensor(tiles[j % 2], y[j % 2], tiles[j % 2], ALU.add)
                        last.then_inc(step_done, 1)
                        dve.wait_ge(step_done, count + 1)
                    if k == 1:
                        of = (lambda j: c.tile(G * g + j)) if s.keep is None else (
                            lambda j: flat(s.keep[:T, bass.ds(G * g + j, 1), :]))
                        link.after(stats(dve, link, six, [
                            (of(j), flat(c.moments[:T, bass.ds(G * g + j, 1), :])) for j in range(G)]))

                def group(link, g, q, part):
                    def carry(n, slot):
                        for x, count in carried(part, n, slot):
                            read(link, x, g - 1 if x in LAST else g + 1, 1 - q, first_step(g, part) + count)

                    if part != "last":
                        start(g + 1)
                    for n in range(nr):
                        r = nr * g + n
                        if not (part == "last" and n == nr - 1):
                            subtract_most(link, r + 1, n + 1)
                        if s.differential and n == 1 and part != "first":
                            norm_heads(link, g - 1, 1 - q)
                        carry(n, 0)
                        carry(n, 1)
                        carry(n, 2)
                        last = divide(link, r, q, n)
                    if s.differential:
                        link.after(last)
                        square(link, q)

                per_round = 4 if s.differential else 2
                per_pairs = 2 * (nr * per_round + (5 if s.differential else 0) + 2 * bool(s.affine)
                                 + 4 * (s.keep is not None) + 3)
                link = Link(dve, link_first)
                for count, x in enumerate(NEXT):
                    read(link, x, 0, 0, count, bank_of(count))
                subtract_most(link, 0, 0)
                group(link, 0, 0, "first")
                with dve.Fori(0, NG // 2 - 1) as i:
                    link = Link(dve, link_pairs, i, per_pairs)
                    for u in range(2):
                        group(link, 2 * i + 1 + u, (1 + u) % 2, "pairs")
                    link.end()
                link = Link(dve, link_last)
                group(link, NG - 1, 1, "last")
                if s.differential:
                    norm_heads(link, NG - 1, 1)
                for count, x in enumerate(LAST):
                    read(link, x, NG - 1, 1, BEFORE_LAST + count)


def scaled_attention(c, a):
    inverse_deviation(c, 1e-5, "tern")
    softmax_attention(c, a, Attention("tern", affine=True))


def weigh_two(c, r):
    with ExitStack() as st:
        above, tie = (c.sb(st, f"two_{n}", [P, B, E, E]) for n in ("above", "tie"))
        rank, taken = (c.sb(st, f"two_{n}", [P, B, E]) for n in ("rank", "taken"))
        before = c.sb(st, "two_before", [P, E, E])
        most, total = (c.sb(st, f"two_{n}", [P, B]) for n in ("most", "total"))
        made, link_s, less_ready, exp_ready = c.sems("made link less_ready exp_ready", "two")
        with c.nc.Block() as block:
            @block.gpsimd
            def _(pool):
                lower_index(pool, made, before)

            @block.scalar
            def _(act):
                act.wait_ge(less_ready, 1)
                act.activation(r.share[:T], r.share[:T], ACT.Exp).then_inc(exp_ready, 1)

            @block.vector
            def _(dve):
                link = Link(dve, link_s)
                dve.wait_ge(made, 2)
                ranks(dve, link, r, above, tie, before, rank)
                dve.tensor_scalar(taken[:T], rank[:T], 2.0, None, ALU.is_lt)
                link.after(dve.tensor_reduce(most[:T, :], r.share[:T], AX.X, ALU.max))
                dve.tensor_tensor(r.share[:T], r.share[:T], most[:T, :].unsqueeze(2).to_broadcast([T, B, E]),
                                  ALU.subtract).then_inc(less_ready, 1)
                dve.wait_ge(exp_ready, 1)
                link.after(dve.tensor_tensor(r.share[:T], r.share[:T], taken[:T], ALU.mult))
                link.after(dve.tensor_reduce(total[:T, :], r.share[:T], AX.X, ALU.add))
                link.after(dve.reciprocal(total[:T, :], total[:T, :]))
                link.after(dve.tensor_tensor(r.share[:T], r.share[:T],
                                             total[:T, :].unsqueeze(2).to_broadcast([T, B, E]), ALU.mult))


def linear_experts(c, r, w):
    nc = c.nc
    flat_share = r.share[:T].rearrange("p b e -> p (b e)")
    pairs = B // 2
    with ExitStack() as st:
        parts = [c.sb(st, f"{r.ph}_w{n}", [P, KD, E * D], F32R) for n in range(2)]
        py = c.banks(st, r.ph + "_py", 8)
        w_high, w_split, y_sum, added = c.sems("w_high w_split y_sum added", r.ph + "_experts")
        with nc.Block() as block:
            @block.tensor
            def _(pe):
                pe.wait_ge(w_split, KD)
                with pe.Fori(0, E) as e:
                    for n in range(pairs):
                        pe.wait_ge(added, pairs * e + n + 1)
                        for j in range(2):
                            b = 2 * n + j
                            for k in range(KD):
                                for x, y in PARTS:
                                    last = pe.matmul(py[:T, n % 8, j * D:(j + 1) * D],
                                                     r.zt[x][:, k, b * T:(b + 1) * T],
                                                     parts[y][:, k, bass.ds(D * e, D)],
                                                     start=k == 0 and (x, y) == PARTS[0],
                                                     stop=k == KD - 1 and (x, y) == PARTS[-1])
                        last.then_inc(y_sum, 1)

            @block.scalar
            def _(act):
                for k in range(KD):
                    act.activation(parts[0][:, k], w[:, k], ACT.Copy).then_inc(w_high, 1)

            @block.vector
            def _(dve):
                for k in range(KD):
                    dve.wait_ge(w_high, k + 1)
                    dve.tensor_tensor(parts[1][:, k], w[:, k], whole(parts[0][:, k]),
                                      ALU.subtract).then_inc(w_split, 1)
                dve.sem_inc(added, 8)
                with dve.Fori(0, E) as e:
                    for n in range(pairs):
                        dve.wait_ge(y_sum, pairs * e + n + 1)
                        dve.wait_ge(added, pairs * e + n + 1)
                        for j in range(2):
                            b = 2 * n + j
                            last = dve.scalar_tensor_tensor(
                                c.resid[:T, b, :], py[:T, n % 8, j * D:(j + 1) * D],
                                flat_share[:, bass.ds(E * b + e, 1)], c.resid[:T, b, :], ALU.mult, ALU.add)
                        last.then_inc(added, 1)


def grouped_block(c, a):
    inverse_deviation(c, 1e-5, "gqa")
    with ExitStack() as st:
        inner = c.sb(st, "gqa_inner", [P, B, D])
        softmax_attention(c, a, Attention("gqa", kv=4, causal=True, norm="gqa_norm", keep=inner))
        (squared,) = c.sems("squared", "gqa_square")
        with c.nc.Block() as block:
            @block.vector
            def _(dve):
                dve.tensor_tensor(c.rstd[:T, :], c.moments[:T, :, 0], c.moments[:T, :, 0], ALU.mult).then_inc(squared, 1)
                dve.wait_ge(squared, 1)
                dve.tensor_tensor(c.moments[:T, :, 1], c.moments[:T, :, 1], c.rstd[:T, :], ALU.add)\
                   .then_inc(squared, 1)
                dve.wait_ge(squared, 2)
        inverse_deviation(c, 1e-6, "gqa_rms")
        r = Routing(c, st, "top2")

        def rms(dve, z, g):
            for j in range(G):
                b = G * g + j
                last = dve.tensor_scalar(z[:T, j, :], flat(inner[:T, bass.ds(b, 1), :]), c.scale(b), None, ALU.mult)
            return last

        w = c.sb(st, "top2_w", [P, KD, E * D])
        gather_tokens(c, r, rms, "top2_wg", (), "top2_norm", a, ahead=(w, "top2_w"))
        weigh_two(c, r)
        linear_experts(c, r, w)
    all_stats(c, "top2")


def differential_attention(c, a):
    inverse_deviation(c, 1e-5, "diff")
    softmax_attention(c, a, Attention("diff", dm=DH // 2, scale=(DH // 2) ** -0.5, differential=True))


CAPACITY = math.ceil(B * T / E)
ENOUGH = 0.9
WAYS = 8


def route_by_threshold(c, r):
    nc = c.nc
    with ExitStack() as st:
        above, tie = (c.sb(st, f"cap_{n}", [P, B, E, E]) for n in ("above", "tie"))
        rank, value, at_least, equal = (c.sb(st, f"cap_{n}", [P, B, E]) for n in ("rank", "value", "at_least", "equal"))
        places, runs, totals = (c.sb(st, f"cap_{n}", [P, E, B]) for n in ("places", "runs", "totals"))
        before = c.sb(st, "cap_before", [P, E, E])
        earlier = c.sb(st, "cap_earlier", [P, P])
        most = c.sb(st, "cap_most", [P, B])
        count, level, gain, room = (c.sb(st, f"cap_{n}", [P, E]) for n in ("count", "level", "gain", "room"))
        counts, step, offset, trial = (c.sb(st, f"cap_{n}", [P, E, WAYS - 1])
                                       for n in ("counts", "step", "offset", "trial"))
        reached = c.sb(st, "cap_reached", [P, B, E, WAYS - 1])
        pc = c.banks(st, "cap_pc", 3)
        made, link_s, less_ready, exp_ready, counted, summed, counted2, summed2, marked, prefixed, scan_s = c.sems(
            "made link less_ready exp_ready counted summed counted2 summed2 marked prefixed scan", "cap")
        steps = 27 // (WAYS.bit_length() - 1)

        def per_expert(x):
            return x[:T].unsqueeze(1).to_broadcast([T, B, E])

        with nc.Block() as block:
            @block.gpsimd
            def _(pool):
                lower_index(pool, made, before)
                pool.memset(earlier[:], 1.0).then_inc(made, 1)
                pool.wait_ge(made, 3)
                pool.affine_select(out=earlier[:], in_=earlier[:], compare_op=ALU.is_gt, fill=0.0, base=0,
                                   pattern=[[1, P]], channel_multiplier=-1).then_inc(made, 1)

            @block.scalar
            def _(act):
                act.wait_ge(less_ready, 1)
                act.activation(r.share[:T], r.share[:T], ACT.Exp).then_inc(exp_ready, 1)

            @block.tensor
            def _(pe):
                with pe.Fori(0, steps) as i:
                    pe.wait_ge(counted, i + 1)
                    pe.matmul(pc[:, 0, :E * (WAYS - 1)], c.ones[:T, :], counts[:T].rearrange("p e k -> p (e k)"),
                              start=True, stop=True).then_inc(summed, 1)
                pe.wait_ge(counted2, 1)
                pe.matmul(pc[:, 0, :E], c.ones[:T, :], count[:T, :], start=True, stop=True).then_inc(summed2, 1)
                pe.wait_ge(made, 4)
                pe.wait_ge(marked, 1)
                marks = equal[:T].rearrange("p b e -> p (b e)")
                pe.matmul(pc[:T, 1, :B * E], earlier[:T, :T], marks, start=True, stop=True)
                pe.matmul(pc[:T, 2, :B * E], c.ones[:T, :T], marks, start=True, stop=True).then_inc(prefixed, 1)

            @block.vector
            def _(dve):
                link = Link(dve, link_s)
                link.after(dve.tensor_reduce(most[:T, :], r.share[:T], AX.X, ALU.max))
                dve.tensor_tensor(r.share[:T], r.share[:T], most[:T, :].unsqueeze(2).to_broadcast([T, B, E]),
                                  ALU.subtract).then_inc(less_ready, 1)
                dve.wait_ge(exp_ready, 1)
                link.after(dve.tensor_reduce(most[:T, :], r.share[:T], AX.X, ALU.add))
                link.after(dve.reciprocal(most[:T, :], most[:T, :]))
                link.after(dve.tensor_tensor(r.share[:T], r.share[:T],
                                             most[:T, :].unsqueeze(2).to_broadcast([T, B, E]), ALU.mult))
                dve.wait_ge(made, 2)
                ranks(dve, link, r, above, tie, before, rank)
                link.after(dve.tensor_tensor(above[:T], above[:T],
                                             r.share[:T].unsqueeze(2).to_broadcast([T, B, E, E]), ALU.mult))
                link.after(dve.tensor_reduce(equal[:T], above[:T], AX.X, ALU.add))
                dve.tensor_scalar(at_least[:T], equal[:T], ENOUGH, None, ALU.is_lt)
                link.after(dve.tensor_scalar(rank[:T], rank[:T], 1.0, None, ALU.add))
                link.after(dve.tensor_tensor(value[:T], r.share[:T], rank[:T], ALU.subtract))
                dve.tensor_tensor(value[:T], value[:T], at_least[:T], ALU.mult)
                link.after(dve.tensor_scalar(equal[:T], at_least[:T], 1.0, 1e9, ALU.subtract, ALU.mult))
                dve.memset(level[:], -8.0)
                dve.memset(step[:], 8.0 / WAYS)
                for k in range(1, WAYS):
                    dve.memset(offset[:, :, k - 1:k], 8.0 / WAYS * k)
                link.after(dve.tensor_tensor(value[:T], value[:T], equal[:T], ALU.add))

                with dve.Fori(0, steps) as i:
                    loop = Link(dve, scan_s, i, 5)
                    three = [T, E, WAYS - 1]
                    loop.after(dve.tensor_tensor(trial[:T], offset[:T], level[:T, :].unsqueeze(2).to_broadcast(three),
                                                 ALU.add))
                    four = [T, B, E, WAYS - 1]
                    loop.after(dve.tensor_tensor(reached[:T], value[:T].unsqueeze(3).to_broadcast(four),
                                                 trial[:T].unsqueeze(1).to_broadcast(four), ALU.is_ge))
                    dve.tensor_reduce(counts[:T], reached[:T].rearrange("p b e k -> p e k b"), AX.X,
                                      ALU.add).then_inc(counted, 1)
                    dve.wait_ge(summed, i + 1)
                    loop.after(dve.scalar_tensor_tensor(
                        trial[:T].rearrange("p e k -> p (e k)"), pc[:T, 0, :E * (WAYS - 1)], float(CAPACITY),
                        step[:T].rearrange("p e k -> p (e k)"), ALU.is_ge, ALU.mult))
                    dve.tensor_scalar(step[:T], step[:T], 1.0 / WAYS, None, ALU.mult)
                    dve.tensor_scalar(offset[:T], offset[:T], 1.0 / WAYS, None, ALU.mult)
                    loop.after(dve.tensor_reduce(gain[:T, :], trial[:T], AX.X, ALU.add))
                    loop.after(dve.tensor_tensor(level[:T, :], level[:T, :], gain[:T, :], ALU.add))
                    loop.end()
                link.after(dve.tensor_tensor(at_least[:T], value[:T], per_expert(level), ALU.is_gt))
                dve.tensor_tensor(equal[:T], value[:T], per_expert(level), ALU.is_equal).then_inc(marked, 1)
                dve.tensor_reduce(count[:T, :], at_least[:T].rearrange("p b e -> p e b"), AX.X,
                                  ALU.add).then_inc(counted2, 1)
                dve.wait_ge(summed2, 1)
                dve.tensor_scalar(room[:T, :], pc[:T, 0, :E], -1.0, float(CAPACITY), ALU.mult, ALU.add)
                dve.memset(runs[:], 1.0)
                dve.wait_ge(prefixed, 1)
                link.after(dve.tensor_copy(totals[:T], pc[:T, 2, :B * E].rearrange("p (b e) -> p e b", e=E)))
                link.after(dve.memset(runs[:, :, 0:1], 0.0))
                link.after(dve.tensor_tensor_scan(places[:T].rearrange("p e b -> p (e b)"),
                                                  runs[:T].rearrange("p e b -> p (e b)"),
                                                  totals[:T].rearrange("p e b -> p (e b)"), 0.0, ALU.mult, ALU.add))
                link.after(dve.tensor_tensor(places[:T], places[:T], totals[:T], ALU.subtract))
                link.after(dve.tensor_tensor(rank[:T], places[:T].rearrange("p e b -> p b e"),
                                             pc[:T, 1, :B * E].rearrange("p (b e) -> p b e", e=E), ALU.add))
                link.after(dve.tensor_tensor(rank[:T], rank[:T], per_expert(room), ALU.is_lt))
                link.after(dve.tensor_tensor(rank[:T], rank[:T], equal[:T], ALU.mult))
                link.after(dve.tensor_tensor(rank[:T], rank[:T], at_least[:T], ALU.add))
                link.after(dve.tensor_tensor(r.share[:T], r.share[:T], rank[:T], ALU.mult))


def capacity_experts(c, a):
    inverse_deviation(c, 1e-5, "xmoe")
    with ExitStack() as st:
        r = Routing(c, st, "xmoe")
        gather_tokens(c, r, lambda dve, z, g: normalize(dve, c, z, g), "xmoe_wg", (), None, a)
        route_by_threshold(c, r)
        experts(c, r, a, ("xmoe_w1", "xmoe_w2"), D // P, ACT.Gelu)


GLA_ACT = {"z0": 0, "z1": 1, "v0": 3, "v1": 5, "f0": 6, "f1": 8, "n0": 9, "n1": 11,
           "t0": 25, "t1": 26, "t2": 27, "t3": 28}
GLA_DVE = {"y0": 4, "y1": 7, "r0": 10, "r1": 13, "r2": 16, "r3": 19}
GLA_WEIGH = 24
GLA_NEXT = ("z0", "z1", "r0", "r1", "r2", "r3", "v0", "v1", "f0", "f1", "n0", "n1", "t0", "t1", "t2", "t3")
GLA_LAST = ("y0", "y1")


def gla_steps(slots, part):
    return [x for x in slots
            if not (part == "first" and x in GLA_LAST or part == "last" and x not in GLA_LAST)]


def gla_first(slots, g, part):
    first = len(gla_steps(slots, "first"))
    return first if part == "first" else len(slots) * g + first - len(gla_steps(slots, "last"))


def gla_before(g, part, x):
    slots = GLA_ACT if x in GLA_ACT else GLA_DVE
    return gla_first(slots, g, part) + gla_steps(slots, part).index(x)


def gla_alone(x):
    slots = GLA_ACT if x in GLA_ACT else GLA_DVE
    if x in GLA_LAST:
        return gla_before(NG - 1, "last", x) + len(gla_steps(slots, "last"))
    return gla_steps(slots, "first").index(x)


def gated_linear_attention(c, a, bit_w):
    nc = c.nc
    inverse_deviation(c, 1e-5, "gla")
    L = T + 1
    NH2 = P // DH
    with ExitStack() as st:
        wqf = c.sb(st, "gla_wqf", [P, KD, 2 * D])
        wv, wo = (c.sb(st, f"gla_w{n}", [P, KD, D]) for n in "vo")
        place = c.sb(st, "gla_place", [P, DH, P])
        falls = c.sb(st, "gla_falls", [P, L])
        nexts = c.sb(st, "gla_nexts", [P, T])
        z = c.sb(st, "gla_z", [P, G, D])
        zt = c.sb(st, "gla_zt", [P, KD, N])
        rows = c.sb(st, "gla_rows", [P, G, 2, D])
        high, total = (c.sb(st, f"gla_{n}", [P, G * 2]) for n in ("high", "total"))
        v = c.sb(st, "gla_v", [P, G, D])
        fall = c.sb(st, "gla_fall", [P, 2, G, D])
        after = c.sb(st, "gla_after", [P, 2, G, D])
        wide = c.sb(st, "gla_wide", [P, 4, G, P])
        weight = c.sb(st, "gla_weight", [P, G, H])
        qt = c.sb(st, "gla_qt", [P, 2, KD, G, T])
        at = c.sb(st, "gla_at", [P, 2, KD, G, L])
        state = c.sb(st, "gla_state", [P, 4, G, L])
        taken = c.sb(st, "gla_taken", [P, 4, G, T])
        ot = c.sb(st, "gla_ot", [P, KD, N])
        six = c.sb(st, "gla_six", [P, G, 9])
        ps = c.banks(st, "gla_ps", 4)
        px = c.banks(st, "gla_px", 1)
        py = c.banks(st, "gla_py", 1)
        po = c.banks(st, "gla_po", 2)
        (w_in, ahead_in, made, z_ready, act_sum, act_done, dve_sum, dve_done, less_ready, exp_ready, rows_ready, spread, state_ready,
         taken_ready, repeated, weighed, o_sum, o_ready, link_first, link_pairs, link_last) = c.sems(
            "w_in ahead_in made z_ready act_sum act_done dve_sum dve_done less_ready exp_ready rows_ready spread state_ready "
            "taken_ready repeated weighed o_sum o_ready link_first link_pairs link_last", "gla")
        nu = KD * DH

        def carried(slots, g, part, w):
            return [(x, gla_before(g, part, x)) for x in gla_steps(slots, part) if slots[x] == w]

        with nc.Block() as block:
            @block.sync
            def _(sp):
                for dst, name in ((wqf[:, :, :D], "gla_wq"), (wqf[:, :, D:], "gla_wf"), (wv[:], "gla_wv"),
                                  (wo[:], "gla_wo")):
                    sp.dma_start(dst, a[name]).then_inc(w_in, 16)
                for n, name in enumerate(("bit_gate", "bit_up", "bit_down")):
                    sp.dma_start(bit_w[:, n, :], a[name].rearrange("p k f -> p (k f)")).then_inc(ahead_in, 16)
                sp.wait_ge(ahead_in, 48)

            @block.gpsimd
            def _(pool):
                def band(x, base, value, width, ready):
                    pool.affine_select(out=x, in_=x, compare_op=ALU.not_equal, fill=value, base=-base,
                                       pattern=[[-1, width]], channel_multiplier=1).then_inc(made, 1)
                    pool.wait_ge(made, ready)

                pool.memset(place[:], 1.0).then_inc(made, 1)
                pool.memset(falls[:], 0.0).then_inc(made, 1)
                pool.memset(nexts[:], 0.0).then_inc(made, 1)
                pool.wait_ge(made, 3)
                heads = place[:].rearrange("p e (h d) -> p e h d", d=DH)

                def keep(compare, base, pattern, channel, ready):
                    pool.affine_select(out=heads, in_=heads, compare_op=compare, fill=0.0, base=base,
                                       pattern=pattern, channel_multiplier=channel).then_inc(made, 1)
                    pool.wait_ge(made, ready)

                keep(ALU.is_ge, 0, [[0, DH], [-DH, NH2], [0, DH]], 1, 4)
                keep(ALU.is_ge, DH - 1, [[0, DH], [DH, NH2], [0, DH]], -1, 5)
                keep(ALU.is_equal, 0, [[-1, DH], [0, NH2], [1, DH]], 0, 6)
                band(falls[:], -1, 1.0, L, 7)
                band(falls[:], 0, -1.0, L, 8)
                band(nexts[:], 1, 1.0, T, 9)
                pool.sem_inc(taken_ready, 4)

                def group(g, q, part):
                    for w in range(nu):
                        pool.wait_ge(state_ready, nu * g + w + 1)
                        pool.wait_ge(o_sum, nu * g + w + 1)
                        pool.tensor_tensor(taken[:, w % 4], state[:, w % 4, :, 1:], qt[:, q, w // DH],
                                           ALU.mult).then_inc(taken_ready, 1)

                group(0, 0, "first")
                with pool.Fori(0, NG // 2 - 1) as i:
                    for u in range(2):
                        group(2 * i + 1 + u, (1 + u) % 2, "pairs")
                group(NG - 1, 1, "last")

            @block.tensor
            def _(pe):
                pe.sem_inc(o_sum, 4)
                pe.sem_inc(spread, 4)

                def step(x, g, count, made):
                    done = act_done if x in GLA_ACT else dve_done
                    if not (isinstance(count, int) and count == 0):
                        pe.wait_ge(done, count)
                    kind, k = x[0], int(x[1])
                    if x == "r0":
                        pe.wait_ge(act_done, made)
                    if x == "z0":
                        pe.wait_ge(z_ready, g + 1)
                    if x == "y0":
                        pe.wait_ge(o_ready, KD * (g + 1))
                    if x == "t0":
                        pe.wait_ge(rows_ready, G * g + G)
                    if kind == "z":
                        for j in range(G):
                            last = pe.transpose(px[:, 0, j * T:(j + 1) * T], z[:T, j, k * P:(k + 1) * P],
                                                c.ident[:T, :T])
                    elif kind == "r":
                        for m in range(KD):
                            last = pe.matmul(py[:T, 0, :], zt[:, m, k * T:(k + 1) * T], wqf[:, m, :],
                                             start=m == 0, stop=m == KD - 1)
                    elif kind in "vy":
                        src, w, bank = (zt, wv, px) if kind == "v" else (ot, wo, py)
                        for j in (2 * k, 2 * k + 1):
                            for m in range(KD):
                                last = pe.matmul(bank[:T, 0, j % 2 * D:(j % 2 + 1) * D], src[:, m, j * T:(j + 1) * T],
                                                 w[:, m, :], start=m == 0, stop=m == KD - 1)
                    elif kind in "fn":
                        shift, width = (falls, L) if kind == "f" else (nexts, T)
                        last = pe.matmul(px[:width, 0, :], shift[:T, :], v[:T, 2 * k:2 * k + 2, :].rearrange(
                            "p j d -> p (j d)"), start=True, stop=True)
                    else:
                        n, m = k // KD, k % KD
                        for j in range(G):
                            last = pe.transpose(px[:, 0, j * T:(j + 1) * T], rows[:T, j, n, m * P:(m + 1) * P],
                                                c.ident[:T, :T])
                    last.then_inc(act_sum if x in GLA_ACT else dve_sum, 1)

                def increments(r, w):
                    if not (isinstance(r, int) and r < 4):
                        pe.wait_ge(state_ready, r - 3)
                    pe.wait_ge(repeated, r + 1)
                    for j in range(G):
                        last = pe.transpose(ps[:, w % 4, j * L:(j + 1) * L], wide[:L, w % 4, j, :],
                                            c.ident[:L, :L])
                    last.then_inc(spread, 1)

                def contract(g, q, w, first):
                    r, m, e = nu * g + w, w // DH, w % DH
                    pe.wait_ge(taken_ready, r + 5)
                    if e == 0 and not first:
                        pe.wait_ge(o_ready, KD * g + m - 1)
                    pe.matmul(po[:, m, :N], place[:, e, :], taken[:, w % 4].rearrange("p j t -> p (j t)"),
                              start=e == 0, stop=e == DH - 1).then_inc(o_sum, 1)
                    if e == 0:
                        pe.wait_ge(weighed, g + 1)
                        for j in range(G):
                            pe.matmul(po[:, m, j * T:(j + 1) * T], after[:T, q, j, m * P:(m + 1) * P],
                                      c.ident[:T, :T], start=False, stop=False)

                def group(g, q, part):
                    for w in range(nu):
                        r = nu * g + w
                        if not (part == "last" and w + 4 >= nu):
                            increments(r + 4, (w + 4) % nu)
                        if w >= 2:
                            contract(g, q, w - 2, part == "first")
                        elif part != "first":
                            contract(g - 1, 1 - q, nu + w - 2, False)
                        for slots in (GLA_ACT, GLA_DVE):
                            for x, count in carried(slots, g, part, w):
                                step(x, g - 1 if x in GLA_LAST else g + 1, count,
                                     gla_before(g, part, "z1") + 1 if x == "r0" else None)

                for x in GLA_NEXT:
                    if x == "r0":
                        pe.wait_ge(w_in, 64)
                    if x == "f0":
                        pe.wait_ge(made, 9)
                    step(x, 0, gla_alone(x), gla_alone("z1") + 1)
                for w in range(4):
                    increments(w, w)
                group(0, 0, "first")
                with pe.Fori(0, NG // 2 - 1) as i:
                    for u in range(2):
                        group(2 * i + 1 + u, (1 + u) % 2, "pairs")
                group(NG - 1, 1, "last")
                for w in (nu - 2, nu - 1):
                    contract(NG - 1, 1, w, False)
                for x in GLA_LAST:
                    step(x, NG - 1, gla_alone(x), None)

            @block.scalar
            def _(act):
                def read(x, q, count):
                    kind, k = x[0], int(x[1])
                    act.wait_ge(act_sum, count + 1)
                    pair = slice(2 * k, 2 * k + 2)
                    if kind == "z":
                        last = act.activation(zt[:, k, :], px[:, 0, :N], ACT.Copy)
                    elif kind == "t":
                        dst = (qt[:, q, k % KD], at[:, q, k % KD, :, 1:])[k // KD]
                        last = act.activation(dst, px[:, 0, :N].rearrange("p (j t) -> p j t", j=G), ACT.Copy)
                    else:
                        rows_of, dst = {"v": (T, v[:T, pair, :]), "f": (L, fall[:L, q, pair, :]),
                                        "n": (T, after[:T, q, pair, :])}[kind]
                        last = act.activation(dst.rearrange("p j d -> p (j d)"), px[:rows_of, 0, :], ACT.Copy)
                    last.then_inc(act_done, 1)

                def exponential(g, j):
                    act.wait_ge(less_ready, G * g + j + 1)
                    x = rows[:T, j].rearrange("p n d -> p (n d)")
                    act.activation(x, x, ACT.Exp).then_inc(exp_ready, 1)

                def finish(g, m):
                    act.wait_ge(o_sum, nu * g + DH * (m + 1) + 4)
                    act.activation(ot[:, m, :], po[:, m, :N], ACT.Copy).then_inc(o_ready, 1)

                def repeat(r, q, w):
                    m, e = w // DH, w % DH
                    act.wait_ge(spread, r + 1)
                    column = fall[:L, q, :, m * P:(m + 1) * P].rearrange("p j (h d) -> p j h d", d=DH)[:, :, :, e:e + 1]
                    act.activation(wide[:L, w % 4].rearrange("p j (h k) -> p j h k", k=DH),
                                   column.to_broadcast([L, G, NH2, DH]), ACT.Copy).then_inc(repeated, 1)

                def group(g, q, part):
                    for w in range(nu):
                        if w + 4 < nu:
                            repeat(nu * g + w + 4, q, w + 4)
                        elif part != "last":
                            repeat(nu * g + w + 4, 1 - q, w + 4 - nu)
                        if w:
                            for x, count in carried(GLA_ACT, g, part, w - 1):
                                read(x, 1 - q, count)
                        if w == 2 and part != "first":
                            finish(g - 1, 1)
                        if w == DH + 2:
                            finish(g, 0)
                        for j in range(G):
                            if part != "last" and w == GLA_DVE[f"r{j}"] + 3:
                                exponential(g + 1, j)

                for x in GLA_NEXT:
                    if x[0] == "r":
                        exponential(0, int(x[1]))
                    else:
                        read(x, 0, gla_alone(x))
                for w in range(4):
                    repeat(w, 0, w)
                group(0, 0, "first")
                with act.Fori(0, NG // 2 - 1) as i:
                    for u in range(2):
                        group(2 * i + 1 + u, (1 + u) % 2, "pairs")
                group(NG - 1, 1, "last")
                finish(NG - 1, 1)

            @block.vector
            def _(dve):
                dve.memset(at[:, :, :, :, 0:1], 0.0)

                def read(link, x, g, count):
                    kind, k = x[0], int(x[1])
                    dve.wait_ge(dve_sum, count + 1)
                    if kind == "r":
                        both = py[:T, 0, :].rearrange("p (n d) -> p n d", n=2)
                        most = high[:T, 2 * k:2 * k + 2]
                        link.after(dve.tensor_reduce(most, both, AX.X, ALU.max))
                        dve.tensor_tensor(rows[:T, k], both, most.unsqueeze(2).to_broadcast([T, 2, D]),
                                          ALU.subtract).then_inc(dve_done, 1)
                        dve.wait_ge(dve_done, count + 1)
                        dve.sem_inc(less_ready, 1)
                        return
                    for j in (2 * k, 2 * k + 1):
                        last = dve.tensor_tensor(c.tile(G * g + j), py[:T, 0, j % 2 * D:(j % 2 + 1) * D],
                                                 c.tile(G * g + j), ALU.add)
                    last.then_inc(dve_done, 1)
                    dve.wait_ge(dve_done, count + 1)
                    if k == 1:
                        link.after(tile_stats(dve, c, link, six, g))

                def softmax(link, g, j):
                    dve.wait_ge(exp_ready, G * g + j + 1)
                    sums = total[:T, 2 * j:2 * j + 2]
                    link.after(dve.tensor_reduce(sums, rows[:T, j], AX.X, ALU.add))
                    link.after(dve.reciprocal(sums, sums))
                    dve.tensor_scalar(rows[:T, j, 0, :], rows[:T, j, 0, :], total[:T, 2 * j:2 * j + 1],
                                      DH ** -0.5, ALU.mult, ALU.mult)
                    dve.tensor_scalar(rows[:T, j, 1, :], rows[:T, j, 1, :], total[:T, 2 * j + 1:2 * j + 2],
                                      None, ALU.mult).then_inc(rows_ready, 1)
                    dve.wait_ge(rows_ready, G * g + j + 1)
                    link.after(dve.tensor_reduce(weight[:T, j], rows[:T, j, 0, :].rearrange("p (h d) -> p h d", d=DH),
                                                 AX.X, ALU.add))

                def weigh(q, count):
                    dve.wait_ge(act_done, count)
                    x = after[:T, q].rearrange("p j (h d) -> p (j h) d", d=DH)
                    dve.tensor_tensor(x, x, weight[:T].rearrange("p j h -> p (j h)").unsqueeze(2)
                                      .to_broadcast([T, G * H, DH]), ALU.mult).then_inc(weighed, 1)

                def group(link, g, q, part):
                    if part != "last":
                        normalize(dve, c, z, g + 1).then_inc(z_ready, 1)
                    for w in range(nu):
                        r = nu * g + w
                        if w == 0:
                            dve.wait_ge(act_done, gla_first(GLA_ACT, g, part))
                        dve.wait_ge(spread, r + 5)
                        dve.wait_ge(taken_ready, r + 1)
                        dve.tensor_tensor_scan(state[:, w % 4].rearrange("p j t -> p (j t)"),
                                               at[:, q, w // DH].rearrange("p j t -> p (j t)"),
                                               ps[:, w % 4, :G * L], 0.0, ALU.mult, ALU.add).then_inc(state_ready, 1)
                        if w >= 2:
                            for x, count in carried(GLA_DVE, g, part, w - 2):
                                read(link, x, g - 1 if x in GLA_LAST else g + 1, count)
                        if part != "last":
                            for j in range(G):
                                if w == GLA_DVE[f"r{j}"] + 4:
                                    softmax(link, g + 1, j)
                            if w == GLA_WEIGH:
                                weigh(1 - q, gla_before(g, part, "n1") + 1)

                normalize(dve, c, z, 0).then_inc(z_ready, 1)
                link = Link(dve, link_first)
                for j in range(G):
                    read(link, f"r{j}", 0, gla_alone(f"r{j}"))
                    softmax(link, 0, j)
                weigh(0, gla_alone("n1") + 1)
                group(link, 0, 0, "first")
                with dve.Fori(0, NG // 2 - 1) as i:
                    link = Link(dve, link_pairs, i, 2 * (4 * G + 3))
                    for u in range(2):
                        group(link, 2 * i + 1 + u, (1 + u) % 2, "pairs")
                    link.end()
                link = Link(dve, link_last)
                group(link, NG - 1, 1, "last")
                for x in GLA_LAST:
                    read(link, x, NG - 1, gla_alone(x))


LEVELS = 127.0
TINY = 1e-5


def ternary_network(c, w):
    nc = c.nc
    inverse_deviation(c, 1e-5, "bit")
    NF = FF // P
    with ExitStack() as st:
        wt = c.sb(st, "bit_wt", [P, 3, KD * FF], BF16)
        gate, up = (wt[:, n, :].rearrange("p (k f) -> p k f", k=KD) for n in range(2))
        down = wt[:, 2, :].rearrange("p (f d) -> p f d", f=NF)
        mean = c.sb(st, "bit_mean", [P, 3])
        factor = c.sb(st, "bit_factor", [P, 3])
        identh = c.sb(st, "bit_identh", [P, P], BF16)
        z = c.sb(st, "bit_z", [P, G, D])
        xh = c.sb(st, "bit_xh", [P, G, D], BF16)
        xt = c.sb(st, "bit_xt", [P, KD, N], BF16)
        size, grid, back, back2 = (c.sb(st, f"bit_{n}", [P, G]) for n in ("size", "grid", "back", "back2"))
        next_back, next_back2 = (c.sb(st, f"bit_next_{n}", [P, G]) for n in ("back", "back2"))
        swish = c.sb(st, "bit_swish", [P, 2, FF])
        inner = c.sb(st, "bit_inner", [P, 2, FF])
        ih = c.sb(st, "bit_ih", [P, 2, FF], BF16)
        it = c.sb(st, "bit_it", [P, 2, NF, T], BF16)
        isize, igrid, iback = (c.sb(st, f"bit_{n}", [P, 2]) for n in ("isize", "igrid", "iback"))
        six = c.sb(st, "bit_six", [P, G, 9])
        pg = c.banks(st, "bit_pg", 4)
        px = st.enter_context(nc.psum_tensor("bit_px", [P, 1, 2 * BANK], BF16))
        pi = st.enter_context(nc.psum_tensor("bit_pi", [P, 1, 2 * BANK], BF16))
        py = c.banks(st, "bit_py", 2)
        (means, mean_sum, prep_s, ready, x_ready, xt_sum, xt_ready, gate_sum, swish_ready, inner_used,
         back_ready, i_ready, it_sum, it_ready, y_sum, done, link_loop, link_last) = c.sems(
            "means mean_sum prep ready x_ready xt_sum xt_ready gate_sum swish_ready inner_used "
            "back_ready i_ready it_sum it_ready y_sum done link_loop link_last", "bit")

        with nc.Block() as block:
            @block.tensor
            def _(pe):
                pe.sem_inc(y_sum, 2)
                pe.wait_ge(means, 1)
                pe.matmul(pg[:, 0, :3], c.ones[:], mean[:], start=True, stop=True).then_inc(mean_sum, 1)
                pe.wait_ge(ready, 1)

                def features(g):
                    pe.wait_ge(x_ready, g + 1)
                    for k in range(KD):
                        for j in range(G):
                            last = pe.transpose(px[:, 0, k * BANK + j * T:k * BANK + (j + 1) * T],
                                                xh[:T, j, k * P:(k + 1) * P], identh[:T, :T])
                    last.then_inc(xt_sum, 1)

                def open_up(r, g, j):
                    if j == 0:
                        pe.wait_ge(xt_ready, g + 1)
                    pe.wait_ge(inner_used, r + 1)
                    for n, weight in enumerate((gate, up)):
                        for f in range(2):
                            for k in range(KD):
                                last = pe.matmul(pg[:T, 2 * n + f, :], xt[:, k, j * T:(j + 1) * T],
                                                 weight[:, k, f * BANK:(f + 1) * BANK],
                                                 start=k == 0, stop=k == KD - 1)
                    last.then_inc(gate_sum, 1)

                def turn(r, j):
                    pe.wait_ge(i_ready, r + 1)
                    pe.wait_ge(it_ready, r + 1)
                    for f in range(NF):
                        last = pe.transpose(pi[:, 0, f * P:f * P + T], ih[:T, j % 2, f * P:(f + 1) * P],
                                            identh[:T, :T])
                    last.then_inc(it_sum, 1)

                def close(r, j):
                    pe.wait_ge(it_ready, r + 2)
                    pe.wait_ge(done, r + 1)
                    for f in range(NF):
                        last = pe.matmul(py[:T, j % 2, :D], it[:, j % 2, f, :], down[:, f, :],
                                         start=f == 0, stop=f == NF - 1)
                    last.then_inc(y_sum, 1)

                def group(g, final):
                    for j in range(G):
                        r = G * g + j
                        if j + 1 < G:
                            open_up(r + 1, g, j + 1)
                        elif not final:
                            open_up(r + 1, g + 1, 0)
                        if j == 2 and not final:
                            features(g + 1)
                        turn(r, j)
                        close(r, j)

                features(0)
                open_up(0, 0, 0)
                with pe.Fori(0, NG - 1) as g:
                    group(g, False)
                group(NG - 1, True)

            @block.scalar
            def _(act):
                act.sem_inc(it_ready, 1)
                act.activation(identh[:], c.ident[:], ACT.Copy).then_inc(ready, 1)

                def features(g):
                    act.wait_ge(xt_sum, g + 1)
                    act.activation(xt[:], px[:, 0, :].rearrange("p (k n) -> p k n", k=KD)[:, :, :N],
                                   ACT.Copy).then_inc(xt_ready, 1)

                def swishes(r, g, j):
                    if j == 0:
                        act.wait_ge(back_ready, g + 1)
                    act.wait_ge(gate_sum, r + 1)
                    act.wait_ge(inner_used, r + 1)
                    act.activation(swish[:T, j % 2, :], pg[:T, 0:2, :].rearrange("p n d -> p (n d)"), ACT.Silu,
                                   scale=back[:T, j:j + 1]).then_inc(swish_ready, 1)

                def turned(r, j):
                    act.wait_ge(it_sum, r + 1)
                    act.wait_ge(y_sum, r + 1)
                    act.activation(it[:, j % 2], pi[:, 0, :].rearrange("p (f n) -> p f n", n=P)[:, :, :T],
                                   ACT.Copy).then_inc(it_ready, 1)

                def group(g, final):
                    for j in range(G):
                        r = G * g + j
                        if j + 1 < G:
                            swishes(r + 1, g, j + 1)
                        elif not final:
                            swishes(r + 1, g + 1, 0)
                        if j == 2 and not final:
                            features(g + 1)
                        turned(r, j)

                features(0)
                swishes(0, 0, 0)
                with act.Fori(0, NG - 1) as g:
                    group(g, False)
                group(NG - 1, True)

            @block.vector
            def _(dve):
                prep = Link(dve, prep_s)
                for n in range(3):
                    last = dve.tensor_reduce(mean[:, n:n + 1], w[:, n, :], AX.X, ALU.add, apply_absolute_value=True)
                last.then_inc(means, 1)
                dve.wait_ge(mean_sum, 1)
                prep.after(dve.tensor_scalar(mean[:], pg[:, 0, :3], 1.0 / (D * FF), TINY, ALU.mult, ALU.max))
                prep.after(dve.reciprocal(factor[:], mean[:]))
                for n in range(3):
                    last = dve.tensor_scalar(w[:, n, :], w[:, n, :], factor[:, n:n + 1], ROUND, ALU.mult, ALU.add)
                prep.after(last)
                flat_w = w[:].rearrange("p n f -> p (n f)")
                prep.after(dve.tensor_scalar(flat_w, flat_w, ROUND, -1.0, ALU.subtract, ALU.max))
                prep.after(dve.tensor_scalar(wt[:].rearrange("p n f -> p (n f)"), flat_w, 1.0, None, ALU.min))
                dve.tensor_scalar(factor[:], mean[:], 1.0 / LEVELS, None, ALU.mult)
                dve.memset(size[:], 0.0)
                dve.wait_ge(ready, 1)
                dve.memset(grid[:], 0.0).then_inc(ready, 1)
                dve.wait_ge(ready, 2)
                dve.sem_inc(done, 2)
                dve.sem_inc(inner_used, 1)

                def measure(link, g):
                    link.after(normalize(dve, c, z, g))
                    link.after(dve.tensor_reduce(size[:T, :], z[:T], AX.X, ALU.max, apply_absolute_value=True))

                def round_rows(link):
                    link.after(dve.tensor_scalar(size[:T, :], size[:T, :], TINY, None, ALU.max))
                    dve.tensor_scalar(next_back[:T, :], size[:T, :], factor[:T, 0:1], None, ALU.mult)
                    dve.tensor_scalar(next_back2[:T, :], size[:T, :], factor[:T, 1:2], None, ALU.mult)
                    link.after(dve.reciprocal(grid[:T, :], size[:T, :]))
                    link.after(dve.tensor_scalar(grid[:T, :], grid[:T, :], LEVELS, None, ALU.mult))
                    for j in range(G):
                        last = dve.tensor_scalar(z[:T, j, :], z[:T, j, :], grid[:T, j:j + 1], ROUND, ALU.mult, ALU.add)
                    link.after(last)
                    dve.tensor_scalar(xh[:T].rearrange("p j d -> p (j d)"), z[:T].rearrange("p j d -> p (j d)"),
                                      ROUND, None, ALU.subtract).then_inc(x_ready, 1)

                def take_back(g):
                    dve.tensor_copy(back[:T, :], next_back[:T, :])
                    dve.tensor_copy(back2[:T, :], next_back2[:T, :]).then_inc(back_ready, 1)
                    dve.wait_ge(back_ready, g + 1)

                def multiply(r, j):
                    dve.wait_ge(swish_ready, r + 1)
                    dve.scalar_tensor_tensor(inner[:T, j % 2, :], pg[:T, 2:4, :].rearrange("p n d -> p (n d)"),
                                             back2[:T, j:j + 1], swish[:T, j % 2, :], ALU.mult,
                                             ALU.mult).then_inc(inner_used, 1)
                    dve.wait_ge(inner_used, r + 2)

                def round_inner(link, n):
                    x = inner[:T, n, :]
                    link.after(dve.tensor_reduce(isize[:T, n:n + 1], x, AX.X, ALU.max, apply_absolute_value=True))
                    link.after(dve.tensor_scalar(isize[:T, n:n + 1], isize[:T, n:n + 1], TINY, None, ALU.max))
                    dve.tensor_scalar(iback[:T, n:n + 1], isize[:T, n:n + 1], factor[:T, 2:3], None, ALU.mult)
                    link.after(dve.reciprocal(igrid[:T, n:n + 1], isize[:T, n:n + 1]))
                    link.after(dve.tensor_scalar(igrid[:T, n:n + 1], igrid[:T, n:n + 1], LEVELS, None, ALU.mult))
                    link.after(dve.tensor_scalar(x, x, igrid[:T, n:n + 1], ROUND, ALU.mult, ALU.add))
                    dve.tensor_scalar(ih[:T, n, :], x, ROUND, None, ALU.subtract).then_inc(i_ready, 1)

                def add(b, n):
                    dve.wait_ge(y_sum, b + 3)
                    dve.scalar_tensor_tensor(c.tile(b), py[:T, n, :D], iback[:T, n:n + 1],
                                             c.tile(b), ALU.mult, ALU.add).then_inc(done, 1)

                def group_stats(link, g):
                    dve.wait_ge(done, G * g + G + 2)
                    link.after(tile_stats(dve, c, link, six, g))

                def group(link, g, first, final):
                    for j in range(G):
                        r = G * g + j
                        multiply(r, j)
                        if j == G - 1 and not final:
                            take_back(g + 1)
                        round_inner(link, j % 2)
                        if j or not first:
                            add(r - 1, (j - 1) % 2)
                        if j == 0 and not first:
                            group_stats(link, g - 1)
                        if not final and j == 0:
                            measure(link, g + 1)
                        if not final and j == 1:
                            round_rows(link)

                link = Link(dve, link_last)
                measure(link, 0)
                round_rows(link)
                link.after(dve.memset(six[:], 0.0))
                take_back(0)
                group(link, 0, True, False)
                with dve.Fori(1, NG - 1) as g:
                    loop = Link(dve, link_loop, g - 1, 5 * G + 3 + 2 + 4)
                    group(loop, g, False, False)
                    loop.end()
                group(link, NG - 1, False, True)
                add(B - 1, 1)
                group_stats(link, NG - 1)


def recurrence_and_ternary_network(c, a):
    with ExitStack() as st:
        bit_w = c.sb(st, "bit_w", [P, 3, KD * FF])
        gated_linear_attention(c, a, bit_w)
        c.end_of_phase()
        ternary_network(c, bit_w)


def matrix(w):
    return w.reshape(-1, P, w.shape[1]).transpose(1, 0, 2)


def matrices(w):
    return w.reshape(w.shape[0], -1, P, w.shape[2]).transpose(0, 2, 1, 3)


def layouts(x):
    image = x["x"].reshape(NG, G, 3, NI // PATCH, PATCH, NI // PATCH, PATCH)
    image = image.transpose(0, 2, 4, 6, 1, 3, 5).reshape(NG, KT, P, G, NPATCH).transpose(0, 2, 1, 3, 4)
    patches = np.zeros((NG, P, KT, G, CLS), image.dtype)
    patches[..., 1:] = image
    t = {"patches": patches, "txt": x["txt"].transpose(1, 0, 2),
         "tok_w": matrix(x["L0_tok_W"].T), "tok_b": x["L0_tok_b"],
         "tok_cls": x["L0_tok_cls_token"][0], "tok_pos": x["L0_tok_pos_embedding"][0]}
    for n in "qkvp":
        t[f"rff_w{n}"] = matrix(x[f"L0_attn_W{n}"].T)
    t["rff_bp"] = x["L0_attn_bp"][None]
    t["rff_br"] = x["L0_attn_br"].T
    t["rff_wr"] = x["L0_attn_Wr"].transpose(1, 0, 2)
    t["top1_wg"] = matrix(x["L0_ffn_gate_w"].T)
    t["top1_gate_b"], t["top1_expert_bias"] = x["L0_ffn_gate_b"], x["L0_ffn_expert_bias"]
    t["top1_b1"] = x["L0_ffn_b1"].reshape(E, FF // P, P).transpose(0, 2, 1)
    t["top1_b2"] = x["L0_ffn_b2"]
    t["top1_w1"] = matrices(x["L0_ffn_w1"])
    t["top1_w2"] = matrices(x["L0_ffn_w2"])
    for n in "qkvo":
        t[f"tern_w{n}"] = matrix(x[f"L1_attn_w_{n}"].T)
        t[f"tern_s{n}"] = np.reshape(x[f"L1_attn_s_{n}"], (1,))
        t[f"tern_b{n}"] = x[f"L1_attn_b_{n}"]
    t["tern_bq"], t["tern_bk"] = (x[f"L1_attn_b_{n}"].reshape(KD, P).T for n in "qk")
    t["gqa_wq"], t["gqa_wo"] = (matrix(x[f"L1_ffn_w{n}"].T) for n in "qo")
    t["gqa_wk"] = matrix(np.repeat(x["L1_ffn_wk"].reshape(4, DH, D), H // 4, axis=0).reshape(D, D).T)
    t["gqa_wv"] = matrix(x["L1_ffn_wv"].T)
    t["gqa_norm"] = x["L1_ffn_attn_norm_w"].reshape(KD, P).T
    t["top2_norm"] = x["L1_ffn_ffn_norm_w"].reshape(KD, P).T
    t["top2_wg"] = matrix(x["L1_ffn_gate_w"].T)
    t["top2_w"] = x["L1_ffn_expert_w"].transpose(2, 0, 1).reshape(KD, P, E * D).transpose(1, 0, 2)
    for n in "qkvo":
        t[f"diff_w{n}"] = matrix(x[f"L3_attn_W{n}"].T)
    for n in ("q1", "k1", "q2", "k2"):
        t[f"diff_lambda_{n}"] = x[f"L3_attn_lambda_{n}"]
    t["diff_subln"] = x["L3_attn_subln_w"]
    t["xmoe_wg"] = matrix(x["L3_ffn_gate_w"].T)
    t["xmoe_w1"] = matrices(x["L3_ffn_w1"].transpose(0, 2, 1))
    t["xmoe_w2"] = matrices(x["L3_ffn_w2"].transpose(0, 2, 1))
    for n, m in zip("qfvo", "qfio"):
        t[f"gla_w{n}"] = matrix(x[f"L2_attn_W{m}"])
    for n in ("gate", "up", "down"):
        t[f"bit_{n}"] = matrix(x[f"L2_ffn_w_{n}"].T)
    return {n: np.ascontiguousarray(v) for n, v in t.items()}


def build_program(nc, a, out):
    with ExitStack() as stack:
        c = Core(nc, stack)
        constants(c)

        def phases(*all_of_them):
            for phase in all_of_them:
                phase(c, a)
                c.end_of_phase()

        phases(tokens, random_feature_attention, top1_experts, scaled_attention, grouped_block,
               recurrence_and_ternary_network, differential_attention, capacity_experts)
        store(c, out)


def kernel(**inputs):
    import concourse.bacc as bacc
    from concourse.bass_utils import run_bass_kernel_spmd

    arrays = {f"in_{n}": v for n, v in layouts({n: np.asarray(v) for n, v in inputs.items()}).items()}
    nc = bacc.Bacc("TRN2", target_bir_lowering=False, num_devices=1)
    a = {n[3:]: nc.dram_tensor(n, v.shape, mybir.dt.from_np(v.dtype), kind="ExternalInput").ap()
         for n, v in arrays.items()}
    out = nc.dram_tensor("out", (B, T, D), F32, kind="ExternalOutput").ap()
    build_program(nc, a, out)
    result = run_bass_kernel_spmd(nc, [arrays], core_ids=[0])
    return result.results[0]["out"]
```
